# Optimizing a Trainium2 kernel written in Bass

```python
import numpy as np
import jax
import jax.numpy as jnp

def _softmax(x, axis=-1):
    return jax.nn.softmax(x, axis=axis)

def _gelu(x):
    return jax.nn.gelu(x, approximate=True)

def _silu(x):
    return jax.nn.silu(x)

def _sigmoid(x):
    return jax.nn.sigmoid(x)

def _layernorm(x, axis=-1, eps=1e-05):
    m = jnp.mean(x, axis=axis, keepdims=True)
    v = jnp.var(x, axis=axis, keepdims=True)
    return (x - m) / jnp.sqrt(v + eps)

def _scatter_add(tgt, idx, src, axis=0):
    return tgt.at[idx].add(src)

def _segment_sum(src, seg, n):
    return jax.ops.segment_sum(src, seg, n)
kernel_name = 'mk_hybrid_d1_jaxref_r8_f56ea9'

def setup_inputs(seed: int=0):
    np.random.seed(seed)
    _w = jnp.asarray

    def _L0_attn_a_setup():
        import jax, jax.numpy as jnp
        import numpy as np
        D_MODEL = 512
        N_HEADS = 32
        HEAD_DIM = D_MODEL // N_HEADS
        CLIP_QKV = 8.0
        ALIBI_BIAS_MAX = 8.0
        LN_EPS = 1e-05

        def _alibi_slopes(n_heads: int, bias_max: float) -> jnp.ndarray:
            next_pow2 = 2 ** int(np.ceil(np.log2(n_heads)))
            m = np.arange(1, next_pow2 + 1, dtype=np.float32) * (bias_max / next_pow2)
            slopes = 1.0 / np.power(2.0, m)
            if next_pow2 != n_heads:
                slopes = np.concatenate([slopes[1::2], slopes[::2]])[:n_heads]
            return jnp.asarray(slopes)

        def _layer_norm(x, w, b):
            mu = jnp.mean(x, axis=-1, keepdims=True)
            var = jnp.mean(jnp.square(x - mu), axis=-1, keepdims=True)
            return (x - mu) * jax.lax.rsqrt(var + LN_EPS) * w + b
        key = jax.random.key(seed)
        ks = jax.random.split(key, 3)
        B, S = (1, 256)
        hidden_states = jax.random.normal(ks[0], (B, S, D_MODEL), dtype=jnp.float32)
        Wqkv = jax.random.normal(ks[1], (3 * D_MODEL, D_MODEL), dtype=jnp.float32) * 0.02
        Wout = jax.random.normal(ks[2], (D_MODEL, D_MODEL), dtype=jnp.float32) * 0.02
        return {'hidden_states': hidden_states, 'Wqkv': Wqkv, 'q_ln_w': jnp.ones((D_MODEL,), jnp.float32), 'q_ln_b': jnp.zeros((D_MODEL,), jnp.float32), 'k_ln_w': jnp.ones((D_MODEL,), jnp.float32), 'k_ln_b': jnp.zeros((D_MODEL,), jnp.float32), 'Wout': Wout}
    _L0_attn_a_in = _L0_attn_a_setup()

    def _L0_attn_b_setup():
        import jax, jax.numpy as jnp
        import numpy as np
        import math
        B, L, D, H = (32, 64, 512, 32)
        HD = D // H
        key = jax.random.key(seed)
        ks = jax.random.split(key, 9)
        s = 1.0 / math.sqrt(D)
        return {'x': jax.random.normal(ks[0], (B, L, D), jnp.float32), 'Wq': jax.random.normal(ks[1], (D, D), jnp.float32) * s, 'bq': jax.random.normal(ks[2], (D,), jnp.float32) * s, 'Wk': jax.random.normal(ks[3], (D, D), jnp.float32) * s, 'bk': jax.random.normal(ks[4], (D,), jnp.float32) * s, 'Wv': jax.random.normal(ks[5], (D, D), jnp.float32) * s, 'bv': jax.random.normal(ks[6], (D,), jnp.float32) * s, 'Wo': jax.random.normal(ks[7], (D, D), jnp.float32) * s, 'bo': jax.random.normal(ks[8], (D,), jnp.float32) * s}
    _L0_attn_b_in = _L0_attn_b_setup()

    def _L0_ffn_setup():
        import jax, jax.numpy as jnp
        import numpy as np
        BATCH, TOK, DIM, OUT = (4, 256, 512, 512)
        E, R, TOP_K = (8, 16, 2)
        SCALING = 16.0 / R
        key = jax.random.key(seed)
        ks = jax.random.split(key, 6)
        return {'x': jax.random.normal(ks[0], (BATCH, TOK, DIM), dtype=jnp.float32), 'W_base': jax.random.normal(ks[1], (OUT, DIM), dtype=jnp.float32) / np.sqrt(DIM), 'b_base': jax.random.normal(ks[2], (OUT,), dtype=jnp.float32) * 0.01, 'W_gate': jax.random.normal(ks[3], (E, DIM), dtype=jnp.float32) * 0.01, 'A': jax.random.normal(ks[4], (E, R, DIM), dtype=jnp.float32) / np.sqrt(DIM), 'B': jax.random.normal(ks[5], (OUT, OUT // OUT * R * 0 + R), dtype=jnp.float32)[None].repeat(E, 0) * 0.0 + jax.random.normal(ks[5], (E, OUT, R), dtype=jnp.float32) * 0.02}
    _L0_ffn_in = _L0_ffn_setup()
    _d = {'L0_attn_a_hidden_states': _L0_attn_a_in['hidden_states'], 'L0_attn_a_Wqkv': _L0_attn_a_in['Wqkv'], 'L0_attn_a_q_ln_w': _L0_attn_a_in['q_ln_w'], 'L0_attn_a_q_ln_b': _L0_attn_a_in['q_ln_b'], 'L0_attn_a_k_ln_w': _L0_attn_a_in['k_ln_w'], 'L0_attn_a_k_ln_b': _L0_attn_a_in['k_ln_b'], 'L0_attn_a_Wout': _L0_attn_a_in['Wout'], 'L0_attn_b_Wq': _L0_attn_b_in['Wq'], 'L0_attn_b_bq': _L0_attn_b_in['bq'], 'L0_attn_b_Wk': _L0_attn_b_in['Wk'], 'L0_attn_b_bk': _L0_attn_b_in['bk'], 'L0_attn_b_Wv': _L0_attn_b_in['Wv'], 'L0_attn_b_bv': _L0_attn_b_in['bv'], 'L0_attn_b_Wo': _L0_attn_b_in['Wo'], 'L0_attn_b_bo': _L0_attn_b_in['bo'], 'L0_ffn_W_base': _L0_ffn_in['W_base'], 'L0_ffn_b_base': _L0_ffn_in['b_base'], 'L0_ffn_W_gate': _L0_ffn_in['W_gate'], 'L0_ffn_A': _L0_ffn_in['A'], 'L0_ffn_B': _L0_ffn_in['B']}
    _x0 = _d['L0_attn_a_hidden_states']
    _d['L0_attn_a_hidden_states'] = jax.random.normal(jax.random.fold_in(jax.random.key(seed), 1), (4, 256, 512), dtype=_x0.dtype)
    del _x0
    return _d

def reference(L0_attn_a_hidden_states, L0_attn_a_Wqkv, L0_attn_a_q_ln_w, L0_attn_a_q_ln_b, L0_attn_a_k_ln_w, L0_attn_a_k_ln_b, L0_attn_a_Wout, L0_attn_b_Wq, L0_attn_b_bq, L0_attn_b_Wk, L0_attn_b_bk, L0_attn_b_Wv, L0_attn_b_bv, L0_attn_b_Wo, L0_attn_b_bo, L0_ffn_W_base, L0_ffn_b_base, L0_ffn_W_gate, L0_ffn_A, L0_ffn_B):

    def _L0_attn_a_ref(hidden_states, Wqkv, q_ln_w, q_ln_b, k_ln_w, k_ln_b, Wout):
        import jax, jax.numpy as jnp
        import numpy as np
        D_MODEL = 512
        N_HEADS = 32
        HEAD_DIM = D_MODEL // N_HEADS
        CLIP_QKV = 8.0
        ALIBI_BIAS_MAX = 8.0
        LN_EPS = 1e-05

        def _alibi_slopes(n_heads: int, bias_max: float) -> jnp.ndarray:
            next_pow2 = 2 ** int(np.ceil(np.log2(n_heads)))
            m = np.arange(1, next_pow2 + 1, dtype=np.float32) * (bias_max / next_pow2)
            slopes = 1.0 / np.power(2.0, m)
            if next_pow2 != n_heads:
                slopes = np.concatenate([slopes[1::2], slopes[::2]])[:n_heads]
            return jnp.asarray(slopes)

        def _layer_norm(x, w, b):
            mu = jnp.mean(x, axis=-1, keepdims=True)
            var = jnp.mean(jnp.square(x - mu), axis=-1, keepdims=True)
            return (x - mu) * jax.lax.rsqrt(var + LN_EPS) * w + b
        B, S, _ = hidden_states.shape
        qkv = jnp.einsum('bsd,ed->bse', hidden_states, Wqkv)
        qkv = jnp.clip(qkv, -CLIP_QKV, CLIP_QKV)
        q, k, v = jnp.split(qkv, [D_MODEL, 2 * D_MODEL], axis=-1)
        q = _layer_norm(q, q_ln_w, q_ln_b)
        k = _layer_norm(k, k_ln_w, k_ln_b)
        q = q.reshape(B, S, N_HEADS, HEAD_DIM)
        k = k.reshape(B, S, N_HEADS, HEAD_DIM)
        v = v.reshape(B, S, N_HEADS, HEAD_DIM)
        scale = HEAD_DIM ** (-0.5)
        scores = jnp.einsum('bqhd,bkhd->bhqk', q, k) * scale
        slopes = _alibi_slopes(N_HEADS, ALIBI_BIAS_MAX)
        pos = jnp.arange(S)
        rel = (pos[None, :] - pos[:, None]).astype(jnp.float32)
        scores = scores + slopes[None, :, None, None] * rel[None, None]
        causal = pos[None, :] <= pos[:, None]
        scores = jnp.where(causal[None, None], scores, jnp.float32(-1e+30))
        probs = jax.nn.softmax(scores, axis=-1)
        out = jnp.einsum('bhqk,bkhd->bqhd', probs, v).reshape(B, S, D_MODEL)
        return jnp.einsum('bsd,ed->bse', out, Wout)

    def _L0_attn_b_ref(x, Wq, bq, Wk, bk, Wv, bv, Wo, bo):
        import jax, jax.numpy as jnp
        import numpy as np
        import math
        B, L, D, H = (32, 64, 512, 32)
        HD = D // H
        b, l, d = x.shape
        h, hd = (H, HD)
        q = (x @ Wq.T + bq).reshape(b, l, h, hd).transpose(0, 2, 1, 3)
        k = (x @ Wk.T + bk).reshape(b, l, h, hd).transpose(0, 2, 1, 3)
        v = (x @ Wv.T + bv).reshape(b, l, h, hd).transpose(0, 2, 1, 3)
        scores = jnp.einsum('bhqd,bhkd->bhqk', q, k) / math.sqrt(hd)
        causal = jnp.tril(jnp.ones((l, l), bool))
        scores = jnp.where(causal, scores, -jnp.inf)
        att = jax.nn.softmax(scores, axis=-1)
        out = jnp.einsum('bhqk,bhkd->bhqd', att, v)
        out = out.transpose(0, 2, 1, 3).reshape(b, l, d)
        return out @ Wo.T + bo

    def _L0_ffn_ref(x, W_base, b_base, W_gate, A, B):
        import jax, jax.numpy as jnp
        import numpy as np
        BATCH, TOK, DIM, OUT = (4, 256, 512, 512)
        E, R, TOP_K = (8, 16, 2)
        SCALING = 16.0 / R
        result = jnp.einsum('bnd,od->bno', x, W_base) + b_base
        logits = jnp.einsum('bnd,ed->bne', x, W_gate)
        probs = jax.nn.softmax(logits.astype(jnp.float32), axis=-1)
        top_p, top_i = jax.lax.top_k(probs, TOP_K)
        top_p = top_p / jnp.sum(top_p, axis=-1, keepdims=True)
        top_p = top_p.astype(x.dtype)
        route_w = jnp.sum(jax.nn.one_hot(top_i, E, dtype=x.dtype) * top_p[..., None], axis=-2)
        h = jnp.einsum('bnd,erd->bner', x, A)
        hw = h * route_w[..., None]
        delta = jnp.einsum('bner,eor->bno', hw, B)
        return result + delta * SCALING
    x = L0_attn_a_hidden_states
    x = x + _L0_attn_a_ref(_layernorm(x, axis=-1), L0_attn_a_Wqkv, L0_attn_a_q_ln_w, L0_attn_a_q_ln_b, L0_attn_a_k_ln_w, L0_attn_a_k_ln_b, L0_attn_a_Wout)
    x = x + _L0_ffn_ref(_layernorm(x, axis=-1), L0_ffn_W_base, L0_ffn_b_base, L0_ffn_W_gate, L0_ffn_A, L0_ffn_B)
    x = x + _L0_attn_b_ref(_layernorm(x, axis=-1), L0_attn_b_Wq, L0_attn_b_bq, L0_attn_b_Wk, L0_attn_b_bk, L0_attn_b_Wv, L0_attn_b_bv, L0_attn_b_Wo, L0_attn_b_bo)
    x = x + _L0_ffn_ref(_layernorm(x, axis=-1), L0_ffn_W_base, L0_ffn_b_base, L0_ffn_W_gate, L0_ffn_A, L0_ffn_B)
    return x

_drawn_inputs = setup_inputs


def setup_inputs(seed=0):
    import zlib

    import numpy as np

    out = dict(_drawn_inputs(seed))
    spreads = {'L0_attn_a_q_ln_w': (1.0, 0.6),
     'L0_attn_a_q_ln_b': (0.0, 0.8),
     'L0_attn_a_k_ln_w': (1.0, 0.6),
     'L0_attn_a_k_ln_b': (0.0, 0.8)}
    factors = {'L0_attn_b_bq': 8.0, 'L0_attn_b_bk': 8.0, 'L0_ffn_b_base': 5.855}
    for name, (base, spread) in spreads.items():
        noise = np.random.default_rng([zlib.crc32(name.encode()), seed]).standard_normal(out[name].shape)
        drawn = base * np.exp(spread * noise) if base else spread * noise
        out[name] = jnp.asarray(drawn.astype(out[name].dtype))
    for name, factor in factors.items():
        out[name] = (out[name] * factor).astype(out[name].dtype)
    return out
```

```python
from contextlib import ExitStack

import concourse.bass as bass
from concourse import mybir

F32 = mybir.dt.float32
F32R = mybir.dt.float32r
BF16 = mybir.dt.bfloat16
ALU = mybir.AluOpType
ACT = mybir.ActivationFunctionType
AX_X = mybir.AxisListType.X

P = 128
D = 512
KC = D // P
H = 32
HD = D // H
SEQ = 256
NT = SEQ // P
NB = 4
NP = H // 2
NG = NP // 4
E = 8
R = 16
STAGES = 2 * NB
HROWS = 64
EXTRA = 3 * HD
LAG = 6
PT_RING = 3
LN_EPS = 1e-5
CLIP = 8.0


def iteration_plan(g):
    last, nxt = g - 1, g + 1
    has_last, has_next = last >= 0, nxt < STAGES
    steps = []

    def add(cond, *step):
        if cond:
            steps.append(step)

    if g < STAGES:
        add(has_next, "ln1", nxt)
        add(True, "t", g, 0)
    add(has_last, "at", last, 0)
    add(has_last, "wo", last, 0)
    if g < STAGES:
        add(True, "expand", g, 1)
    add(has_last, "at", last, 1)
    add(has_last, "wo", last, 1)
    if g < STAGES:
        add(True, "t", g, 1)
        add(True, "vcopy", g)
    add(has_last, "wo_out", last, 0)
    add(has_last, "wo_out", last, 1)
    fill = {}

    def put(slot, cond, *step):
        if cond:
            fill.setdefault(slot, []).append(step)

    put(0, has_next, "xt", nxt, 0)
    put(1, has_next, "qkv", nxt, 0, 0)
    put(2, has_last, "ln2", last)
    put(2, has_next, "qkv", nxt, 0, 1)
    put(3, has_next, "qkv_out", nxt, 0, 0)
    put(3, has_next, "qkv", nxt, 0, 2)
    put(4, has_next, "qkv_out", nxt, 0, 1)
    put(4, has_last, "x2t", last, 0)
    put(5, has_next, "qkv_out", nxt, 0, 2)
    put(5, has_last, "x2t", last, 1)
    put(6, has_last, "h", last, 0)
    put(6, has_last, "h", last, 1)
    put(7, has_last, "route", last)
    put(8, has_next, "xt", nxt, 1)
    put(9, has_next, "expand", nxt, 0)
    put(10, has_last, "hwt", last)
    put(11, has_last, "ffn", last, 0)
    put(13, has_last, "ffn", last, 1)
    put(14, has_last, "ffn_out", last, 0)
    put(15, has_next, "qkv", nxt, 1, 0)
    put(16, has_last, "ffn_out", last, 1)
    put(17, has_next, "qkv_out", nxt, 1, 0)
    put(17, has_next, "qkv", nxt, 1, 1)
    put(19, has_next, "qkv_out", nxt, 1, 1)
    put(19, has_next, "qkv", nxt, 1, 2)
    put(21, has_next, "qkv_out", nxt, 1, 2)
    for s in range(NP + LAG + 3):
        if g < STAGES:
            add(s < NP, "s", g, s)
            if s % 4 == 0 and 4 <= s <= NP:
                add(True, "m", g, s // 4 - 1)
            p = s - LAG
            add(0 <= p < NP, "st", g, p)
        steps += fill.get(s, [])
        if g < STAGES:
            add(p >= 2 and p % 2 == 0 and p // 2 - 1 < NP // 2, "pv", g, p // 2 - 1)
            add(p >= 3 and p % 2 == 1 and (p - 3) // 2 < NP // 2 and (p - 3) // 2 >= 0, "o", g, (p - 3) // 2)
            if s == NP + LAG + 2:
                add(True, "o", g, NP // 2 - 1)
    return steps


def whole_plan():
    steps = [("ln1", 0), ("xt", 0, 0)]
    steps += [("qkv", 0, 0, n) for n in range(3)] + [("qkv_out", 0, 0, n) for n in range(3)]
    steps += [("expand", 0, 0), ("xt", 0, 1)]
    steps += [("qkv", 0, 1, n) for n in range(3)] + [("qkv_out", 0, 1, n) for n in range(3)]
    for g in range(STAGES + 1):
        steps += iteration_plan(g)
    return list(dict.fromkeys(steps))


def build(nc, x_in, consts, wqkv, wout, wbase, wgate, wlow, rows, mid, out):
    c_ident, c_small, c_kaug, c_qaug, c_kblock = consts
    plan = whole_plan()

    mm_units = [s for s in plan if s[0] in ("wo", "h", "ffn", "qkv")]
    tr_units = [s for s in plan if s[0] in ("xt", "at", "x2t", "hwt", "m", "o")]
    mm_no = {s: n for n, s in enumerate(mm_units)}
    tr_no = {s: n for n, s in enumerate(tr_units)}

    with ExitStack() as ctx:
        def sb(name, shape, dt=F32):
            return ctx.enter_context(nc.sbuf_tensor(name, shape, dt))

        def sem(name):
            return ctx.enter_context(nc.semaphore(name))

        wq_h = sb("wq_h", [P, 3, KC, D], F32R)
        wq_l = sb("wq_l", [P, 3, KC, D], F32R)
        wo_h = sb("wo_h", [P, KC, D], F32R)
        wo_l = sb("wo_l", [P, KC, D], F32R)
        wb_h = sb("wb_h", [P, KC, D], F32R)
        wb_l = sb("wb_l", [P, KC, D], F32R)
        wg_h = sb("wg_h", [P, KC, E + E * R], F32R)
        wg_l = sb("wg_l", [P, KC, E + E * R], F32R)
        wl_h = sb("wl_h", [P, D], F32R)
        wl_l = sb("wl_l", [P, D], F32R)
        stage = sb("stage", [P, 2, D])
        row = sb("row", [P, 5, D])
        qt = sb("qt", [P, NP, SEQ], F32R)
        kt = sb("kt", [P, NP, SEQ], F32R)
        qa = sb("qa", [P, H, HROWS], F32R)
        ka = sb("ka", [P, H, HROWS], F32R)
        qf = sb("qf", [P, 2, D])
        vn = sb("vn", [P, NT, D])
        v = sb("v", [P, NT, H, HD + 1])
        pt = sb("pt", [P, PT_RING, 2, SEQ + P])
        xa = sb("xa", [P, NT, D])
        x2 = sb("x2", [P, NT, D])
        xt_h = sb("xt_h", [P, NT, KC, P], F32R)
        xt_l = sb("xt_l", [P, NT, KC, P], F32R)
        at_h = sb("at_h", [P, NT, KC, P], F32R)
        at_l = sb("at_l", [P, NT, KC, P], F32R)
        on = sb("on", [P, NT, D])
        ot = sb("ot", [P, SEQ])
        hs = sb("hs", [P, NT, E + E * R])
        hw_h = sb("hw_h", [P, NT, P], F32R)
        hw_l = sb("hw_l", [P, NT, P], F32R)
        ident_r = sb("ident_r", [P, P], F32R)
        ident = ident_r[:, :].bitcast(F32)
        cbf = sb("cbf", [P, 2 * P], BF16)
        nmt_f = hs[:, 0, 0:P]
        kblock = sb("kblock", [P, H, 2])
        fence = sb("fence", [P, 2, NT, 8], BF16)
        tri = sb("tri", [P, E, E], BF16)
        neg_half = sb("neg_half", [P, 2])
        st1 = sb("st1", [P, NT, 6])
        mv1 = sb("mv1", [P, NT, 2])
        ve1 = sb("ve1", [P, NT])
        rs1 = sb("rs1", [P, NT])
        st2 = sb("st2", [P, NT, 6])
        mv2 = sb("mv2", [P, NT, 2])
        ve2 = sb("ve2", [P, NT])
        rs2 = sb("rs2", [P, NT])
        stq = sb("stq", [P, 2, 6])
        mvq = sb("mvq", [P, 2, 2])
        veq = sb("veq", [P, 2])
        rsq = sb("rsq", [P, 2])
        pm = sb("pm", [P, NP, 2, 3])
        nm = sb("nm", [P, 2, 4, NT])
        nms = sb("nms", [P, NG, 2, 2, 4 * NT], F32R)
        nmt = sb("nmt", [P, P], F32R)
        rc = sb("rc", [P, NT, 4])
        mxl = sb("mxl", [P, NT])
        zl = sb("zl", [P, NT, E])
        el = sb("el", [P, NT, E])
        esum = sb("esum", [P, NT])
        erec = sb("erec", [P, NT])
        pr = sb("pr", [P, NT, E])
        gt = sb("gt", [P, NT * E, E], BF16)
        ge = sb("ge", [P, NT * E, E], BF16)
        rank = sb("rank", [P, NT, E])

        ps_s = ctx.enter_context(nc.psum_tensor("ps_s", [P, 1024], F32))
        ps_st = ctx.enter_context(nc.psum_tensor("ps_st", [P, 1024], F32))
        ps_mm = ctx.enter_context(nc.psum_tensor("ps_mm", [P, 2, D], F32))
        ps_tr = ctx.enter_context(nc.psum_tensor("ps_tr", [P, D], F32))
        ps_pv = ctx.enter_context(nc.psum_tensor("ps_pv", [P, D], F32))

        names = """const_in small_ready ident_ready kaug_ready rt2_step half_ready ones_ready nms_zeroed pv_zeroed
            stage_a stage_b stage_c wsplit_h wsplit_l row_in
            xa_in x2_in x2_bias ln1_step ln1_rstd ln1_norm xt_done xth_ready xtl_ready
            qkv_done qkv_out lnq_step lnq_rstd lnq_norm q_scaled q_ready exp_hi exp_lo aug_set
            t_done t_dve t_act v_copied s_done s_max nm_step mt_done nmt_copied mrow_in
            st_done st_exp p_masked pv_done o_copied ot_done o_rec o_norm at_done ath_ready atl_ready
            wo_done wo_out ln2_step ln2_rstd ln2_norm x2t_done x2h_ready x2l_ready x2_plus
            h_done h_out rt_step rt_exp hw_ready hwt_done hwh_ready hwl_ready ffn_done y_ready y_stored""".split()
        S = {n: sem(n) for n in names}

        def v_tile(g, t):
            return NT * g + t + 1

        reads_done = {
            "xt": lambda g, t: (S["xtl_ready"], v_tile(g, t)),
            "at": lambda g, t: (S["atl_ready"], v_tile(g, t)),
            "x2t": lambda g, t: (S["x2l_ready"], v_tile(g, t)),
            "hwt": lambda g: (S["hwl_ready"], g + 1),
            "m": lambda g, n: (S["nmt_copied"], NG * g + n + 1),
            "o": lambda g, n: (S["o_norm"], NP // 2 * g + n + 1),
            "wo": lambda g, t: (S["wo_out"], v_tile(g, t)),
            "h": lambda g, t: (S["h_out"], v_tile(g, t)),
            "ffn": lambda g, t: (S["y_ready"], v_tile(g, t)),
            "qkv": lambda g, t, n: (S["qkv_out"], 3 * NT * g + 3 * t + n + 1),
        }

        def wait_tr_free(eng, step):
            if tr_no[step] >= 1:
                prev = tr_units[tr_no[step] - 1]
                eng.wait_ge(*reads_done[prev[0]](*prev[1:]))

        def wait_mm_free(eng, step):
            if mm_no[step] >= 2:
                prev = mm_units[mm_no[step] - 2]
                eng.wait_ge(*reads_done[prev[0]](*prev[1:]))

        def mm_bank(step):
            return ps_mm[:, mm_no[step] % 2, :]

        def chunks(kind):
            big = [(wqkv[kind, n, c], wq_h[:, n, c, :], wq_l[:, n, c, :]) for n in range(3) for c in range(KC)]
            small = [(wout[kind, c], wo_h[:, c, :], wo_l[:, c, :]) for c in range(KC)]
            return big, small

        big_a, out_a = chunks(0)
        big_b, out_b = chunks(1)
        ffn_w = [(wbase[c], wb_h[:, c, :], wb_l[:, c, :]) for c in range(KC)]
        ffn_w += [(wgate[c], wg_h[:, c, :], wg_l[:, c, :]) for c in range(KC)]
        ffn_w += [(wlow, wl_h[:, :], wl_l[:, :])]
        pieces = big_a + out_a + ffn_w + big_b + out_b
        N_QKV_A = len(big_a)
        N_OUT_A = N_QKV_A + len(out_a)
        N_FFN = N_OUT_A + len(ffn_w)
        N_QKV_B = N_FFN + len(big_b)
        N_OUT_B = N_QKV_B + len(out_b)
        N_EARLY = N_QKV_A
        ring = [stage[:, 0, :], stage[:, 1, :], *(pt[:, i, :, :].rearrange("p e q -> p (e q)")[:, 0:D] for i in range(PT_RING))]
        sem_in = [sem(f"piece_in{i}") for i in range(len(ring))]
        slot_of, count_of, uses, prev_of = [], [], [0] * len(ring), []
        last_use = {}
        for n in range(len(pieces)):
            i = n % len(ring) if n < N_EARLY else n % 2
            slot_of.append(i)
            uses[i] += 1
            count_of.append(16 * uses[i])
            prev_of.append(last_use.get(i))
            last_use[i] = n

        def width(n):
            return pieces[n][0].shape[-1]

        block = ctx.enter_context(nc.Block())

        @block.sync
        def _(sp):
            def load_piece(n):
                if prev_of[n] is not None:
                    sp.wait_ge(S["wsplit_l"], prev_of[n] + 1)
                if n == N_FFN:
                    sp.wait_ge(S["qkv_done"], 3 * NT * NB)
                sp.dma_start(ring[slot_of[n]][:, 0:width(n)], pieces[n][0]).then_inc(sem_in[slot_of[n]], 16)

            def source(g):
                src = x_in if g < NB else mid
                b = g % NB
                return src[b * SEQ:(b + 1) * SEQ, :].rearrange("(t p) d -> p t d", p=P)

            sp.dma_start(xa[:, :, :], source(0)).then_inc(S["xa_in"], 16)
            load_piece(0)
            load_piece(1)
            sp.dma_start(nmt_f[:, :], c_ident).then_inc(S["const_in"], 16)
            sp.dma_start(qf[:, 0, 0:c_small.shape[-1]], c_small).then_inc(S["const_in"], 16)
            sp.dma_start(kblock[:, :, :], c_kblock).then_inc(S["const_in"], 16)
            sp.dma_start(x2[:, 0, :], c_kaug).then_inc(S["const_in"], 16)
            sp.dma_start(x2[:, 1, :], c_qaug).then_inc(S["const_in"], 16)
            for n in range(2, 5):
                load_piece(n)
            for n in range(4):
                sp.dma_start(row[:, n, :], rows[n:n + 1, :].partition_broadcast(P)).then_inc(S["row_in"], 16)
            sp.dma_start(row[:, 4, :], rows[8:9, :].partition_broadcast(P)).then_inc(S["row_in"], 16)
            for n in range(5, N_FFN):
                load_piece(n)
            sp.wait_ge(S["kaug_ready"], 2)
            sp.dma_start(x2[:, :, :], source(0)).then_inc(S["x2_in"], 16)

            for step in plan:
                kind, g = step[0], step[1]
                if kind == "xt" and step[2] == 1 and g + 1 < STAGES:
                    sp.wait_ge(S["xt_done"], v_tile(g, 1))
                    if g + 1 >= NB:
                        sp.wait_ge(S["y_stored"], 16 * (g + 1 - NB + 1))
                    sp.dma_start(xa[:, :, :], source(g + 1)).then_inc(S["xa_in"], 16)
                if kind == "m":
                    n = step[2]
                    sp.wait_ge(S["nmt_copied"], NG * g + n + 1)
                    for e in range(2):
                        r0 = 32 * n + 16 * e
                        sp.dma_start(qt[HROWS * e + EXTRA:HROWS * e + EXTRA + 2, 4 * n:4 * n + 4, :]
                                     .bitcast(F32),
                                     nmt[r0:r0 + 16, :].bitcast(F32)).then_inc(S["mrow_in"], 16)
                if kind == "ffn_out" and step[2] == 1:
                    sp.wait_ge(S["y_ready"], v_tile(g, 1))
                    dst = mid if g < NB else out
                    b = g % NB
                    sp.dma_start(dst[b * SEQ:(b + 1) * SEQ, :].rearrange("(t p) d -> p t d", p=P),
                                 x2[:, :, :]).then_inc(S["y_stored"], 16)
                    if g + 1 < STAGES:
                        sp.wait_ge(S["y_stored"], 16 * (g + 1))
                        sp.dma_start(x2[:, :, :], source(g + 1)).then_inc(S["x2_in"], 16)
                if kind == "qkv_out" and g == NB - 1 and step[2:] == (1, 2):
                    sp.wait_ge(S["q_ready"], 2 * NT * NB)
                    for n in range(4):
                        sp.dma_start(row[:, n, :], rows[4 + n:5 + n, :].partition_broadcast(P))\
                          .then_inc(S["row_in"], 16)
                    for n in range(N_FFN, N_QKV_B):
                        load_piece(n)
                if kind == "wo_out" and g == NB - 1 and step[2] == 1:
                    for n in range(N_QKV_B, N_OUT_B):
                        load_piece(n)
            sp.wait_ge(S["y_stored"], 16 * STAGES)

        @block.tensor
        def _(pe):
            def split_product(dst, a_h, a_l, b_h, b_l, n_chunks, start=True, stop=True):
                todo = [(a, b, c) for c in range(n_chunks) for a, b in ((a_h, b_h), (a_h, b_l), (a_l, b_h))]
                for i, (a, b, c) in enumerate(todo):
                    ins = pe.matmul(dst, a(c), b(c), start=start and i == 0, stop=stop and i == len(todo) - 1)
                return ins

            def turn(src, parts, done):
                for c in range(parts):
                    ins = pe.transpose(ps_tr[:, c * P:(c + 1) * P], src(c), ident)
                ins.then_inc(done, 1)

            def xt(g, t):
                pe.wait_ge(S["ln1_norm"], v_tile(g, t))
                wait_tr_free(pe, ("xt", g, t))
                turn(lambda c: xa[:, t, c * P:(c + 1) * P], KC, S["xt_done"])

            def qkv(g, t, n):
                pe.wait_ge(S["xtl_ready"], v_tile(g, t))
                wait_mm_free(pe, ("qkv", g, t, n))
                pe.wait_ge(S["wsplit_l"], (0 if g < NB else N_FFN) + KC * (n + 1))
                split_product(mm_bank(("qkv", g, t, n)), lambda c: xt_h[:, t, c, :], lambda c: xt_l[:, t, c, :],
                              lambda c: wq_h[:, n, c, :], lambda c: wq_l[:, n, c, :], KC).then_inc(S["qkv_done"], 1)

            def t_step(g, t):
                pe.wait_ge(S["exp_lo"], 2 * v_tile(g, t))
                pe.wait_ge(S["aug_set"], v_tile(g, t))
                for u, src in enumerate((qa, ka)):
                    for half in range(2):
                        dst = (ps_s, ps_st)[half]
                        k = 4 * g + 2 * t + u
                        if half == 0:
                            if k >= 1:
                                pe.wait_ge(S["t_dve"], k)
                            pe.wait_ge(S["s_max"], NP * g) if g else None
                        else:
                            if k >= 1:
                                pe.wait_ge(S["t_act"], k)
                            pe.wait_ge(S["st_exp"], NP * g) if g else None
                        for i in range(8):
                            p = 8 * half + i
                            ins = pe.matmul(dst[:, i * P:(i + 1) * P], src[:, 2 * p:2 * p + 2, :], ident_r[:, :],
                                            start=True, stop=True)
                        ins.then_inc(S["t_done"], 1)

            def s_step(g, p):
                if p == 0:
                    pe.wait_ge(S["t_dve"], 4 * g + 4)
                    pe.wait_ge(S["t_act"], 4 * g + 4)
                else:
                    pe.wait_ge(S["s_max"], NP * g + p)
                for e in range(2):
                    bank = ps_s[:, e * D:(e + 1) * D]
                    pe.matmul(bank[:, 0:2 * P], cbf[:, 0:P],
                              cbf[:, P:2 * P].rearrange("p (r k) -> p r k", r=1).broadcast_to([P, 2, P]),
                              start=True, stop=False, skip_group_check=True)
                for e in range(2):
                    r = slice(HROWS * e, HROWS * (e + 1))
                    bank = ps_s[:, e * D:(e + 1) * D]
                    pe.matmul(bank[:, 0:P], qt[r, p, 0:P], kt[r, p, 0:P], start=False, stop=False,
                              skip_group_check=True)
                    pe.matmul(bank[:, P:2 * P], qt[r, p, P:2 * P], kt[r, p, P:2 * P], start=False, stop=False,
                              skip_group_check=True)
                    ins = pe.matmul(bank[:, 2 * P:3 * P], qt[r, p, P:2 * P], kt[r, p, 0:P], start=False,
                                    stop=True, skip_group_check=True)
                ins.then_inc(S["s_done"], 1)

            def m_step(g, n):
                pe.wait_ge(S["nm_step"], 4 * (NG * g + n + 1))
                wait_tr_free(pe, ("m", g, n))
                pe.matmul(ps_tr[:, 0:P], nms[:, :, :, :, :], ident_r[:, :], start=True, stop=True)\
                  .then_inc(S["mt_done"], 1)

            def st_step(g, p):
                if p:
                    pe.wait_ge(S["st_exp"], NP * g + p)
                if p % 4 == 0:
                    pe.wait_ge(S["mrow_in"], 32 * (NG * g + p // 4 + 1))
                for e in range(2):
                    r = slice(HROWS * e, HROWS * (e + 1))
                    bank = ps_st[:, e * D:(e + 1) * D]
                    pe.matmul(bank[:, 0:3 * P].rearrange("p (b q) -> p b q", b=3)[:, 0:3:2, :], kt[r, p, 0:P],
                              qt[r, p, :].rearrange("p (b q) -> p b q", b=2), start=True, stop=True)
                    ins = pe.matmul(bank[:, P:2 * P], kt[r, p, P:2 * P], qt[r, p, P:2 * P], start=True,
                                    stop=True)
                ins.then_inc(S["st_done"], 1)

            def pv_step(g, n):
                pe.wait_ge(S["p_masked"], NP * g + 2 * n + 2)
                if n == 0:
                    pe.wait_ge(S["v_copied"], g + 1)
                k = NP // 2 * g + n
                pe.wait_ge(S["o_copied"], k) if k else pe.wait_ge(S["pv_zeroed"], 1)
                for part in range(NT):
                    for j in range(4):
                        h, e = 4 * n + j, j % 2
                        pair = pt[:, (2 * n + j // 2) % PT_RING, e, :]
                        if part == 0:
                            rhs = pair.rearrange("p (b q) -> p b q", b=3)[:, 0:3:2, :]
                            cols = slice(0, SEQ)
                        else:
                            rhs, cols = pair[:, P:2 * P], slice(P, SEQ)
                        ins = pe.matmul(ps_pv[32 * j:32 * j + HD + 1, cols], v[:, part, h, :], rhs,
                                        start=part == 0, stop=part == 1, skip_group_check=True,
                                        tile_position=(0, 32 * j))
                ins.then_inc(S["pv_done"], 1)

            def o_step(g, n):
                k = NP // 2 * g + n
                pe.wait_ge(S["o_copied"], k + 1)
                wait_tr_free(pe, ("o", g, n))
                for t in range(NT):
                    ins = pe.transpose(ps_tr[:, t * P:(t + 1) * P], ot[:, t * P:(t + 1) * P], ident)
                ins.then_inc(S["ot_done"], 1)

            def at(g, t):
                pe.wait_ge(S["o_norm"], NP // 2 * (g + 1))
                wait_tr_free(pe, ("at", g, t))
                turn(lambda c: on[:, t, c * P:(c + 1) * P], KC, S["at_done"])

            def wo(g, t):
                pe.wait_ge(S["atl_ready"], v_tile(g, t))
                wait_mm_free(pe, ("wo", g, t))
                pe.wait_ge(S["wsplit_l"], N_OUT_A if g < NB else N_OUT_B)
                split_product(mm_bank(("wo", g, t)), lambda c: at_h[:, t, c, :], lambda c: at_l[:, t, c, :],
                              lambda c: wo_h[:, c, :], lambda c: wo_l[:, c, :], KC).then_inc(S["wo_done"], 1)

            def x2t(g, t):
                pe.wait_ge(S["ln2_norm"], v_tile(g, t))
                wait_tr_free(pe, ("x2t", g, t))
                turn(lambda c: on[:, t, c * P:(c + 1) * P], KC, S["x2t_done"])

            def h_step(g, t):
                pe.wait_ge(S["x2l_ready"], v_tile(g, t))
                wait_mm_free(pe, ("h", g, t))
                pe.wait_ge(S["wsplit_l"], N_FFN)
                split_product(mm_bank(("h", g, t))[:, 0:E + E * R], lambda c: at_h[:, t, c, :],
                              lambda c: at_l[:, t, c, :], lambda c: wg_h[:, c, :], lambda c: wg_l[:, c, :], KC)\
                    .then_inc(S["h_done"], 1)

            def hwt(g):
                pe.wait_ge(S["hw_ready"], g + 1)
                wait_tr_free(pe, ("hwt", g))
                turn(lambda t: hs[:, t, E:E + E * R], NT, S["hwt_done"])

            def ffn(g, t):
                wait_mm_free(pe, ("ffn", g, t))
                dst = mm_bank(("ffn", g, t))
                split_product(dst, lambda c: at_h[:, t, c, :], lambda c: at_l[:, t, c, :],
                              lambda c: wb_h[:, c, :], lambda c: wb_l[:, c, :], KC, stop=False)
                pe.wait_ge(S["hwl_ready"], g + 1)
                split_product(dst, lambda c: hw_h[:, t, :], lambda c: hw_l[:, t, :],
                              lambda c: wl_h[:, :], lambda c: wl_l[:, :], 1, start=False)\
                    .then_inc(S["ffn_done"], 1)

            pe.wait_ge(S["const_in"], 16 * 5)
            pe.wait_ge(S["ident_ready"], 1)
            pe.wait_ge(S["small_ready"], 1)
            does = {"xt": xt, "qkv": qkv, "t": t_step, "s": s_step, "m": m_step, "st": st_step, "pv": pv_step,
                    "o": o_step, "at": at, "wo": wo, "x2t": x2t, "h": h_step, "hwt": hwt, "ffn": ffn}
            for step in plan:
                if step[0] in does:
                    does[step[0]](*step[1:])

        @block.scalar
        def _(act):
            def split_high(n):
                act.wait_ge(sem_in[slot_of[n]], count_of[n])
                if n == N_FFN:
                    act.wait_ge(S["qkv_done"], 3 * NT * NB)
                if n == N_QKV_B:
                    act.wait_ge(S["wo_done"], NT * NB)
                nc.scalar.activation(pieces[n][1], ring[slot_of[n]][:, 0:width(n)], ACT.Copy)\
                    .then_inc(S["wsplit_h"], 1)

            def high(dst, done, ready, n):
                act.wait_ge(done, n)
                nc.scalar.activation(dst, ps_tr[:, :].rearrange("p (c q) -> p c q", c=KC), ACT.Copy).then_inc(ready, 1)

            def xt(g, t):
                if g:
                    act.wait_ge(S["qkv_done"], 3 * NT * (g - 1) + 3 * t + 3)
                high(xt_h[:, t, :, :], S["xt_done"], S["xth_ready"], v_tile(g, t))

            def expand(g, t):
                for u, dst in enumerate((qa, ka)):
                    act.wait_ge(S["q_ready"], 2 * (NT * g + t) + u + 1)
                    k = NT * g + t
                    if k:
                        act.wait_ge(S["t_done"], 4 * k)
                    act.wait_ge(S["kaug_ready"], 2) if k == 0 else None
                    step = (2, 1)[u]
                    o = dst[:, :, 0:EXTRA + HD].rearrange("p h (r d) -> p h r d", d=HD)[:, :, 0:step + 1:step, :]
                    i = qf[:, u, :].rearrange("p (h r d) -> p h r d", h=H, r=1).broadcast_to([P, H, 2, HD])
                    nc.scalar.activation(o, i, ACT.Copy).then_inc(S["exp_hi"], 1)

            def t_step(g, t):
                for u, dst in enumerate((qt, kt)):
                    act.wait_ge(S["t_done"], 4 * (NT * g + t) + 2 * u + 2)
                    nc.scalar.activation(dst[:, 8:16, t * P:(t + 1) * P],
                                         ps_st[:, :].rearrange("p (i q) -> p i q", i=8), ACT.Copy)\
                        .then_inc(S["t_act"], 1)

            def v_copy(g):
                if g:
                    act.wait_ge(S["pv_done"], NP // 2 * g)
                else:
                    act.wait_ge(S["ones_ready"], 1)
                act.wait_ge(S["qkv_out"], 3 * NT * (g + 1))
                nc.scalar.activation(v[:, :, :, 0:HD], vn[:, :, :].rearrange("p t (h d) -> p t h d", d=HD), ACT.Copy)\
                    .then_inc(S["v_copied"], 1)

            def m_step(g, n):
                act.wait_ge(S["mt_done"], NG * g + n + 1)
                if g:
                    act.wait_ge(S["mrow_in"], 32 * (NG * (g - 1) + n + 1))
                r = slice(32 * n, 32 * n + 32)
                nc.scalar.activation(nmt[r, :], ps_tr[r, 0:P], ACT.Copy).then_inc(S["nmt_copied"], 1)

            def st_step(g, p):
                act.wait_ge(S["st_done"], NP * g + p + 1)
                if p >= PT_RING:
                    act.wait_ge(S["pv_done"], NP // 2 * g + (p - PT_RING) // 2 + 1)
                elif g:
                    act.wait_ge(S["pv_done"], NP // 2 * g)
                else:
                    act.wait_ge(S["wsplit_l"], N_EARLY)
                nc.scalar.activation(pt[:, p % PT_RING, :, :],
                                     ps_st[:, :].rearrange("p (e q) -> p e q", e=2)[:, :, 0:SEQ + P], ACT.Exp, scale=HD ** -0.5)\
                    .then_inc(S["st_exp"], 1)

            def pv_step(g, n):
                k = NP // 2 * g + n
                act.wait_ge(S["pv_done"], k + 1)
                if k:
                    act.wait_ge(S["ot_done"], k)
                nc.scalar.activation(ot[:, :], ps_pv[:, 0:SEQ], ACT.Copy).then_inc(S["o_copied"], 1)

            def at(g, t):
                if g:
                    act.wait_ge(S["ffn_done"], v_tile(g - 1, t))
                high(at_h[:, t, :, :], S["at_done"], S["ath_ready"], v_tile(g, t))

            def x2t(g, t):
                act.wait_ge(S["wo_done"], v_tile(g, t))
                high(at_h[:, t, :, :], S["x2t_done"], S["x2h_ready"], v_tile(g, t))

            def route(g):
                act.wait_ge(S["rt_step"], 8 * g + 2)
                nc.scalar.activation(el[:, :, :], zl[:, :, :], ACT.Exp).then_inc(S["rt_exp"], 1)

            def hwt(g):
                act.wait_ge(S["hwt_done"], g + 1)
                if g:
                    act.wait_ge(S["ffn_done"], NT * g)
                nc.scalar.activation(hw_h[:, :, :], ps_tr[:, 0:NT * P].rearrange("p (t q) -> p t q", t=NT), ACT.Copy)\
                    .then_inc(S["hwh_ready"], 1)

            def qkv_out(g, t, n):
                if g == NB - 1 and (t, n) == (1, 2):
                    for k in range(N_FFN, N_QKV_B):
                        split_high(k)

            def wo_out(g, t):
                if g == NB - 1 and t == 1:
                    for k in range(N_QKV_B, N_OUT_B):
                        split_high(k)

            for n in range(N_QKV_A):
                split_high(n)
            does = {"xt": xt, "expand": expand, "t": t_step, "vcopy": v_copy, "m": m_step, "st": st_step,
                    "pv": pv_step, "at": at, "x2t": x2t, "route": route, "hwt": hwt, "qkv_out": qkv_out,
                    "wo_out": wo_out}
            for step in plan:
                if step == ("ln1", 1):
                    for n in range(N_QKV_A, N_FFN):
                        split_high(n)
                if step[0] in does:
                    does[step[0]](*step[1:])

        @block.gpsimd
        def _(pool):
            def split_low(n):
                pool.wait_ge(S["wsplit_h"], n + 1)
                w = width(n)
                nc.gpsimd.tensor_tensor(pieces[n][2], ring[slot_of[n]][:, 0:w], pieces[n][1], ALU.subtract)\
                    .then_inc(S["wsplit_l"], 1)

            def power(dst, src, n):
                return nc.gpsimd.tensor_tensor(dst, src, neg_half[:, 0:n], ALU.pow)

            def ln1(g):
                pool.wait_ge(S["ln1_step"], 3 * NT * (g + 1))
                if g:
                    pool.wait_ge(S["ln1_norm"], NT * g)
                power(rs1[:, :], ve1[:, :], NT).then_inc(S["ln1_rstd"], 1)

            def ln2(g):
                pool.wait_ge(S["ln2_step"], 3 * NT * (g + 1))
                if g:
                    pool.wait_ge(S["ln2_norm"], NT * g)
                power(rs2[:, :], ve2[:, :], NT).then_inc(S["ln2_rstd"], 1)

            def qkv_out(g, t, n):
                if n < 2 and g < NB:
                    k = 2 * (NT * g + t) + n
                    pool.wait_ge(S["lnq_step"], 3 * (k + 1))
                    power(rsq[:, n:n + 1], veq[:, n:n + 1], 1).then_inc(S["lnq_rstd"], 1)
                    pool.wait_ge(S["lnq_norm"], k + 1)
                    pool.wait_ge(S["row_in"], 16 * 5) if k == 0 else None
                    nc.gpsimd.tensor_tensor(qf[:, n, :], qf[:, n, :], row[:, 2 * n, :], ALU.mult)\
                        .then_inc(S["q_scaled"], 1)
                    pool.wait_ge(S["q_scaled"], k + 1)
                    nc.gpsimd.tensor_tensor(qf[:, n, :], qf[:, n, :], row[:, 2 * n + 1, :], ALU.add)\
                        .then_inc(S["q_ready"], 1)
                if g == NB - 1 and (t, n) == (1, 2):
                    for k in range(N_FFN, N_QKV_B):
                        split_low(k)

            def expand(g, t):
                for u, dst in enumerate((qa, ka)):
                    k = 2 * (NT * g + t) + u
                    pool.wait_ge(S["exp_hi"], k + 1)
                    c = (HD, 2 * HD)[u]
                    nc.gpsimd.tensor_tensor(dst[:, :, c:c + HD],
                                            qf[:, u, :].rearrange("p (h d) -> p h d", d=HD),
                                            dst[:, :, 0:HD], ALU.subtract).then_inc(S["exp_lo"], 1)
                for dst, c in ((qa, 0), (ka, 1)):
                    nc.gpsimd.tensor_copy(dst[:, :, EXTRA + 8:HROWS],
                                          fence[:, c, t, :].rearrange("p (h r) -> p h r", h=1)
                                          .broadcast_to([P, H, 8]))
                if g < NB:
                    nc.gpsimd.memset(qa[:, :, EXTRA + 6:EXTRA + 8].bitcast(F32), float(t))
                    if t == 0:
                        nc.gpsimd.tensor_copy(ka[:, :, EXTRA + 6:EXTRA + 8], kblock[:, :, :])\
                            .then_inc(S["aug_set"], 1)
                    else:
                        nc.gpsimd.memset(ka[:, :, EXTRA + 6:EXTRA + 8].bitcast(F32), 0.0).then_inc(S["aug_set"], 1)
                else:
                    nc.gpsimd.memset(ka[:, :, EXTRA + 2:EXTRA + 8].bitcast(F32), 0.0).then_inc(S["aug_set"], 1)

            def st_step(g, p):
                pool.wait_ge(S["st_exp"], NP * g + p + 1)
                w = pt[:, p % PT_RING, :, 0:2 * P]
                ins = nc.gpsimd.affine_select(out=w, in_=w, compare_op=ALU.is_ge, fill=0.0, base=0,
                                              pattern=[[0, 4], [1, P]], channel_multiplier=-1)
                ins.then_inc(S["p_masked"], 1)

            def wo_out(g, t):
                if g == NB - 1 and t == 1:
                    for k in range(N_QKV_B, N_OUT_B):
                        split_low(k)

            def h_step(g, t):
                pool.wait_ge(S["ln2_norm"], v_tile(g, t))
                nc.gpsimd.tensor_tensor(x2[:, t, :], x2[:, t, :], row[:, 4, :], ALU.add).then_inc(S["x2_plus"], 1)

            def at(g, t):
                if g >= NB:
                    if t == 0:
                        pool.wait_ge(S["x2_in"], 16 * (g + 1))
                        pool.wait_ge(S["row_in"], 16 * 9)
                    nc.gpsimd.tensor_tensor(x2[:, t, :], x2[:, t, :], row[:, 3, :], ALU.add)\
                        .then_inc(S["x2_bias"], 1)

            nc.gpsimd.memset(neg_half[:, :], -0.5).then_inc(S["half_ready"], 1)
            pool.wait_ge(S["half_ready"], 1)
            for n in range(N_QKV_A):
                split_low(n)
                if n == 3:
                    ln1(0)
            does = {"ln1": ln1, "ln2": ln2, "qkv_out": qkv_out, "expand": expand, "st": st_step, "wo_out": wo_out,
                    "h": h_step, "at": at}
            for step in plan:
                if step == ("ln1", 1):
                    for n in range(N_QKV_A, N_FFN):
                        split_low(n)
                if step != ("ln1", 0) and step[0] in does:
                    does[step[0]](*step[1:])

        @block.vector
        def _(dve):
            def norm_stats(src, st, mv, ve, steps, n):
                nc.vector.bn_stats(st, src).then_inc(steps, 1)
                dve.wait_ge(steps, 3 * n + 1)
                nc.vector.bn_aggr(mv, st).then_inc(steps, 1)
                dve.wait_ge(steps, 3 * n + 2)
                nc.vector.tensor_scalar(ve, mv[:, 1:2], LN_EPS, None, ALU.add).then_inc(steps, 1)

            def ln1(g):
                dve.wait_ge(S["xa_in"], 16 * (g + 1))
                for t in range(NT):
                    norm_stats(xa[:, t, :], st1[:, t, :], mv1[:, t, :], ve1[:, t:t + 1], S["ln1_step"], NT * g + t)
                dve.wait_ge(S["ln1_rstd"], g + 1)
                for t in range(NT):
                    nc.vector.tensor_scalar(xa[:, t, :], xa[:, t, :], mv1[:, t, 0:1], rs1[:, t:t + 1],
                                            ALU.subtract, ALU.mult).then_inc(S["ln1_norm"], 1)

            def low(hi, lo, ready_h, ready_l, n):
                dve.wait_ge(ready_h, n)
                nc.vector.tensor_tensor(lo, ps_tr[:, :].rearrange("p (c q) -> p c q", c=KC), hi, ALU.subtract)\
                    .then_inc(ready_l, 1)

            def xt(g, t):
                low(xt_h[:, t, :, :], xt_l[:, t, :, :], S["xth_ready"], S["xtl_ready"], v_tile(g, t))

            def qkv_out(g, t, n):
                src = mm_bank(("qkv", g, t, n))
                dve.wait_ge(S["qkv_done"], 3 * NT * g + 3 * t + n + 1)
                k = 2 * (NT * g + t) + n
                if n == 2:
                    dst = vn[:, t, :]
                    if g:
                        dve.wait_ge(S["v_copied"], g)
                else:
                    dst = qf[:, n, :]
                    if k >= 2:
                        dve.wait_ge(S["exp_lo"], k - 1)
                if g < NB:
                    nc.vector.tensor_scalar(dst, src, CLIP, -CLIP, ALU.min, ALU.max).then_inc(S["qkv_out"], 1)
                    if n < 2:
                        dve.wait_ge(S["qkv_out"], 3 * NT * g + 3 * t + n + 1)
                        norm_stats(dst, stq[:, n, :], mvq[:, n, :], veq[:, n:n + 1], S["lnq_step"], k)
                        dve.wait_ge(S["lnq_rstd"], k + 1)
                        nc.vector.tensor_scalar(dst, dst, mvq[:, n, 0:1], rsq[:, n:n + 1], ALU.subtract, ALU.mult)\
                            .then_inc(S["lnq_norm"], 1)
                else:
                    dve.wait_ge(S["row_in"], 16 * 9)
                    if n < 2:
                        nc.vector.tensor_tensor(dst, src, row[:, n, :], ALU.add).then_inc(S["qkv_out"], 1)
                        dve.wait_ge(S["qkv_out"], 3 * NT * g + 3 * t + n + 1)
                        nc.vector.engine_nop().then_inc(S["q_ready"], 1)
                    else:
                        nc.vector.tensor_tensor(dst, src, row[:, n, :], ALU.add).then_inc(S["qkv_out"], 1)

            def t_step(g, t):
                for u, dst in enumerate((qt, kt)):
                    dve.wait_ge(S["t_done"], 4 * (NT * g + t) + 2 * u + 1)
                    nc.vector.tensor_copy(dst[:, 0:8, t * P:(t + 1) * P],
                                          ps_s[:, :].rearrange("p (i q) -> p i q", i=8)).then_inc(S["t_dve"], 1)

            def s_step(g, p):
                dve.wait_ge(S["s_done"], NP * g + p + 1)
                nc.vector.tensor_reduce(pm[:, p, :, :],
                                        ps_s[:, :].rearrange("p (e b k) -> p e b k", e=2, b=4)[:, :, 0:3, :], AX_X,
                                        ALU.max, negate=True).then_inc(S["s_max"], 1)

            def m_step(g, n):
                k = 4 * (NG * g + n)
                dve.wait_ge(S["s_max"], NP * g + 4 * (n + 1))
                part = pm[:, 4 * n:4 * n + 4, :, :].rearrange("p i e b -> p e i b")
                nc.vector.tensor_copy(nm[:, :, :, 0], part[:, :, :, 0])\
                    .then_inc(S["nm_step"], 1)
                nc.vector.tensor_tensor(nm[:, :, :, 1], part[:, :, :, 1],
                                        part[:, :, :, 2], ALU.min)\
                    .then_inc(S["nm_step"], 1)
                flat = nm[:, :, :, :].rearrange("p e i t -> p e (i t)")
                dve.wait_ge(S["nm_step"], k + 2)
                if g or n:
                    dve.wait_ge(S["mt_done"], NG * g + n)
                else:
                    dve.wait_ge(S["nms_zeroed"], 1)
                nc.vector.tensor_copy(nms[:, n, :, 0, :], flat).then_inc(S["nm_step"], 1)
                dve.wait_ge(S["nm_step"], k + 3)
                nc.vector.tensor_tensor(nms[:, n, :, 1, :], flat, nms[:, n, :, 0, :], ALU.subtract)\
                    .then_inc(S["nm_step"], 1)

            def o_step(g, n):
                k = NP // 2 * g + n
                dve.wait_ge(S["ot_done"], k + 1)
                view = ps_tr[:, 0:NT * P].rearrange("p (t j r) -> p t j r", t=NT, j=4)
                if k:
                    dve.wait_ge(S["o_norm"], k)
                nc.vector.reciprocal(rc[:, :, :], view[:, :, :, HD]).then_inc(S["o_rec"], 1)
                dve.wait_ge(S["o_rec"], k + 1)
                if g and n == 0:
                    dve.wait_ge(S["x2t_done"], NT * g)
                o = on[:, :, 4 * HD * n:4 * HD * (n + 1)].rearrange("p t (j d) -> p t j d", j=4)
                nc.vector.tensor_tensor(o, view[:, :, :, 0:HD],
                                        rc[:, :, :].rearrange("p t (j r) -> p t j r", r=1).broadcast_to([P, NT, 4, HD]),
                                        ALU.mult).then_inc(S["o_norm"], 1)

            def at(g, t):
                low(at_h[:, t, :, :], at_l[:, t, :, :], S["ath_ready"], S["atl_ready"], v_tile(g, t))

            def wo_out(g, t):
                dve.wait_ge(S["wo_done"], v_tile(g, t))
                dve.wait_ge(S["x2_in"], 16 * (g + 1))
                if g >= NB:
                    dve.wait_ge(S["x2_bias"], v_tile(g - NB, t))
                nc.vector.tensor_tensor(x2[:, t, :], mm_bank(("wo", g, t)), x2[:, t, :], ALU.add)\
                    .then_inc(S["wo_out"], 1)

            def ln2(g):
                for t in range(NT):
                    dve.wait_ge(S["wo_out"], v_tile(g, t))
                    norm_stats(x2[:, t, :], st2[:, t, :], mv2[:, t, :], ve2[:, t:t + 1], S["ln2_step"], NT * g + t)

            def x2t_norm(g, t):
                dve.wait_ge(S["ln2_rstd"], g + 1)
                dve.wait_ge(S["at_done"], v_tile(g, t))
                nc.vector.tensor_scalar(on[:, t, :], x2[:, t, :], mv2[:, t, 0:1], rs2[:, t:t + 1],
                                        ALU.subtract, ALU.mult).then_inc(S["ln2_norm"], 1)

            def x2t(g, t):
                low(at_h[:, t, :, :], at_l[:, t, :, :], S["x2h_ready"], S["x2l_ready"], v_tile(g, t))

            def h_step(g, t):
                dve.wait_ge(S["h_done"], v_tile(g, t))
                if g:
                    dve.wait_ge(S["hwt_done"], g)
                nc.vector.tensor_copy(hs[:, t, :], mm_bank(("h", g, t))[:, 0:E + E * R]).then_inc(S["h_out"], 1)

            def route(g):
                k = 8 * g
                st = S["rt_step"]

                def bc(ap):
                    return ap.rearrange("p (t r) -> p t r", r=1).broadcast_to([P, NT, E])

                dve.wait_ge(S["h_out"], NT * (g + 1))
                nc.vector.tensor_reduce(mxl[:, :], hs[:, :, 0:E], AX_X, ALU.max).then_inc(st, 1)
                dve.wait_ge(st, k + 1)
                nc.vector.tensor_tensor(zl[:, :, :], hs[:, :, 0:E], bc(mxl[:, :]), ALU.subtract).then_inc(st, 1)
                dve.wait_ge(S["rt_exp"], g + 1)
                nc.vector.tensor_reduce(esum[:, :], el[:, :, :], AX_X, ALU.add).then_inc(st, 1)
                dve.wait_ge(st, k + 3)
                nc.vector.reciprocal(erec[:, :], esum[:, :]).then_inc(st, 1)
                dve.wait_ge(st, k + 4)
                nc.vector.tensor_tensor(pr[:, :, :], el[:, :, :], bc(erec[:, :]), ALU.mult).then_inc(st, 1)
                dve.wait_ge(st, k + 5)
                for t in range(NT):
                    pj = pr[:, t, :].rearrange("p (i j) -> p i j", i=1).broadcast_to([P, E, E])
                    pi = pr[:, t, :].rearrange("p (i j) -> p i j", j=1).broadcast_to([P, E, E])
                    nc.vector.tensor_tensor(gt[:, t * E:(t + 1) * E, :], pj, pi, ALU.is_gt)
                    ins = nc.vector.tensor_tensor(ge[:, t * E:(t + 1) * E, :], pj, pi, ALU.is_ge)
                ins.then_inc(st, 1)
                dve.wait_ge(st, k + 6)
                tri2 = tri[:, :, :]
                for t in range(NT):
                    ins = nc.vector.tensor_tensor(ge[:, t * E:(t + 1) * E, :], ge[:, t * E:(t + 1) * E, :], tri2,
                                                  ALU.mult)
                ins.then_inc(st, 1)
                dve.wait_ge(st, k + 7)
                nc.vector.tensor_tensor(gt[:, :, :], gt[:, :, :], ge[:, :, :], ALU.max).then_inc(st, 1)
                dve.wait_ge(st, k + 8)
                r2 = S["rt2_step"]
                k2 = 5 * g
                nc.vector.tensor_reduce(rank[:, :, :].rearrange("p t i -> p (t i)"), gt[:, :, :], AX_X, ALU.add)\
                    .then_inc(r2, 1)
                dve.wait_ge(r2, k2 + 1)
                nc.vector.scalar_tensor_tensor(pr[:, :, :].rearrange("p t i -> p (t i)"),
                                               rank[:, :, :].rearrange("p t i -> p (t i)"), 1.5,
                                               pr[:, :, :].rearrange("p t i -> p (t i)"), ALU.is_lt, ALU.mult)\
                    .then_inc(r2, 1)
                dve.wait_ge(r2, k2 + 2)
                nc.vector.tensor_reduce(esum[:, :], pr[:, :, :], AX_X, ALU.add).then_inc(r2, 1)
                dve.wait_ge(r2, k2 + 3)
                nc.vector.reciprocal(erec[:, :], esum[:, :]).then_inc(r2, 1)
                dve.wait_ge(r2, k2 + 4)
                nc.vector.tensor_tensor(pr[:, :, :], pr[:, :, :], bc(erec[:, :]), ALU.mult).then_inc(r2, 1)
                dve.wait_ge(r2, k2 + 5)
                for t in range(NT):
                    o = hs[:, t, E:E + E * R].rearrange("p (e r) -> p e r", e=E)
                    w = pr[:, t, :].rearrange("p (e r) -> p e r", r=1).broadcast_to([P, E, R])
                    ins = nc.vector.tensor_tensor(o, o, w, ALU.mult)
                ins.then_inc(S["hw_ready"], 1)

            def hwt(g):
                dve.wait_ge(S["hwh_ready"], g + 1)
                nc.vector.tensor_tensor(hw_l[:, :, :], ps_tr[:, 0:NT * P].rearrange("p (t q) -> p t q", t=NT),
                                        hw_h[:, :, :], ALU.subtract).then_inc(S["hwl_ready"], 1)

            def ffn_out(g, t):
                dve.wait_ge(S["ffn_done"], v_tile(g, t))
                dve.wait_ge(S["x2_plus"], v_tile(g, t))
                nc.vector.tensor_tensor(x2[:, t, :], mm_bank(("ffn", g, t)), x2[:, t, :], ALU.add)\
                    .then_inc(S["y_ready"], 1)

            nc.vector.memset(ps_pv[:, :], 0.0).then_inc(S["pv_zeroed"], 1)
            nc.vector.memset(v[:, :, :, HD:HD + 1], 1.0).then_inc(S["ones_ready"], 1)
            nc.vector.memset(nms[:, :, :, :, :].bitcast(F32), 0.0).then_inc(S["nms_zeroed"], 1)
            dve.wait_ge(S["const_in"], 16 * 5)
            nc.vector.tensor_copy(ident_r[:, :], nmt_f[:, :]).then_inc(S["ident_ready"], 1)
            nc.vector.tensor_copy(cbf[:, :], qf[:, 0, 0:2 * P])
            nc.vector.tensor_copy(fence[:, :, :, :].rearrange("p c t r -> p (c t r)"), qf[:, 0, 2 * P:2 * P + 32])
            nc.vector.tensor_copy(tri[:, :, :].rearrange("p i j -> p (i j)"), qf[:, 0, 2 * P + 32:2 * P + 96])\
                .then_inc(S["small_ready"], 1)
            nc.vector.tensor_copy(ka[:, :, EXTRA:HROWS], x2[:, 0, :].rearrange("p (h r) -> p h r", h=H))\
                .then_inc(S["kaug_ready"], 1)
            nc.vector.tensor_copy(qa[:, :, EXTRA:HROWS], x2[:, 1, :].rearrange("p (h r) -> p h r", h=H))\
                .then_inc(S["kaug_ready"], 1)
            does = {"ln1": ln1, "xt": xt, "qkv_out": qkv_out, "t": t_step, "s": s_step, "m": m_step, "o": o_step,
                    "at": at, "wo_out": wo_out, "ln2": ln2, "x2t": x2t, "h": h_step, "route": route, "hwt": hwt,
                    "ffn_out": ffn_out}
            for step in plan:
                if step[0] == "x2t":
                    x2t_norm(*step[1:])
                if step[0] in does:
                    does[step[0]](*step[1:])


def constants():
    import numpy as np

    def high(a):
        m, e = np.frexp(a.astype(np.float64))
        return np.ldexp(np.rint(m * 4096) / 4096, e).astype(np.float32)

    ident = np.eye(P, dtype=np.float32)
    q, k = np.arange(P)[:, None], np.arange(P)[None, :]
    mask = np.where(k > q, -(2.0 ** 100), 0.0).astype(np.float32)
    m = np.arange(1, H + 1, dtype=np.float32) * np.float32(8.0 / H)
    slope = (1.0 / np.power(np.float32(2.0), m)).astype(np.float32)
    root = np.float32(HD ** 0.5)
    kaug = np.zeros((P, H, HD), np.float32)
    qaug = np.zeros((P, H, HD), np.float32)
    pos = np.arange(P, dtype=np.float32)[:, None]
    kaug[:, :, 0:2] = 1.0
    a = (slope[None, :] * pos).astype(np.float32) * root
    kaug[:, :, 2] = high(a)
    kaug[:, :, 3] = a - high(a)
    qaug[:, :, 2:4] = 1.0
    s4 = slope * root
    kaug[:, :, 4] = -high(s4)
    kaug[:, :, 5] = -(s4 - high(s4))
    qaug[:, :, 4:6] = pos[:, :, None]
    kblock = np.zeros((P, H, 2), np.float32)
    kblock[:, :, 0] = -high(s4) * P
    kblock[:, :, 1] = -(s4 - high(s4)) * P
    blk = (np.arange(NT)[None, :] * P + np.arange(P)[:, None]) // 32
    n8 = np.arange(8)
    fence = np.zeros((P, 2, NT, 8), np.float32)
    fence[:, 0] = blk[:, :, None] < n8
    fence[:, 1] = np.where(blk[:, :, None] == n8, -(2.0 ** 100), 0.0)
    tri = np.broadcast_to(np.tril(np.ones((E, E), np.float32), -1)[None], (P, E, E))
    small = np.concatenate([ident, mask, fence.reshape(P, -1), tri.reshape(P, -1)], 1)
    return [ident, small, kaug.reshape(P, H * HD), qaug.reshape(P, H * HD), kblock]


def kernel(**inputs):
    import numpy as np
    import concourse.bacc as bacc
    from concourse.bass_utils import run_bass_kernel_spmd as run

    nc = bacc.Bacc("TRN2", target_bir_lowering=False, num_devices=1)
    i = {k: np.asarray(a) for k, a in inputs.items()}
    arrays = {}

    def given(name, a):
        a = np.ascontiguousarray(a)
        arrays[name] = a
        return nc.dram_tensor(name, a.shape, mybir.dt.from_np(a.dtype), kind="ExternalInput").ap()

    def turned(w):
        return w.T.reshape(KC, P, -1)

    x = given("x", i["L0_attn_a_hidden_states"].reshape(NB * SEQ, D))
    consts = [given(f"const{n}", a) for n, a in enumerate(constants())]
    a3 = i["L0_attn_a_Wqkv"].reshape(3, D, D)
    b3 = np.stack([i["L0_attn_b_Wq"], i["L0_attn_b_Wk"], i["L0_attn_b_Wv"]])
    wqkv = given("wqkv", np.stack([np.stack([turned(w) for w in ws]) for ws in (a3, b3)]))
    wout = given("wout", np.stack([turned(i["L0_attn_a_Wout"]), turned(i["L0_attn_b_Wo"])]))
    wbase = given("wbase", turned(i["L0_ffn_W_base"]))
    wgate = given("wgate", turned(np.concatenate([i["L0_ffn_W_gate"], i["L0_ffn_A"].reshape(E * R, D)])))
    wlow = given("wlow", i["L0_ffn_B"].transpose(0, 2, 1).reshape(E * R, D))
    rows = given("rows", np.stack([i["L0_attn_a_q_ln_w"], i["L0_attn_a_q_ln_b"], i["L0_attn_a_k_ln_w"],
                                   i["L0_attn_a_k_ln_b"], i["L0_attn_b_bq"], i["L0_attn_b_bk"],
                                   i["L0_attn_b_bv"], i["L0_attn_b_bo"], i["L0_ffn_b_base"]]))
    mid = nc.dram_tensor("mid", (NB * SEQ, D), F32, kind="Internal").ap()
    out = nc.dram_tensor("out", (NB * SEQ, D), F32, kind="ExternalOutput").ap()
    build(nc, x, consts, wqkv, wout, wbase, wgate, wlow, rows, mid, out)
    r = run(nc, [arrays], core_ids=[0])
    return r.results[0]["out"].reshape(NB, SEQ, D)
```

```python
from contextlib import ExitStack

import concourse.bass as bass
from concourse import mybir

F32 = mybir.dt.float32
F32R = mybir.dt.float32r
BF16 = mybir.dt.bfloat16
ALU = mybir.AluOpType
ACT = mybir.ActivationFunctionType
AX_X = mybir.AxisListType.X

P = 128
D = 512
KC = D // P
H = 32
HD = D // H
SEQ = 256
NT = SEQ // P
NB = 4
NP = H // 2
NG = NP // 4
E = 8
R = 16
STAGES = 2 * NB
HROWS = 64
EXTRA = 3 * HD
PT_RING = 4
LN_EPS = 1e-5
CLIP = 8.0


URGENCY = dict(x_load=2.6, ln1_stats=8.5, ln1_norm=7.7, xt=5, xt_high=8.4, xt_low=3.4, qkv=8, qkv_out=3.0,
               qk_power=6.6, qk_norm=4, qk_affine=5.5, expand_high=3.2, expand_low=1.3, expand_extra=5.7,
               head_turn=1, turn_dve=4.1, turn_act=2.1, at=5.1, at_high=4.0, at_low=1.0, wo=7.1, wo_out=3,
               ln2_stats=4, ln2_norm=2.1, x2t=4.7, x2t_high=3.2, x2t_low=4.7, x2_plus=0.5, h=7.0, h_out=6.1,
               ffn=4.7, ffn_out=6.6, ln1_power=4.0, ln2_power=0.6, x2_load=1.2, y_store=6.7, v_copy=6.1,
               route_max=3.1, route_exp=1.3, route_rank=7.1, route_weight=5, hwt=2.0, hwt_high=2.2,
               hwt_low=6.9, s=2, s_max=0, st=0, exp=2.6, mask=5.6, m_split=3.5, m_turn=0, m_copy=8.9,
               m_rows=3.4, pv=7.6, o_copy=3.8, o_turn=1, o_norm=5.4, w_high=7.2, w_low=5, w_load=3.6,
               small_constants=0.2, b_rows=8.5, x2_bias=4.0, piece_in=2.4)


def work():
    steps = {}

    def add(kind, at, engine, length, after, take=None, give=None):
        steps[(kind, *at)] = (engine, length, after, take, give)

    N_A, N_OUT, N_BASE, N_GATE, N_LOW = (KC * 3, KC * 4, KC * 5, KC * 6, KC * 6 + 1)
    N_B = N_LOW + 3 * KC
    for n in range(3 * KC):
        add("piece_in", (n,), "queue", 6.0 if n == 0 else 0.9 if n != KC else 3.0,
            [("piece_in", n - 1)] if n else [])
    for m in range(8):
        after = [("qkv_out", 0, 0, 2)] if m < 4 else [("qkv", NB - 1, 1, m - 4, KC - 1)] if m < 7 else \
            [("wo", NB - 1, 1, KC - 1)]
        add("w_load", (m,), "SP", 4.0, after + ([("w_load", m - 1)] if m else []))
    for n in range(N_B + KC):
        m = 0 if n < N_OUT else 1 if n < N_BASE else 2 if n < N_GATE else 3 if n < N_LOW else 4 + (n - N_LOW) // KC
        add("w_high", (n,), "ACT", 0.45, [("piece_in", n) if n < N_A else ("w_load", m)])
        add("w_low", (n,), "DVE", 0.46, [("w_high", n)])
    add("small_constants", (0,), "DVE", 3.0, [("piece_in", KC)])
    add("b_rows", (0,), "SP", 2.0, [("qk_affine", NB - 1, 1, 1)])

    for g in range(STAGES):
        a = g < NB
        b = g - 1
        add("x_load", (g,), "SP", 2.6, [("xt", b, 1), ("y_store", g - NB)])
        add("ln1_power", (g,), "POOL", 0.6, [("ln1_stats", g, 0), ("ln1_stats", g, 1)])
        for t in range(NT):
            add("ln1_stats", (g, t), "DVE", 0.9, [("x_load", g)])
            add("ln1_norm", (g, t), "DVE", 0.45, [("ln1_power", g)])
            add("xt", (g, t), "PE", 0.43, [("ln1_norm", g, t), ("qkv", b, t, 2, KC - 1)], take="turns")
            add("xt_high", (g, t), "ACT", 0.5, [("xt", g, t)])
            add("xt_low", (g, t), "DVE", 0.62, [("xt_high", g, t)], give="turns")
            for n in range(3):
                last = (g, 0) if t else (b, 1)
                first = [("xt_low", g, t), ("v_copy", b) if n == 2 else ("expand_low", *last, n)]
                if t == 0 and g % NB == 0:
                    first.append(("w_low", KC * (n + 1) - 1 + (0 if a else N_LOW)))
                if g == NB:
                    first.append(("b_rows", 0))
                for c in range(KC):
                    add("qkv", (g, t, n, c), "PE", 0.66, first if c == 0 else [("qkv", g, t, n, c - 1)],
                        take="products" if c == 0 else None)
                add("qkv_out", (g, t, n), "DVE", 1.6 if n < 2 and a else 0.62, [("qkv", g, t, n, KC - 1)],
                    give="products")
                if n < 2 and a:
                    add("qk_power", (g, t, n), "POOL", 0.5, [("qkv_out", g, t, n)])
                    add("qk_norm", (g, t, n), "DVE", 0.46, [("qk_power", g, t, n)])
                    add("qk_affine", (g, t, n), "POOL", 2.55, [("qk_norm", g, t, n)])
            for u in range(2):
                last = ("head_turn", g, 0, u, 1) if t else ("head_turn", b, 1, u, 1)
                add("expand_high", (g, t, u), "ACT", 0.95,
                    [("qk_affine" if a else "qkv_out", g, t, u), last, ("small_constants", 0)])
                add("expand_low", (g, t, u), "POOL", 1.23, [("expand_high", g, t, u)])
                add("expand_extra", (g, t, u), "POOL", 1.1 if a else 0.6, [last, ("small_constants", 0)])
                for half in range(2):
                    out = ("turn_dve", "turn_act")[half]
                    if u:
                        free = (out, g, t, 0)
                    elif t:
                        free = (out, g, 0, 1)
                    else:
                        free = (("s_max", "exp")[half], b, NP - 1)
                    add("head_turn", (g, t, u, half), "PE", 0.46,
                        [("expand_low", g, t, u), ("expand_extra", g, t, u), free, ("st", b, NP - 1)])
                add("turn_dve", (g, t, u), "DVE", 1.13, [("head_turn", g, t, u, 0)])
                add("turn_act", (g, t, u), "ACT", 0.9, [("head_turn", g, t, u, 1)])
        add("v_copy", (g,), "ACT", 0.95, [("qkv_out", g, 0, 2), ("qkv_out", g, 1, 2), ("pv", b, NP // 2 - 1)])
        for p in range(NP):
            add("s", (g, p), "PE", 0.56, [("s_max", g, p - 1)] if p else [("turn_dve", g, 1, 1), ("turn_act", g, 1, 1)])
            add("s_max", (g, p), "DVE", 0.87, [("s", g, p)])
            add("st", (g, p), "PE", 0.33, [("m_rows", g, p // 4), ("exp", g, p - 1)])
            add("exp", (g, p), "ACT", 0.69,
                [("st", g, p), ("pv", g, (p - PT_RING) // 2) if p >= PT_RING else ("pv", b, NP // 2 - 1)])
            add("mask", (g, p), "POOL", 0.6, [("exp", g, p)])
        for n in range(NG):
            add("m_split", (g, n), "DVE", 0.75, [("s_max", g, 4 * n + 3), ("m_turn", g, n - 1)])
            add("m_turn", (g, n), "PE", 0.06, [("m_split", g, n)], take="turns")
            add("m_copy", (g, n), "ACT", 0.16, [("m_turn", g, n)], give="turns")
            add("m_rows", (g, n), "SP", 2.6, [("m_copy", g, n)])
        for n in range(NP // 2):
            add("pv", (g, n), "PE", 0.8, [("mask", g, 2 * n + 1), ("v_copy", g),
                                          ("o_copy", g, n - 1) if n else ("o_copy", b, NP // 2 - 1)])
            add("o_copy", (g, n), "ACT", 0.26, [("pv", g, n), ("o_turn", g, n - 1) if n else ("o_turn", b, NP // 2 - 1)])
            add("o_turn", (g, n), "PE", 0.22, [("o_copy", g, n)] + ([] if n else [("x2t", b, 1)]), take="turns")
            add("o_norm", (g, n), "DVE", 0.4, [("o_turn", g, n)], give="turns")
        add("x2_load", (g,), "SP", 2.6, [("y_store", b)] if g else [("small_constants", 0)])
        add("ln2_power", (g,), "POOL", 0.6, [("ln2_stats", g, 0), ("ln2_stats", g, 1)])
        for t in range(NT):
            add("at", (g, t), "PE", 0.43, [("o_norm", g, NP // 2 - 1), ("ffn", b, t, KC)], take="turns")
            add("at_high", (g, t), "ACT", 0.5, [("at", g, t)])
            add("at_low", (g, t), "DVE", 0.62, [("at_high", g, t)], give="turns")
            first = [("at_low", g, t), ("x2_load", g)]
            if g % NB == 0:
                first.append(("w_low", (N_OUT if a else N_B + KC) - 1))
            if not a:
                add("x2_bias", (g, t), "POOL", 1.23, [("x2_load", g)])
                first.append(("x2_bias", g, t))
            for c in range(KC):
                add("wo", (g, t, c), "PE", 0.66, first if c == 0 else [("wo", g, t, c - 1)],
                    take="products" if c == 0 else None)
            add("wo_out", (g, t), "DVE", 0.62, [("wo", g, t, KC - 1)], give="products")
            add("ln2_stats", (g, t), "DVE", 0.9, [("wo_out", g, t)])
            add("ln2_norm", (g, t), "DVE", 0.46, [("ln2_power", g)])
            add("x2_plus", (g, t), "POOL", 1.23, [("ln2_norm", g, t)])
            add("x2t", (g, t), "PE", 0.43, [("ln2_norm", g, t), ("wo", g, t, KC - 1)], take="turns")
            add("x2t_high", (g, t), "ACT", 0.5, [("x2t", g, t)])
            add("x2t_low", (g, t), "DVE", 0.62, [("x2t_high", g, t)], give="turns")
            add("h", (g, t), "PE", 0.72, [("x2t_low", g, t), ("hwt", b), ("w_low", N_GATE - 1)], take="products")
            add("h_out", (g, t), "DVE", 0.25, [("h", g, t)], give="products")
            for c in range(KC + 1):
                first = [("x2t_low", g, t), ("x2_plus", g, t), ("w_low", N_LOW - 1), ("route_exp", g)]
                add("ffn", (g, t, c), "PE", 0.66, (first if c == 0 else [("ffn", g, t, c - 1)]) +
                    ([("hwt_low", g)] if c == KC else []), take="products" if c == 0 else None)
            add("ffn_out", (g, t), "DVE", 0.62, [("ffn", g, t, KC)], give="products")
        add("route_max", (g,), "DVE", 0.32, [("h_out", g, 0), ("h_out", g, 1)])
        add("route_exp", (g,), "ACT", 0.22, [("route_max", g)])
        add("route_rank", (g,), "DVE", 1.7, [("route_exp", g)])
        add("route_weight", (g,), "DVE", 1.6, [("route_rank", g)])
        add("hwt", (g,), "PE", 0.22, [("route_weight", g), ("ffn", b, 1, KC)], take="turns")
        add("hwt_high", (g,), "ACT", 0.26, [("hwt", g)])
        add("hwt_low", (g,), "DVE", 0.33, [("hwt_high", g)], give="turns")
        add("y_store", (g,), "SP", 2.6, [("ffn_out", g, 0), ("ffn_out", g, 1)])
    return steps


def order_of_work(urgency=URGENCY):
    steps = work()
    hop = 0.12
    taken_by = {"wo_out": "wo", "ffn_out": "ffn", "h_out": "h", "qkv_out": "qkv"}
    needs, users = {}, {k: [] for k in steps}
    for k, (_, _, after, _, _) in steps.items():
        known = [d for d in after if d in steps]
        needs[k] = len(known)
        for d in known:
            users[d].append(k)
    queue = {}
    for k in sorted(steps):
        queue.setdefault(k[0], []).append(k)
    kinds = {}
    for kind, ks in queue.items():
        kinds.setdefault(steps[ks[0]][0], []).append(kind)
    head = {kind: 0 for kind in queue}
    free = {e: 0.0 for e in kinds}
    banks, turns_free, units, given = 2, True, {}, set()
    order, events, now = [], [], 0.0
    while len(order) < len(steps):
        moved = True
        while moved:
            moved = False
            for engine in kinds:
                if free[engine] > now + 1e-9:
                    continue
                best = None
                for kind in kinds[engine]:
                    if head[kind] == len(queue[kind]):
                        continue
                    k = queue[kind][head[kind]]
                    take = steps[k][3]
                    if needs[k] or (take == "turns" and not turns_free):
                        continue
                    if take == "products" and len(units) >= banks and len(units) - banks not in given:
                        continue
                    rank = (urgency.get(kind, 5.0), k[1:])
                    if best is None or rank < best[0]:
                        best = (rank, k)
                if best:
                    k = best[1]
                    length, take = steps[k][1], steps[k][3]
                    head[k[0]] += 1
                    order.append(k)
                    if take == "turns":
                        turns_free = False
                    if take == "products":
                        units[k[:-1] if k[0] != "h" else k] = len(units)
                    free[engine] = now + (0.5 if engine == "SP" else length)
                    events += [(now + length + hop, k), (free[engine], None)]
                    moved = True
        if not events:
            raise RuntimeError("the order of work is stuck")
        now = min(events, key=lambda e: e[0])[0]
        for _, k in [e for e in events if e[0] <= now + 1e-9]:
            if k:
                if steps[k][4] == "turns":
                    turns_free = True
                if steps[k][4] == "products":
                    given.add(units[(taken_by[k[0]], *k[1:])])
                for u in users[k]:
                    needs[u] -= 1
        events = [e for e in events if e[0] > now + 1e-9]
    return order, now


def build(nc, x_in, consts, wqkv, wout, wbase, wgate, wlow, rows, mid, scratch, out):
    c_ident, c_small, c_kaug, c_qaug, c_kblock = consts
    plan, _ = order_of_work()

    mm_units = [s[:4] if s[0] == "qkv" else s[:3] for s in plan if s[0] in ("wo", "h", "ffn", "qkv")]
    mm_units = list(dict.fromkeys(mm_units))
    tr_units = [s for s in plan if s[0] in ("xt", "at", "x2t", "hwt", "m_turn", "o_turn")]
    mm_no = {s: n for n, s in enumerate(mm_units)}
    tr_no = {s: n for n, s in enumerate(tr_units)}

    with ExitStack() as ctx:
        def sb(name, shape, dt=F32):
            return ctx.enter_context(nc.sbuf_tensor(name, shape, dt))

        def sem(name):
            return ctx.enter_context(nc.semaphore(name))

        wq_h = sb("wq_h", [P, 3, KC, D], F32R)
        wq_l = sb("wq_l", [P, 3, KC, D], F32R)
        wo_h = sb("wo_h", [P, KC, D], F32R)
        wo_l = sb("wo_l", [P, KC, D], F32R)
        wb_h = sb("wb_h", [P, KC, D], F32R)
        wb_l = sb("wb_l", [P, KC, D], F32R)
        wg_h = sb("wg_h", [P, KC, E + E * R], F32R)
        wg_l = sb("wg_l", [P, KC, E + E * R], F32R)
        wl_h = sb("wl_h", [P, 1, D], F32R)
        wl_l = sb("wl_l", [P, 1, D], F32R)
        row = sb("row", [P, 5, D])
        qt = sb("qt", [P, NP, SEQ], F32R)
        kt = sb("kt", [P, NP, SEQ], F32R)
        qa = sb("qa", [P, H, HROWS], F32R)
        ka = sb("ka", [P, H, HROWS], F32R)
        qf = sb("qf", [P, 2, D])
        vn = sb("vn", [P, NT, D])
        v = sb("v", [P, NT, H, HD + 1])
        pt = sb("pt", [P, PT_RING, 2, SEQ + P])
        xa = sb("xa", [P, NT, D])
        x2 = sb("x2", [P, NT, D])
        xt_h = sb("xt_h", [P, NT, KC, P], F32R)
        xt_l = sb("xt_l", [P, NT, KC, P], F32R)
        at_h = sb("at_h", [P, NT, KC, P], F32R)
        at_l = sb("at_l", [P, NT, KC, P], F32R)
        on = sb("on", [P, NT, D])
        ot = sb("ot", [P, SEQ])
        hs = sb("hs", [P, NT, E + E * R])
        hw_h = sb("hw_h", [P, NT, P], F32R)
        hw_l = sb("hw_l", [P, NT, P], F32R)
        ident_r = sb("ident_r", [P, P], F32R)
        ident = ident_r[:, :].bitcast(F32)
        cbf = sb("cbf", [P, 2 * P], BF16)
        nmt_f = hs[:, 0, 0:P]
        kblock = sb("kblock", [P, H, 2])
        fence = sb("fence", [P, 2, NT, 8], BF16)
        tri = sb("tri", [P, E, E], BF16)
        neg_half = sb("neg_half", [P, 2])
        st1 = sb("st1", [P, NT, 6])
        mv1 = sb("mv1", [P, NT, 2])
        ve1 = sb("ve1", [P, NT])
        rs1 = sb("rs1", [P, NT])
        st2 = sb("st2", [P, NT, 6])
        mv2 = sb("mv2", [P, NT, 2])
        ve2 = sb("ve2", [P, NT])
        rs2 = sb("rs2", [P, NT])
        stq = sb("stq", [P, 2, 6])
        mvq = sb("mvq", [P, 2, 2])
        veq = sb("veq", [P, 2])
        rsq = sb("rsq", [P, 2])
        pm = sb("pm", [P, NP, 2, 3])
        nm = sb("nm", [P, 2, 4, NT])
        nms = sb("nms", [P, NG, 2, 2, 4 * NT], F32R)
        nmt = sb("nmt", [P, P], F32R)
        rc = sb("rc", [P, NT, 4])
        mxl = sb("mxl", [P, NT])
        zl = sb("zl", [P, NT, E])
        el = sb("el", [P, NT, E])
        esum = sb("esum", [P, NT])
        erec = sb("erec", [P, NT])
        pr = sb("pr", [P, NT, E])
        gt = sb("gt", [P, NT * E, E], BF16)
        ge = sb("ge", [P, NT * E, E], BF16)
        rank = sb("rank", [P, NT, E])

        ps_s = ctx.enter_context(nc.psum_tensor("ps_s", [P, 1024], F32))
        ps_st = ctx.enter_context(nc.psum_tensor("ps_st", [P, 1024], F32))
        ps_mm = ctx.enter_context(nc.psum_tensor("ps_mm", [P, 2, D], F32))
        ps_tr = ctx.enter_context(nc.psum_tensor("ps_tr", [P, D], F32))
        ps_pv = ctx.enter_context(nc.psum_tensor("ps_pv", [P, D], F32))

        names = """ident_in const_in small_ready ident_ready kaug_ready rt2_step half_ready ones_ready nms_zeroed pv_zeroed
            wsplit_h wsplit_l row_in
            xa_in x2_in x2_bias ln1_step ln1_rstd ln1_norm xt_done xth_ready xtl_ready
            qkv_done qkv_out lnq_step lnq_rstd lnq_norm q_scaled q_ready exp_hi exp_lo aug_set
            t_done t_dve t_act v_copied s_done s_max nm_step mt_done nmt_copied mrow_in
            st_done st_exp p_masked pv_done o_copied ot_done o_rec o_norm at_done ath_ready atl_ready
            wo_done wo_out ln2_step ln2_rstd ln2_norm x2t_done x2h_ready x2l_ready x2_plus
            h_done h_out rt_step rt_exp hw_ready hwt_done hwh_ready hwl_ready ffn_done y_ready y_stored""".split()
        S = {n: sem(n) for n in names}

        def v_tile(g, t):
            return NT * g + t + 1

        reads_done = {
            "xt": lambda g, t: (S["xtl_ready"], v_tile(g, t)),
            "at": lambda g, t: (S["atl_ready"], v_tile(g, t)),
            "x2t": lambda g, t: (S["x2l_ready"], v_tile(g, t)),
            "hwt": lambda g: (S["hwl_ready"], g + 1),
            "m_turn": lambda g, n: (S["nmt_copied"], NG * g + n + 1),
            "o_turn": lambda g, n: (S["o_norm"], NP // 2 * g + n + 1),
            "wo": lambda g, t: (S["wo_out"], v_tile(g, t)),
            "h": lambda g, t: (S["h_out"], v_tile(g, t)),
            "ffn": lambda g, t: (S["y_ready"], v_tile(g, t)),
            "qkv": lambda g, t, n: (S["qkv_out"], 3 * NT * g + 3 * t + n + 1),
        }

        def wait_tr_free(eng, step):
            if tr_no[step] >= 1:
                prev = tr_units[tr_no[step] - 1]
                eng.wait_ge(*reads_done[prev[0]](*prev[1:]))

        def wait_mm_free(eng, step):
            if mm_no[step] >= 2:
                prev = mm_units[mm_no[step] - 2]
                eng.wait_ge(*reads_done[prev[0]](*prev[1:]))

        def mm_bank(step):
            return ps_mm[:, mm_no[step] % 2, :]

        pt_flat = pt[:, :, :, :].rearrange("p i e q -> p (i e q)")
        spare = [pt_flat[:, i * D:(i + 1) * D] for i in range(6)] + [vn[:, 0, :], vn[:, 1, :], on[:, 0, :], on[:, 1, :]]
        pieces = []
        for n in range(3):
            for c in range(KC):
                pieces.append((spare[len(pieces) % len(spare)], wq_h[:, n, c, :], wq_l[:, n, c, :]))
        N_QKV_A = len(pieces)
        matrices = []

        def bounced(src, n, high, low, n_chunks):
            matrices.append((src, scratch[n], low.bitcast(F32)))
            for c in range(n_chunks):
                pieces.append((low[:, c].bitcast(F32), high[:, c], low[:, c]))

        bounced(wout[0], 0, wo_h[:, :, :], wo_l[:, :, :], KC)
        N_OUT_A = len(pieces)
        bounced(wbase, 1, wb_h[:, :, :], wb_l[:, :, :], KC)
        N_BASE = len(pieces)
        bounced(wgate, 2, wg_h[:, :, :], wg_l[:, :, :], KC)
        N_GATE = len(pieces)
        bounced(wlow, 3, wl_h[:, :, :], wl_l[:, :, :], 1)
        N_LOW = len(pieces)
        for n in range(3):
            bounced(wqkv[1, n], 4 + n, wq_h[:, n, :, :], wq_l[:, n, :, :], KC)
        N_QKV_B = len(pieces)
        bounced(wout[1], 7, wo_h[:, :, :], wo_l[:, :, :], KC)
        N_OUT_B = len(pieces)
        piece_in = [sem(f"piece_in{n}") for n in range(N_QKV_A)]
        bounce_done = [sem(f"bounce_done{m}") for m in range(len(matrices))]
        matrix_in = [sem(f"matrix_in{m}") for m in range(len(matrices))]
        matrix_of = [0] * KC + [1] * KC + [2] * KC + [3] + [4 + n // KC for n in range(4 * KC)]

        block = ctx.enter_context(nc.Block())

        @block.sync
        def _(sp):
            def source(g):
                src = x_in if g < NB else mid
                b = g % NB
                return src[b * SEQ:(b + 1) * SEQ, :].rearrange("(t p) d -> p t d", p=P)

            def load_piece(n):
                if n >= len(spare):
                    sp.wait_ge(S["wsplit_l"], n - len(spare) + 1)
                sp.dma_start(pieces[n][0], wqkv[0, n // KC, :, n % KC, :]).then_inc(piece_in[n], 16)

            def load_rows(n, first):
                sp.dma_start(row[:, n, :], rows[first:first + 1, :].partition_broadcast(P)).then_inc(S["row_in"], 16)

            def x_load(g):
                sp.wait_ge(S["xt_done"], v_tile(g - 1, 1))
                if g >= NB:
                    sp.wait_ge(S["y_stored"], 16 * (g - NB + 1))
                sp.dma_start(xa[:, :, :], source(g)).then_inc(S["xa_in"], 16)

            def x2_load(g):
                if g:
                    sp.wait_ge(S["y_stored"], 16 * g)
                else:
                    sp.wait_ge(S["kaug_ready"], 2)
                sp.dma_start(x2[:, :, :], source(g)).then_inc(S["x2_in"], 16)

            def y_store(g):
                sp.wait_ge(S["y_ready"], v_tile(g, 1))
                dst = mid if g < NB else out
                b = g % NB
                sp.dma_start(dst[b * SEQ:(b + 1) * SEQ, :].rearrange("(t p) d -> p t d", p=P),
                             x2[:, :, :]).then_inc(S["y_stored"], 16)

            def m_rows(g, n):
                sp.wait_ge(S["nmt_copied"], NG * g + n + 1)
                for e in range(2):
                    r0 = 32 * n + 16 * e
                    sp.dma_start(qt[HROWS * e + EXTRA:HROWS * e + EXTRA + 2, 4 * n:4 * n + 4, :].bitcast(F32),
                                 nmt[r0:r0 + 16, :].bitcast(F32)).then_inc(S["mrow_in"], 16)

            def w_load(m):
                sp.wait_ge(bounce_done[m], 16)
                if 4 <= m < 7:
                    sp.wait_ge(S["qkv_done"], 3 * NT * (NB - 1) + 3 + m - 4 + 1)
                if m == 7:
                    sp.wait_ge(S["wo_done"], NT * NB)
                sp.dma_start(matrices[m][2], matrices[m][1].bitcast(F32)).then_inc(matrix_in[m], 16)

            def b_rows(_):
                sp.wait_ge(S["q_ready"], 2 * NT * NB)
                for n in range(4):
                    load_rows(n, 4 + n)

            sp.dma_start(xa[:, :, :], source(0)).then_inc(S["xa_in"], 16)
            sp.dma_start(nmt_f[:, :], c_ident).then_inc(S["ident_in"], 16)
            for n in range(KC):
                load_piece(n)
            sp.dma_start(qf[:, 0, 0:c_small.shape[-1]], c_small).then_inc(S["const_in"], 16)
            sp.dma_start(kblock[:, :, :], c_kblock).then_inc(S["const_in"], 16)
            sp.dma_start(x2[:, 0, :], c_kaug).then_inc(S["const_in"], 16)
            sp.dma_start(x2[:, 1, :], c_qaug).then_inc(S["const_in"], 16)
            for n in range(KC, 2 * KC):
                load_piece(n)
            for n in range(4):
                load_rows(n, n)
            load_rows(4, 8)
            for n in range(2 * KC, N_QKV_A):
                load_piece(n)
            for m, (src, via, _) in enumerate(matrices):
                sp.dma_start(via, src).then_inc(bounce_done[m], 16)
            does = {"x_load": x_load, "x2_load": x2_load, "y_store": y_store, "m_rows": m_rows, "w_load": w_load,
                    "b_rows": b_rows}
            for step in plan:
                if step[0] in does and step != ("x_load", 0):
                    does[step[0]](*step[1:])
            sp.wait_ge(S["y_stored"], 16 * STAGES)

        @block.tensor
        def _(pe):
            def passes(dst, a_h, a_l, b_h, b_l, c, start, stop):
                pe.matmul(dst, a_h(c), b_h(c), start=start, stop=False)
                pe.matmul(dst, a_h(c), b_l(c), start=False, stop=False)
                return pe.matmul(dst, a_l(c), b_h(c), start=False, stop=stop)

            def turn(src, parts, done):
                for c in range(parts):
                    ins = pe.transpose(ps_tr[:, c * P:(c + 1) * P], src(c), ident)
                ins.then_inc(done, 1)

            def xt(g, t):
                pe.wait_ge(S["ln1_norm"], v_tile(g, t))
                wait_tr_free(pe, ("xt", g, t))
                turn(lambda c: xa[:, t, c * P:(c + 1) * P], KC, S["xt_done"])

            def qkv(g, t, n, c):
                if c == 0:
                    pe.wait_ge(S["xtl_ready"], v_tile(g, t))
                    wait_mm_free(pe, ("qkv", g, t, n))
                if g == 0 and t == 0:
                    pe.wait_ge(S["wsplit_l"], KC * n + c + 1)
                elif g == NB and t == 0 and c == 0:
                    pe.wait_ge(S["wsplit_l"], N_LOW + KC * (n + 1))
                ins = passes(mm_bank(("qkv", g, t, n)), lambda c: xt_h[:, t, c, :], lambda c: xt_l[:, t, c, :],
                             lambda c: wq_h[:, n, c, :], lambda c: wq_l[:, n, c, :], c, c == 0, c == KC - 1)
                if c == KC - 1:
                    ins.then_inc(S["qkv_done"], 1)

            def head_turn(g, t, u, half):
                pe.wait_ge(S["exp_lo"], 2 * NT * g + 2 * t + u + 1)
                pe.wait_ge(S["aug_set"], 2 * NT * g + 2 * t + u + 1)
                src, dst = (qa, ka)[u], (ps_s, ps_st)[half]
                if t == 0 and u == 0:
                    if g:
                        pe.wait_ge((S["s_max"], S["st_exp"])[half], NP * g)
                else:
                    pe.wait_ge((S["t_dve"], S["t_act"])[half], 4 * g + 2 * t + u)
                for i in range(8):
                    p = 8 * half + i
                    ins = pe.matmul(dst[:, i * P:(i + 1) * P], src[:, 2 * p:2 * p + 2, :], ident_r[:, :],
                                    start=True, stop=True)
                ins.then_inc(S["t_done"], 1)

            def s_step(g, p):
                if p == 0:
                    pe.wait_ge(S["t_dve"], 4 * g + 4)
                    pe.wait_ge(S["t_act"], 4 * g + 4)
                else:
                    pe.wait_ge(S["s_max"], NP * g + p)
                for e in range(2):
                    bank = ps_s[:, e * D:(e + 1) * D]
                    pe.matmul(bank[:, 0:2 * P], cbf[:, 0:P],
                              cbf[:, P:2 * P].rearrange("p (r k) -> p r k", r=1).broadcast_to([P, 2, P]),
                              start=True, stop=False, skip_group_check=True)
                for e in range(2):
                    r = slice(HROWS * e, HROWS * (e + 1))
                    bank = ps_s[:, e * D:(e + 1) * D]
                    pe.matmul(bank[:, 0:P], qt[r, p, 0:P], kt[r, p, 0:P], start=False, stop=False,
                              skip_group_check=True)
                    pe.matmul(bank[:, P:2 * P], qt[r, p, P:2 * P], kt[r, p, P:2 * P], start=False, stop=False,
                              skip_group_check=True)
                    ins = pe.matmul(bank[:, 2 * P:3 * P], qt[r, p, P:2 * P], kt[r, p, 0:P], start=False,
                                    stop=True, skip_group_check=True)
                ins.then_inc(S["s_done"], 1)

            def m_turn(g, n):
                pe.wait_ge(S["nm_step"], 4 * (NG * g + n + 1))
                wait_tr_free(pe, ("m_turn", g, n))
                pe.matmul(ps_tr[:, 0:P], nms[:, :, :, :, :], ident_r[:, :], start=True, stop=True)\
                  .then_inc(S["mt_done"], 1)

            def st_step(g, p):
                if p:
                    pe.wait_ge(S["st_exp"], NP * g + p)
                if p % 4 == 0:
                    pe.wait_ge(S["mrow_in"], 32 * (NG * g + p // 4 + 1))
                for e in range(2):
                    r = slice(HROWS * e, HROWS * (e + 1))
                    bank = ps_st[:, e * D:(e + 1) * D]
                    pe.matmul(bank[:, 0:3 * P].rearrange("p (b q) -> p b q", b=3)[:, 0:3:2, :], kt[r, p, 0:P],
                              qt[r, p, :].rearrange("p (b q) -> p b q", b=2), start=True, stop=True)
                    ins = pe.matmul(bank[:, P:2 * P], kt[r, p, P:2 * P], qt[r, p, P:2 * P], start=True,
                                    stop=True)
                ins.then_inc(S["st_done"], 1)

            def pv_step(g, n):
                k = NP // 2 * g + n
                pe.wait_ge(S["p_masked"], NP * g + 2 * n + 2)
                if n == 0:
                    pe.wait_ge(S["v_copied"], g + 1)
                if k:
                    pe.wait_ge(S["o_copied"], k)
                else:
                    pe.wait_ge(S["pv_zeroed"], 1)
                for part in range(NT):
                    for j in range(4):
                        h, e = 4 * n + j, j % 2
                        pair = pt[:, (2 * n + j // 2) % PT_RING, e, :]
                        if part == 0:
                            rhs = pair.rearrange("p (b q) -> p b q", b=3)[:, 0:3:2, :]
                            cols = slice(0, SEQ)
                        else:
                            rhs, cols = pair[:, P:2 * P], slice(P, SEQ)
                        ins = pe.matmul(ps_pv[32 * j:32 * j + HD + 1, cols], v[:, part, h, :], rhs,
                                        start=part == 0, stop=part == 1, skip_group_check=True,
                                        tile_position=(0, 32 * j))
                ins.then_inc(S["pv_done"], 1)

            def o_turn(g, n):
                pe.wait_ge(S["o_copied"], NP // 2 * g + n + 1)
                wait_tr_free(pe, ("o_turn", g, n))
                turn(lambda t: ot[:, t * P:(t + 1) * P], NT, S["ot_done"])

            def at(g, t):
                pe.wait_ge(S["o_norm"], NP // 2 * (g + 1))
                wait_tr_free(pe, ("at", g, t))
                turn(lambda c: on[:, t, c * P:(c + 1) * P], KC, S["at_done"])

            def wo(g, t, c):
                if c == 0:
                    pe.wait_ge(S["atl_ready"], v_tile(g, t))
                    wait_mm_free(pe, ("wo", g, t))
                    if g % NB == 0:
                        pe.wait_ge(S["wsplit_l"], N_OUT_A if g < NB else N_OUT_B)
                ins = passes(mm_bank(("wo", g, t)), lambda c: at_h[:, t, c, :], lambda c: at_l[:, t, c, :],
                             lambda c: wo_h[:, c, :], lambda c: wo_l[:, c, :], c, c == 0, c == KC - 1)
                if c == KC - 1:
                    ins.then_inc(S["wo_done"], 1)

            def x2t(g, t):
                pe.wait_ge(S["ln2_norm"], v_tile(g, t))
                wait_tr_free(pe, ("x2t", g, t))
                turn(lambda c: on[:, t, c * P:(c + 1) * P], KC, S["x2t_done"])

            def h_step(g, t):
                pe.wait_ge(S["x2l_ready"], v_tile(g, t))
                wait_mm_free(pe, ("h", g, t))
                if g == 0:
                    pe.wait_ge(S["wsplit_l"], N_GATE)
                for c in range(KC):
                    ins = passes(mm_bank(("h", g, t))[:, 0:E + E * R], lambda c: at_h[:, t, c, :],
                                 lambda c: at_l[:, t, c, :], lambda c: wg_h[:, c, :], lambda c: wg_l[:, c, :],
                                 c, c == 0, c == KC - 1)
                ins.then_inc(S["h_done"], 1)

            def hwt(g):
                pe.wait_ge(S["hw_ready"], g + 1)
                wait_tr_free(pe, ("hwt", g))
                turn(lambda t: hs[:, t, E:E + E * R], NT, S["hwt_done"])

            def ffn(g, t, c):
                dst = mm_bank(("ffn", g, t))
                if c == 0:
                    pe.wait_ge(S["x2l_ready"], v_tile(g, t))
                    wait_mm_free(pe, ("ffn", g, t))
                    if g == 0:
                        pe.wait_ge(S["wsplit_l"], N_LOW)
                if c < KC:
                    passes(dst, lambda c: at_h[:, t, c, :], lambda c: at_l[:, t, c, :],
                           lambda c: wb_h[:, c, :], lambda c: wb_l[:, c, :], c, c == 0, False)
                else:
                    pe.wait_ge(S["hwl_ready"], g + 1)
                    passes(dst, lambda c: hw_h[:, t, :], lambda c: hw_l[:, t, :],
                           lambda c: wl_h[:, 0, :], lambda c: wl_l[:, 0, :], c, False, True)\
                        .then_inc(S["ffn_done"], 1)

            pe.wait_ge(S["ident_ready"], 1)
            does = {"xt": xt, "qkv": qkv, "head_turn": head_turn, "s": s_step, "m_turn": m_turn, "st": st_step,
                    "pv": pv_step, "o_turn": o_turn, "at": at, "wo": wo, "x2t": x2t, "h": h_step, "hwt": hwt,
                    "ffn": ffn}
            for step in plan:
                if step == ("s", 0, 0):
                    pe.wait_ge(S["small_ready"], 1)
                if step[0] in does:
                    does[step[0]](*step[1:])

        @block.scalar
        def _(act):
            def w_high(n):
                if n < N_QKV_A:
                    act.wait_ge(piece_in[n], 16)
                else:
                    act.wait_ge(matrix_in[matrix_of[n - N_QKV_A]], 16)
                nc.scalar.activation(pieces[n][1], pieces[n][0], ACT.Copy).then_inc(S["wsplit_h"], 1)

            def high(dst, done, ready, n):
                act.wait_ge(done, n)
                nc.scalar.activation(dst, ps_tr[:, :].rearrange("p (c q) -> p c q", c=KC), ACT.Copy).then_inc(ready, 1)

            def xt_high(g, t):
                if g:
                    act.wait_ge(S["qkv_done"], 3 * NT * (g - 1) + 3 * t + 3)
                high(xt_h[:, t, :, :], S["xt_done"], S["xth_ready"], v_tile(g, t))

            def expand_high(g, t, u):
                k = NT * g + t
                if g < NB:
                    act.wait_ge(S["q_ready"], 2 * k + u + 1)
                else:
                    act.wait_ge(S["qkv_out"], 3 * k + u + 1)
                if k:
                    act.wait_ge(S["t_done"], 4 * (k - 1) + 2 * u + 2)
                dst = (qa, ka)[u]
                step = (2, 1)[u]
                o = dst[:, :, 0:EXTRA + HD].rearrange("p h (r d) -> p h r d", d=HD)[:, :, 0:step + 1:step, :]
                i = qf[:, u, :].rearrange("p (h r d) -> p h r d", h=H, r=1).broadcast_to([P, H, 2, HD])
                nc.scalar.activation(o, i, ACT.Copy).then_inc(S["exp_hi"], 1)

            def turn_act(g, t, u):
                act.wait_ge(S["t_done"], 4 * (NT * g + t) + 2 * u + 2)
                nc.scalar.activation((qt, kt)[u][:, 8:16, t * P:(t + 1) * P],
                                     ps_st[:, :].rearrange("p (i q) -> p i q", i=8), ACT.Copy)\
                    .then_inc(S["t_act"], 1)

            def v_copy(g):
                if g:
                    act.wait_ge(S["pv_done"], NP // 2 * g)
                else:
                    act.wait_ge(S["ones_ready"], 1)
                act.wait_ge(S["qkv_out"], 3 * NT * (g + 1))
                nc.scalar.activation(v[:, :, :, 0:HD], vn[:, :, :].rearrange("p t (h d) -> p t h d", d=HD), ACT.Copy)\
                    .then_inc(S["v_copied"], 1)

            def m_copy(g, n):
                act.wait_ge(S["mt_done"], NG * g + n + 1)
                if g:
                    act.wait_ge(S["mrow_in"], 32 * (NG * (g - 1) + n + 1))
                r = slice(32 * n, 32 * n + 32)
                nc.scalar.activation(nmt[r, :], ps_tr[r, 0:P], ACT.Copy).then_inc(S["nmt_copied"], 1)

            def exp_step(g, p):
                act.wait_ge(S["st_done"], NP * g + p + 1)
                if p >= PT_RING:
                    act.wait_ge(S["pv_done"], NP // 2 * g + (p - PT_RING) // 2 + 1)
                elif g:
                    act.wait_ge(S["pv_done"], NP // 2 * g)
                else:
                    act.wait_ge(S["wsplit_l"], N_QKV_A)
                nc.scalar.activation(pt[:, p % PT_RING, :, :],
                                     ps_st[:, :].rearrange("p (e q) -> p e q", e=2)[:, :, 0:SEQ + P],
                                     ACT.Exp, scale=HD ** -0.5).then_inc(S["st_exp"], 1)

            def o_copy(g, n):
                k = NP // 2 * g + n
                act.wait_ge(S["pv_done"], k + 1)
                if k:
                    act.wait_ge(S["ot_done"], k)
                nc.scalar.activation(ot[:, :], ps_pv[:, 0:SEQ], ACT.Copy).then_inc(S["o_copied"], 1)

            def at_high(g, t):
                if g:
                    act.wait_ge(S["ffn_done"], v_tile(g - 1, t))
                high(at_h[:, t, :, :], S["at_done"], S["ath_ready"], v_tile(g, t))

            def x2t_high(g, t):
                act.wait_ge(S["wo_done"], v_tile(g, t))
                high(at_h[:, t, :, :], S["x2t_done"], S["x2h_ready"], v_tile(g, t))

            def route_exp(g):
                act.wait_ge(S["rt_step"], 8 * g + 2)
                nc.scalar.activation(el[:, :, :], zl[:, :, :], ACT.Exp).then_inc(S["rt_exp"], 1)

            def hwt_high(g):
                act.wait_ge(S["hwt_done"], g + 1)
                if g:
                    act.wait_ge(S["ffn_done"], NT * g)
                nc.scalar.activation(hw_h[:, :, :], ps_tr[:, 0:NT * P].rearrange("p (t q) -> p t q", t=NT), ACT.Copy)\
                    .then_inc(S["hwh_ready"], 1)

            does = {"w_high": w_high, "xt_high": xt_high, "expand_high": expand_high, "turn_act": turn_act,
                    "v_copy": v_copy, "m_copy": m_copy, "exp": exp_step, "o_copy": o_copy, "at_high": at_high,
                    "x2t_high": x2t_high, "route_exp": route_exp, "hwt_high": hwt_high}
            for step in plan:
                if step == ("expand_high", 0, 0, 0):
                    act.wait_ge(S["kaug_ready"], 2)
                if step[0] in does:
                    does[step[0]](*step[1:])

        @block.gpsimd
        def _(pool):
            def power(dst, src, n):
                return nc.gpsimd.tensor_tensor(dst, src, neg_half[:, 0:n], ALU.pow)

            def ln1_power(g):
                pool.wait_ge(S["ln1_step"], 3 * NT * (g + 1))
                power(rs1[:, :], ve1[:, :], NT).then_inc(S["ln1_rstd"], 1)

            def ln2_power(g):
                pool.wait_ge(S["ln2_step"], 3 * NT * (g + 1))
                power(rs2[:, :], ve2[:, :], NT).then_inc(S["ln2_rstd"], 1)

            def qk_power(g, t, n):
                pool.wait_ge(S["lnq_step"], 3 * (2 * (NT * g + t) + n + 1))
                power(rsq[:, n:n + 1], veq[:, n:n + 1], 1).then_inc(S["lnq_rstd"], 1)

            def qk_affine(g, t, n):
                k = 2 * (NT * g + t) + n
                pool.wait_ge(S["lnq_norm"], k + 1)
                if k == 0:
                    pool.wait_ge(S["row_in"], 16 * 5)
                nc.gpsimd.tensor_tensor(qf[:, n, :], qf[:, n, :], row[:, 2 * n, :], ALU.mult)\
                    .then_inc(S["q_scaled"], 1)
                pool.wait_ge(S["q_scaled"], k + 1)
                nc.gpsimd.tensor_tensor(qf[:, n, :], qf[:, n, :], row[:, 2 * n + 1, :], ALU.add)\
                    .then_inc(S["q_ready"], 1)

            def expand_low(g, t, u):
                dst = (qa, ka)[u]
                pool.wait_ge(S["exp_hi"], 2 * (NT * g + t) + u + 1)
                c = (HD, 2 * HD)[u]
                nc.gpsimd.tensor_tensor(dst[:, :, c:c + HD], qf[:, u, :].rearrange("p (h d) -> p h d", d=HD),
                                        dst[:, :, 0:HD], ALU.subtract).then_inc(S["exp_lo"], 1)

            def expand_extra(g, t, u):
                dst = (qa, ka)[u]
                if g == 0 and t == 0:
                    pool.wait_ge(S["kaug_ready"], 2)
                else:
                    pool.wait_ge(S["t_done"], 4 * (NT * g + t - 1) + 2 * u + 2)
                extra = nc.gpsimd.tensor_copy(dst[:, :, EXTRA + 8:HROWS],
                                              fence[:, u, t, :].rearrange("p (h r) -> p h r", h=1)
                                              .broadcast_to([P, H, 8]))
                tile_rows = dst[:, :, EXTRA + 6:EXTRA + 8]
                if g < NB and u == 0:
                    extra = nc.gpsimd.memset(tile_rows.bitcast(F32), float(t))
                elif g < NB and t == 0:
                    extra = nc.gpsimd.tensor_copy(tile_rows, kblock[:, :, :])
                elif g < NB:
                    extra = nc.gpsimd.memset(tile_rows.bitcast(F32), 0.0)
                elif g == NB and t == 0 and u == 1:
                    extra = nc.gpsimd.memset(ka[:, :, EXTRA + 2:EXTRA + 8].bitcast(F32), 0.0)
                extra.then_inc(S["aug_set"], 1)

            def mask(g, p):
                pool.wait_ge(S["st_exp"], NP * g + p + 1)
                w = pt[:, p % PT_RING, :, 0:2 * P]
                nc.gpsimd.affine_select(out=w, in_=w, compare_op=ALU.is_ge, fill=0.0, base=0,
                                        pattern=[[0, 4], [1, P]], channel_multiplier=-1).then_inc(S["p_masked"], 1)

            def x2_plus(g, t):
                pool.wait_ge(S["ln2_norm"], v_tile(g, t))
                if g == 0:
                    pool.wait_ge(S["row_in"], 16 * 5)
                nc.gpsimd.tensor_tensor(x2[:, t, :], x2[:, t, :], row[:, 4, :], ALU.add).then_inc(S["x2_plus"], 1)

            def x2_bias(g, t):
                if t == 0:
                    pool.wait_ge(S["x2_in"], 16 * (g + 1))
                    pool.wait_ge(S["row_in"], 16 * 9)
                nc.gpsimd.tensor_tensor(x2[:, t, :], x2[:, t, :], row[:, 3, :], ALU.add).then_inc(S["x2_bias"], 1)

            nc.gpsimd.memset(neg_half[:, :], -0.5).then_inc(S["half_ready"], 1)
            nc.gpsimd.memset(nms[:, :, :, :, :].bitcast(F32), 0.0).then_inc(S["nms_zeroed"], 1)
            pool.wait_ge(S["half_ready"], 1)
            does = {"ln1_power": ln1_power, "ln2_power": ln2_power, "qk_power": qk_power, "qk_affine": qk_affine,
                    "expand_low": expand_low, "expand_extra": expand_extra, "mask": mask, "x2_plus": x2_plus,
                    "x2_bias": x2_bias}
            for step in plan:
                if step == ("expand_extra", 0, 0, 0):
                    pool.wait_ge(S["small_ready"], 1)
                if step[0] in does:
                    does[step[0]](*step[1:])

        @block.vector
        def _(dve):
            def w_low(n):
                dve.wait_ge(S["wsplit_h"], n + 1)
                nc.vector.tensor_tensor(pieces[n][2], pieces[n][0], pieces[n][1], ALU.subtract)\
                    .then_inc(S["wsplit_l"], 1)

            def norm_stats(src, st, mv, ve, steps, n):
                nc.vector.bn_stats(st, src).then_inc(steps, 1)
                dve.wait_ge(steps, 3 * n + 1)
                nc.vector.bn_aggr(mv, st).then_inc(steps, 1)
                dve.wait_ge(steps, 3 * n + 2)
                nc.vector.tensor_scalar(ve, mv[:, 1:2], LN_EPS, None, ALU.add).then_inc(steps, 1)

            def ln1_stats(g, t):
                dve.wait_ge(S["xa_in"], 16 * (g + 1))
                norm_stats(xa[:, t, :], st1[:, t, :], mv1[:, t, :], ve1[:, t:t + 1], S["ln1_step"], NT * g + t)

            def ln1_norm(g, t):
                dve.wait_ge(S["ln1_rstd"], g + 1)
                nc.vector.tensor_scalar(xa[:, t, :], xa[:, t, :], mv1[:, t, 0:1], rs1[:, t:t + 1],
                                        ALU.subtract, ALU.mult).then_inc(S["ln1_norm"], 1)

            def low(hi, lo, ready_h, ready_l, n):
                dve.wait_ge(ready_h, n)
                nc.vector.tensor_tensor(lo, ps_tr[:, :].rearrange("p (c q) -> p c q", c=KC), hi, ALU.subtract)\
                    .then_inc(ready_l, 1)

            def xt_low(g, t):
                low(xt_h[:, t, :, :], xt_l[:, t, :, :], S["xth_ready"], S["xtl_ready"], v_tile(g, t))

            def qkv_out(g, t, n):
                src = mm_bank(("qkv", g, t, n))
                dve.wait_ge(S["qkv_done"], 3 * NT * g + 3 * t + n + 1)
                k = 2 * (NT * g + t) + n
                if n == 2:
                    dst = vn[:, t, :]
                    if g:
                        dve.wait_ge(S["v_copied"], g)
                else:
                    dst = qf[:, n, :]
                    if k >= 2:
                        dve.wait_ge(S["exp_lo"], k - 1)
                if g < NB:
                    nc.vector.tensor_scalar(dst, src, CLIP, -CLIP, ALU.min, ALU.max).then_inc(S["qkv_out"], 1)
                    if n < 2:
                        dve.wait_ge(S["qkv_out"], 3 * NT * g + 3 * t + n + 1)
                        norm_stats(dst, stq[:, n, :], mvq[:, n, :], veq[:, n:n + 1], S["lnq_step"], k)
                else:
                    dve.wait_ge(S["row_in"], 16 * 9)
                    nc.vector.tensor_tensor(dst, src, row[:, n, :], ALU.add).then_inc(S["qkv_out"], 1)

            def qk_norm(g, t, n):
                dve.wait_ge(S["lnq_rstd"], 2 * (NT * g + t) + n + 1)
                nc.vector.tensor_scalar(qf[:, n, :], qf[:, n, :], mvq[:, n, 0:1], rsq[:, n:n + 1],
                                        ALU.subtract, ALU.mult).then_inc(S["lnq_norm"], 1)

            def turn_dve(g, t, u):
                dve.wait_ge(S["t_done"], 4 * (NT * g + t) + 2 * u + 1)
                nc.vector.tensor_copy((qt, kt)[u][:, 0:8, t * P:(t + 1) * P],
                                      ps_s[:, :].rearrange("p (i q) -> p i q", i=8)).then_inc(S["t_dve"], 1)

            def s_max(g, p):
                dve.wait_ge(S["s_done"], NP * g + p + 1)
                nc.vector.tensor_reduce(pm[:, p, :, :],
                                        ps_s[:, :].rearrange("p (e b k) -> p e b k", e=2, b=4)[:, :, 0:3, :], AX_X,
                                        ALU.max, negate=True).then_inc(S["s_max"], 1)

            def m_split(g, n):
                k = 4 * (NG * g + n)
                dve.wait_ge(S["s_max"], NP * g + 4 * (n + 1))
                part = pm[:, 4 * n:4 * n + 4, :, :].rearrange("p i e b -> p e i b")
                nc.vector.tensor_copy(nm[:, :, :, 0], part[:, :, :, 0]).then_inc(S["nm_step"], 1)
                nc.vector.tensor_tensor(nm[:, :, :, 1], part[:, :, :, 1], part[:, :, :, 2], ALU.min)\
                    .then_inc(S["nm_step"], 1)
                flat = nm[:, :, :, :].rearrange("p e i t -> p e (i t)")
                dve.wait_ge(S["nm_step"], k + 2)
                if k:
                    dve.wait_ge(S["mt_done"], NG * g + n)
                else:
                    dve.wait_ge(S["nms_zeroed"], 1)
                nc.vector.tensor_copy(nms[:, n, :, 0, :], flat).then_inc(S["nm_step"], 1)
                dve.wait_ge(S["nm_step"], k + 3)
                nc.vector.tensor_tensor(nms[:, n, :, 1, :], flat, nms[:, n, :, 0, :], ALU.subtract)\
                    .then_inc(S["nm_step"], 1)

            def o_norm(g, n):
                k = NP // 2 * g + n
                dve.wait_ge(S["ot_done"], k + 1)
                view = ps_tr[:, 0:NT * P].rearrange("p (t j r) -> p t j r", t=NT, j=4)
                if k:
                    dve.wait_ge(S["o_norm"], k)
                nc.vector.reciprocal(rc[:, :, :], view[:, :, :, HD]).then_inc(S["o_rec"], 1)
                dve.wait_ge(S["o_rec"], k + 1)
                if g and n == 0:
                    dve.wait_ge(S["x2t_done"], NT * g)
                o = on[:, :, 4 * HD * n:4 * HD * (n + 1)].rearrange("p t (j d) -> p t j d", j=4)
                nc.vector.tensor_tensor(o, view[:, :, :, 0:HD],
                                        rc[:, :, :].rearrange("p t (j r) -> p t j r", r=1).broadcast_to([P, NT, 4, HD]),
                                        ALU.mult).then_inc(S["o_norm"], 1)

            def at_low(g, t):
                low(at_h[:, t, :, :], at_l[:, t, :, :], S["ath_ready"], S["atl_ready"], v_tile(g, t))

            def wo_out(g, t):
                dve.wait_ge(S["wo_done"], v_tile(g, t))
                dve.wait_ge(S["x2_in"], 16 * (g + 1))
                if g >= NB:
                    dve.wait_ge(S["x2_bias"], v_tile(g - NB, t))
                nc.vector.tensor_tensor(x2[:, t, :], mm_bank(("wo", g, t)), x2[:, t, :], ALU.add)\
                    .then_inc(S["wo_out"], 1)

            def ln2_stats(g, t):
                dve.wait_ge(S["wo_out"], v_tile(g, t))
                norm_stats(x2[:, t, :], st2[:, t, :], mv2[:, t, :], ve2[:, t:t + 1], S["ln2_step"], NT * g + t)

            def ln2_norm(g, t):
                dve.wait_ge(S["ln2_rstd"], g + 1)
                dve.wait_ge(S["at_done"], v_tile(g, t))
                nc.vector.tensor_scalar(on[:, t, :], x2[:, t, :], mv2[:, t, 0:1], rs2[:, t:t + 1],
                                        ALU.subtract, ALU.mult).then_inc(S["ln2_norm"], 1)

            def x2t_low(g, t):
                low(at_h[:, t, :, :], at_l[:, t, :, :], S["x2h_ready"], S["x2l_ready"], v_tile(g, t))

            def h_out(g, t):
                dve.wait_ge(S["h_done"], v_tile(g, t))
                if g:
                    dve.wait_ge(S["hwt_done"], g)
                nc.vector.tensor_copy(hs[:, t, :], mm_bank(("h", g, t))[:, 0:E + E * R]).then_inc(S["h_out"], 1)

            def each_expert(ap):
                return ap.rearrange("p (t r) -> p t r", r=1).broadcast_to([P, NT, E])

            def route_max(g):
                k, st = 8 * g, S["rt_step"]
                dve.wait_ge(S["h_out"], NT * (g + 1))
                nc.vector.tensor_reduce(mxl[:, :], hs[:, :, 0:E], AX_X, ALU.max).then_inc(st, 1)
                dve.wait_ge(st, k + 1)
                nc.vector.tensor_tensor(zl[:, :, :], hs[:, :, 0:E], each_expert(mxl[:, :]), ALU.subtract).then_inc(st, 1)

            def route_rank(g):
                k, st = 8 * g, S["rt_step"]
                dve.wait_ge(S["rt_exp"], g + 1)
                nc.vector.tensor_reduce(esum[:, :], el[:, :, :], AX_X, ALU.add).then_inc(st, 1)
                dve.wait_ge(st, k + 3)
                nc.vector.reciprocal(erec[:, :], esum[:, :]).then_inc(st, 1)
                dve.wait_ge(st, k + 4)
                nc.vector.tensor_tensor(pr[:, :, :], el[:, :, :], each_expert(erec[:, :]), ALU.mult).then_inc(st, 1)
                dve.wait_ge(st, k + 5)
                for t in range(NT):
                    pj = pr[:, t, :].rearrange("p (i j) -> p i j", i=1).broadcast_to([P, E, E])
                    pi = pr[:, t, :].rearrange("p (i j) -> p i j", j=1).broadcast_to([P, E, E])
                    nc.vector.tensor_tensor(gt[:, t * E:(t + 1) * E, :], pj, pi, ALU.is_gt)
                    ins = nc.vector.tensor_tensor(ge[:, t * E:(t + 1) * E, :], pj, pi, ALU.is_ge)
                ins.then_inc(st, 1)
                dve.wait_ge(st, k + 6)
                for t in range(NT):
                    ins = nc.vector.tensor_tensor(ge[:, t * E:(t + 1) * E, :], ge[:, t * E:(t + 1) * E, :],
                                                  tri[:, :, :], ALU.mult)
                ins.then_inc(st, 1)
                dve.wait_ge(st, k + 7)
                nc.vector.tensor_tensor(gt[:, :, :], gt[:, :, :], ge[:, :, :], ALU.max).then_inc(st, 1)

            def route_weight(g):
                k, st = 5 * g, S["rt2_step"]
                dve.wait_ge(S["rt_step"], 8 * (g + 1))
                flat = pr[:, :, :].rearrange("p t i -> p (t i)")
                ranks = rank[:, :, :].rearrange("p t i -> p (t i)")
                nc.vector.tensor_reduce(ranks, gt[:, :, :], AX_X, ALU.add).then_inc(st, 1)
                dve.wait_ge(st, k + 1)
                nc.vector.scalar_tensor_tensor(flat, ranks, 1.5, flat, ALU.is_lt, ALU.mult).then_inc(st, 1)
                dve.wait_ge(st, k + 2)
                nc.vector.tensor_reduce(esum[:, :], pr[:, :, :], AX_X, ALU.add).then_inc(st, 1)
                dve.wait_ge(st, k + 3)
                nc.vector.reciprocal(erec[:, :], esum[:, :]).then_inc(st, 1)
                dve.wait_ge(st, k + 4)
                nc.vector.tensor_tensor(pr[:, :, :], pr[:, :, :], each_expert(erec[:, :]), ALU.mult).then_inc(st, 1)
                dve.wait_ge(st, k + 5)
                for t in range(NT):
                    o = hs[:, t, E:E + E * R].rearrange("p (e r) -> p e r", e=E)
                    w = pr[:, t, :].rearrange("p (e r) -> p e r", r=1).broadcast_to([P, E, R])
                    ins = nc.vector.tensor_tensor(o, o, w, ALU.mult)
                ins.then_inc(S["hw_ready"], 1)

            def hwt_low(g):
                dve.wait_ge(S["hwh_ready"], g + 1)
                nc.vector.tensor_tensor(hw_l[:, :, :], ps_tr[:, 0:NT * P].rearrange("p (t q) -> p t q", t=NT),
                                        hw_h[:, :, :], ALU.subtract).then_inc(S["hwl_ready"], 1)

            def ffn_out(g, t):
                dve.wait_ge(S["ffn_done"], v_tile(g, t))
                dve.wait_ge(S["x2_plus"], v_tile(g, t))
                nc.vector.tensor_tensor(x2[:, t, :], mm_bank(("ffn", g, t)), x2[:, t, :], ALU.add)\
                    .then_inc(S["y_ready"], 1)

            def small_constants(_):
                dve.wait_ge(S["const_in"], 16 * 4)
                nc.vector.tensor_copy(cbf[:, :], qf[:, 0, 0:2 * P])
                nc.vector.tensor_copy(fence[:, :, :, :].rearrange("p c t r -> p (c t r)"), qf[:, 0, 2 * P:2 * P + 32])
                nc.vector.tensor_copy(tri[:, :, :].rearrange("p i j -> p (i j)"), qf[:, 0, 2 * P + 32:2 * P + 96])\
                    .then_inc(S["small_ready"], 1)
                nc.vector.tensor_copy(ka[:, :, EXTRA:HROWS], x2[:, 0, :].rearrange("p (h r) -> p h r", h=H))\
                    .then_inc(S["kaug_ready"], 1)
                nc.vector.tensor_copy(qa[:, :, EXTRA:HROWS], x2[:, 1, :].rearrange("p (h r) -> p h r", h=H))\
                    .then_inc(S["kaug_ready"], 1)
                dve.wait_ge(S["small_ready"], 1)

            does = {"w_low": w_low, "ln1_stats": ln1_stats, "ln1_norm": ln1_norm, "xt_low": xt_low,
                    "qkv_out": qkv_out, "qk_norm": qk_norm, "turn_dve": turn_dve, "s_max": s_max,
                    "m_split": m_split, "o_norm": o_norm, "at_low": at_low, "wo_out": wo_out,
                    "ln2_stats": ln2_stats, "ln2_norm": ln2_norm, "x2t_low": x2t_low, "h_out": h_out,
                    "route_max": route_max, "route_rank": route_rank, "route_weight": route_weight,
                    "hwt_low": hwt_low, "ffn_out": ffn_out, "small_constants": small_constants}
            nc.vector.memset(ps_pv[:, :], 0.0).then_inc(S["pv_zeroed"], 1)
            nc.vector.memset(v[:, :, :, HD:HD + 1], 1.0).then_inc(S["ones_ready"], 1)
            for step in plan:
                if step == ("ln1_norm", 0, 0):
                    dve.wait_ge(S["ident_in"], 16)
                    nc.vector.tensor_copy(ident_r[:, :], nmt_f[:, :]).then_inc(S["ident_ready"], 1)
                if step[0] in does:
                    does[step[0]](*step[1:])


def constants():
    import numpy as np

    def high(a):
        m, e = np.frexp(a.astype(np.float64))
        return np.ldexp(np.rint(m * 4096) / 4096, e).astype(np.float32)

    ident = np.eye(P, dtype=np.float32)
    q, k = np.arange(P)[:, None], np.arange(P)[None, :]
    mask = np.where(k > q, -(2.0 ** 100), 0.0).astype(np.float32)
    m = np.arange(1, H + 1, dtype=np.float32) * np.float32(8.0 / H)
    slope = (1.0 / np.power(np.float32(2.0), m)).astype(np.float32)
    root = np.float32(HD ** 0.5)
    kaug = np.zeros((P, H, HD), np.float32)
    qaug = np.zeros((P, H, HD), np.float32)
    pos = np.arange(P, dtype=np.float32)[:, None]
    kaug[:, :, 0:2] = 1.0
    a = (slope[None, :] * pos).astype(np.float32) * root
    kaug[:, :, 2] = high(a)
    kaug[:, :, 3] = a - high(a)
    qaug[:, :, 2:4] = 1.0
    s4 = slope * root
    kaug[:, :, 4] = -high(s4)
    kaug[:, :, 5] = -(s4 - high(s4))
    qaug[:, :, 4:6] = pos[:, :, None]
    kblock = np.zeros((P, H, 2), np.float32)
    kblock[:, :, 0] = -high(s4) * P
    kblock[:, :, 1] = -(s4 - high(s4)) * P
    blk = (np.arange(NT)[None, :] * P + np.arange(P)[:, None]) // 32
    n8 = np.arange(8)
    fence = np.zeros((P, 2, NT, 8), np.float32)
    fence[:, 0] = blk[:, :, None] < n8
    fence[:, 1] = np.where(blk[:, :, None] == n8, -(2.0 ** 100), 0.0)
    tri = np.broadcast_to(np.tril(np.ones((E, E), np.float32), -1)[None], (P, E, E))
    small = np.concatenate([ident, mask, fence.reshape(P, -1), tri.reshape(P, -1)], 1)
    return [ident, small, kaug.reshape(P, H * HD), qaug.reshape(P, H * HD), kblock]


def kernel(**inputs):
    import numpy as np
    import concourse.bacc as bacc
    from concourse.bass_utils import run_bass_kernel_spmd as run

    nc = bacc.Bacc("TRN2", target_bir_lowering=False, num_devices=1)
    i = {k: np.asarray(a) for k, a in inputs.items()}
    arrays = {}

    def given(name, a):
        a = np.ascontiguousarray(a)
        arrays[name] = a
        return nc.dram_tensor(name, a.shape, mybir.dt.from_np(a.dtype), kind="ExternalInput").ap()

    def turned(w):
        return w.T.reshape(KC, P, -1).transpose(1, 0, 2)

    x = given("x", i["L0_attn_a_hidden_states"].reshape(NB * SEQ, D))
    consts = [given(f"const{n}", a) for n, a in enumerate(constants())]
    a3 = i["L0_attn_a_Wqkv"].reshape(3, D, D)
    b3 = np.stack([i["L0_attn_b_Wq"], i["L0_attn_b_Wk"], i["L0_attn_b_Wv"]])
    wqkv = given("wqkv", np.stack([np.stack([turned(w) for w in ws]) for ws in (a3, b3)]))
    wout = given("wout", np.stack([turned(i["L0_attn_a_Wout"]), turned(i["L0_attn_b_Wo"])]))
    wbase = given("wbase", turned(i["L0_ffn_W_base"]))
    wgate = given("wgate", turned(np.concatenate([i["L0_ffn_W_gate"], i["L0_ffn_A"].reshape(E * R, D)])))
    wlow = given("wlow", i["L0_ffn_B"].transpose(0, 2, 1).reshape(E * R, 1, D))
    rows = given("rows", np.stack([i["L0_attn_a_q_ln_w"], i["L0_attn_a_q_ln_b"], i["L0_attn_a_k_ln_w"],
                                   i["L0_attn_a_k_ln_b"], i["L0_attn_b_bq"], i["L0_attn_b_bk"],
                                   i["L0_attn_b_bv"], i["L0_attn_b_bo"], i["L0_ffn_b_base"]]))
    mid = nc.dram_tensor("mid", (NB * SEQ, D), F32, kind="Internal").ap()
    scratch = [nc.dram_tensor(f"scratch{n}", w.shape, F32, kind="Internal").ap()
               for n, w in enumerate([wout[0], wbase, wgate, wlow, wqkv[1, 0], wqkv[1, 1], wqkv[1, 2], wout[1]])]
    out = nc.dram_tensor("out", (NB * SEQ, D), F32, kind="ExternalOutput").ap()
    build(nc, x, consts, wqkv, wout, wbase, wgate, wlow, rows, mid, scratch, out)
    r = run(nc, [arrays], core_ids=[0])
    return r.results[0]["out"].reshape(NB, SEQ, D)
```

```python
from contextlib import ExitStack

import concourse.bass as bass
from concourse import mybir

F32 = mybir.dt.float32
F32R = mybir.dt.float32r
BF16 = mybir.dt.bfloat16
ALU = mybir.AluOpType
ACT = mybir.ActivationFunctionType
AX_X = mybir.AxisListType.X

P = 128
D = 512
KC = D // P
H = 32
HD = D // H
SEQ = 256
NT = SEQ // P
NB = 4
NP = H // 2
NG = NP // 4
E = 8
R = 16
STAGES = 2 * NB
HROWS = 64
EXTRA = 3 * HD
PT_RING = 4
LN_EPS = 1e-5
CLIP = 8.0


URGENCY = dict(x_load=(6.4, 6.4, 6.4, 6.4), ln1_stats=(1.5, 5.8, 7.6, 1.8), ln1_norm=(2.0, 2.4, 7.5, 2.4),
               xt=(7.7, 3.7, 3.7, 1.3), xt_high=(7.9, 2.9, 2.9, 8.9), xt_low=(0.8, 1.7, 1.4, 2.5),
               qkv=(7.9, 7.7, 7.6, 7.9), qkv_out=(4.9, 5.0, 3.3, 8.4), qk_power=(6.8, 6.8, 6.8, 6.8),
               qk_norm=(4.7, 3.2, 7.1, 5.5), expand_high=(4.5, 2.3, 1.6, 2.3),
               expand_low=(8.0, 2.9, 2.9, 3.2), expand_extra=(8.8, 4.1, 4.1, 2.0),
               head_turn=(6.7, 2.5, 6.3, 1.8), turn_dve=(7.6, 5.1, 1.9, 7.5), turn_act=(2.4, 2.4, 2.4, 2.4),
               at=(5.2, 6.2, 2.9, 8.1), at_high=(7.8, 1.3, 1.3, 7.8), at_low=(6.8, 3.2, 3.2, 6.8),
               wo=(7.6, 6.3, 7.4, 5.4), wo_out=(6.9, 0.3, 2.1, 7.8), ln2_stats=(8.7, 1.5, 8.6, 4.0),
               ln2_norm=(2.3, 3.2, 6.3, 3.8), x2t=(2.7, 2.0, 6.7, 6.4), x2t_high=(4.8, 4.8, 4.8, 4.8),
               x2t_low=(7.3, 4.9, 3.1, 2.1), x2_plus=(5.0, 1.2, 1.2, 2.2), h=(5.5, 3.3, 0.8, 2.9),
               h_out=(9.0, 5.0, 5.8, 2.2), ffn=(5.4, 4.8, 4.9, 4.2), ffn_out=(8.7, 1.5, 1.5, 5.4),
               ln1_power=(3.0, 1.8, 0.0, 8.1), ln2_power=(6.4, 5.1, 5.7, 6.4), x2_load=(5.7, 5.7, 5.7, 5.7),
               y_store=(3.8, 9.0, 9.0, 3.4), v_copy=(7.5, 6.8, 4.3, 1.6), route_max=(1.7, 2.9, 7.9, 5.1),
               route_exp=(6.4, 6.5, 5.6, 6.4), route_rank=(6.7, 7.1, 7.1, 2.2),
               route_weight=(0.5, 4.9, 7.3, 7.9), hwt=(1.7, 1.6, 1.2, 5.9), hwt_high=(2.8, 4.9, 8.7, 2.8),
               hwt_low=(7.7, 5.1, 5.1, 4.2), s=(3.4, 2.2, 3.5, 1.6), s_max=(1.3, 2.3, 0.4, 0.3),
               st=(0.3, 0.2, 2.0, 1.9), exp=(4.4, 8.8, 3.0, 3.1), mask=(1.0, 1.2, 4.6, 7.9),
               m_split=(0.8, 3.0, 2.5, 2.0), m_turn=(1.0, 1.0, 0.5, 0.1), m_copy=(7.3, 8.4, 8.4, 6.3),
               m_rows=(2.6, 2.0, 2.0, 3.8), pv=(6.3, 2.8, 7.3, 3.5), o_copy=(0.5, 8.1, 8.1, 8.9),
               o_turn=(2.4, 2.5, 2.5, 0.2), o_norm=(5.0, 2.8, 6.0, 3.1), w_high=(8.6,), w_low=(5.1,),
               w_load=(2.0,), small_constants=(5.5,), b_rows=(1.2,), bounce=(2.5,),
               x2_bias=(7.2, 4.4, 7.0, 7.0), piece_in=(8.3,))


def work():
    steps = {}

    def add(kind, at, engine, length, after, take=None, give=None):
        steps[(kind, *at)] = (engine, length, after, take, give)

    N_A, N_OUT, N_BASE, N_GATE, N_LOW = (KC * 3, KC * 4, KC * 5, KC * 6, KC * 6 + 1)
    N_B = N_LOW + 3 * KC
    for n in range(3 * KC):
        add("piece_in", (n,), "queue", 5.0 if n == 0 else 3.0 if n == 2 * KC else 0.74,
            [("constants_in", 0)] if n == 2 * KC else [("piece_in", n - 1)] if n else [])
    for m in range(8):
        after = [("qkv_out", 0, 0, 2)] if m < 4 else [("qkv", NB - 1, 1, m - 4, KC - 1)] if m < 7 else \
            [("wo", NB - 1, 1, KC - 1)]
        add("bounce", (m,), "SP", 5.0, [("x_load", 1)] if m < 4 else [("s", 0, 4 * m - 16, 0)])
        add("w_load", (m,), "SP", 4.0, after + [("bounce", m)] + ([("w_load", m - 1)] if m else []))
    for n in range(N_B + KC):
        m = 0 if n < N_OUT else 1 if n < N_BASE else 2 if n < N_GATE else 3 if n < N_LOW else 4 + (n - N_LOW) // KC
        add("w_high", (n,), "ACT", 0.52, [("piece_in", n) if n < N_A else ("w_load", m)])
        add("w_low", (n,), "DVE", 0.6, [("w_high", n)])
    add("constants_in", (0,), "queue", 2.3, [("piece_in", 2 * KC - 1)])
    add("small_constants", (0,), "DVE", 1.1, [("constants_in", 0)])
    add("b_rows", (0,), "SP", 2.0, [("qk_norm", NB - 1, 1, 1)])

    for g in range(STAGES):
        a = g < NB
        b = g - 1
        add("x_load", (g,), "SP", 3.5,
            [("xt", b, 1), ("y_store", g - NB, 1)] + ([("piece_in", 3 * KC - 1)] if g == 1 else []))
        for t in range(NT):
            add("ln1_stats", (g, t), "DVE", 1.0, [("x_load", g)])
            add("ln1_power", (g, t), "POOL", 0.46, [("ln1_stats", g, t)])
            add("ln1_norm", (g, t), "DVE", 0.45, [("ln1_power", g, t)])
            add("xt", (g, t), "PE", 0.43, [("ln1_norm", g, t), ("qkv", b, t, 2, KC - 1)], take="turns")
            add("xt_high", (g, t), "ACT", 0.5, [("xt", g, t)])
            add("xt_low", (g, t), "DVE", 0.62, [("xt_high", g, t)], give="turns")
            for n in range(3):
                last = (g, 0) if t else (b, 1)
                first = [("xt_low", g, t), ("v_copy", b) if n == 2 else ("expand_low", *last, n)]
                if t == 0 and g % NB == 0:
                    first.append(("w_low", KC * (n + 1) - 1 + (0 if a else N_LOW)))
                if g == NB:
                    first.append(("b_rows", 0))
                for c in range(KC):
                    add("qkv", (g, t, n, c), "PE", 0.66, first if c == 0 else [("qkv", g, t, n, c - 1)],
                        take="products" if c == 0 else None)
                add("qkv_out", (g, t, n), "DVE", 2.35 if n < 2 and a else 0.62,
                    [("qkv", g, t, n, KC - 1), ("small_constants", 0)],
                    give="products")
                if n < 2 and a:
                    add("qk_power", (g, t, n), "POOL", 0.5, [("qkv_out", g, t, n)])
                    add("qk_norm", (g, t, n), "DVE", 0.6, [("qk_power", g, t, n)])
            for u in range(2):
                last = ("head_turn", g, 0, u, 1) if t else ("head_turn", b, 1, u, 1)
                add("expand_high", (g, t, u), "ACT", 0.95,
                    [("qk_norm" if a else "qkv_out", g, t, u), last, ("small_constants", 0)])
                add("expand_low", (g, t, u), "POOL", 1.23, [("expand_high", g, t, u)])
                add("expand_extra", (g, t, u), "POOL", 1.1 if a else 0.6, [last, ("small_constants", 0)])
                for half in range(2):
                    out = ("turn_dve", "turn_act")[half]
                    if u:
                        free = (out, g, t, 0)
                    elif t:
                        free = (out, g, 0, 1)
                    else:
                        free = (("s_max", "exp")[half], b, NP - 1, 1)
                    add("head_turn", (g, t, u, half), "PE", 0.81,
                        [("expand_low", g, t, u), ("expand_extra", g, t, u), free, ("st", b, NP - 1, 1)])
                add("turn_dve", (g, t, u), "DVE", 1.13, [("head_turn", g, t, u, 0)])
                add("turn_act", (g, t, u), "ACT", 0.9, [("head_turn", g, t, u, 1)])
        add("v_copy", (g,), "ACT", 0.95, [("qkv_out", g, 0, 2), ("qkv_out", g, 1, 2), ("pv", b, NP // 2 - 1)])
        for p in range(NP):
            for e in range(2):
                add("s", (g, p, e), "PE", 0.32,
                    [("s_max", g, p - 1, e)] if p else [("turn_dve", g, 1, 1), ("turn_act", g, 1, 1)])
                add("s_max", (g, p, e), "DVE", 0.465, [("s", g, p, e)])
                add("st", (g, p, e), "PE", 0.165, [("m_rows", g, p // 4), ("exp", g, p - 1, e)])
                add("exp", (g, p, e), "ACT", 0.375,
                    [("st", g, p, e), ("pv", g, (p - PT_RING) // 2) if p >= PT_RING else ("pv", b, NP // 2 - 1)])
            add("mask", (g, p), "POOL", 0.6, [("exp", g, p, 1)])
        for n in range(NG):
            add("m_split", (g, n), "DVE", 0.57, [("s_max", g, 4 * n + 3, 1), ("m_turn", g, n - 1)])
            add("m_turn", (g, n), "PE", 0.06, [("m_split", g, n)], take="turns")
            add("m_copy", (g, n), "ACT", 0.16, [("m_turn", g, n)], give="turns")
            add("m_rows", (g, n), "SP", 2.9, [("m_copy", g, n)])
        for n in range(NP // 2):
            add("pv", (g, n), "PE", 0.8, [("mask", g, 2 * n + 1), ("v_copy", g),
                                          ("o_copy", g, n - 1) if n else ("o_copy", b, NP // 2 - 1)])
            add("o_copy", (g, n), "ACT", 0.26,
                [("pv", g, n), ("o_turn", g, n - 1) if n else ("o_turn", b, NP // 2 - 1)])
            add("o_turn", (g, n), "PE", 0.22, [("o_copy", g, n)] + ([] if n else [("x2t", b, 1)]), take="turns")
            add("o_norm", (g, n), "DVE", 0.45, [("o_turn", g, n)], give="turns")
        add("x2_load", (g,), "SP", 3.5, [("y_store", b, 1)] if g else [("small_constants", 0)])
        for t in range(NT):
            add("at", (g, t), "PE", 0.43, [("o_norm", g, NP // 2 - 1), ("ffn", b, t, KC)], take="turns")
            add("at_high", (g, t), "ACT", 0.5, [("at", g, t)])
            add("at_low", (g, t), "DVE", 0.62, [("at_high", g, t)], give="turns")
            first = [("at_low", g, t), ("x2_load", g)]
            if g % NB == 0:
                first.append(("w_low", (N_OUT if a else N_B + KC) - 1))
            if not a:
                add("x2_bias", (g, t), "POOL", 1.23, [("x2_load", g)])
                first.append(("x2_bias", g, t))
            for c in range(KC):
                add("wo", (g, t, c), "PE", 0.66, first if c == 0 else [("wo", g, t, c - 1)],
                    take="products" if c == 0 else None)
            add("wo_out", (g, t), "DVE", 0.62, [("wo", g, t, KC - 1)], give="products")
            add("ln2_stats", (g, t), "DVE", 1.0, [("wo_out", g, t)])
            add("ln2_power", (g, t), "POOL", 0.46, [("ln2_stats", g, t)])
            add("ln2_norm", (g, t), "DVE", 0.46, [("ln2_power", g, t)])
            add("x2_plus", (g, t), "POOL", 1.23, [("ln2_norm", g, t)])
            add("x2t", (g, t), "PE", 0.43, [("ln2_norm", g, t), ("wo", g, t, KC - 1)], take="turns")
            add("x2t_high", (g, t), "ACT", 0.5, [("x2t", g, t)])
            add("x2t_low", (g, t), "DVE", 0.62, [("x2t_high", g, t)], give="turns")
            add("h", (g, t), "PE", 1.24, [("x2t_low", g, t), ("hwt", b), ("w_low", N_GATE - 1)], take="products")
            add("h_out", (g, t), "DVE", 0.25, [("h", g, t)], give="products")
            for c in range(KC + 1):
                first = [("x2t_low", g, t), ("x2_plus", g, t), ("w_low", N_LOW - 1), ("h", g, 1)]
                add("ffn", (g, t, c), "PE", 0.66, (first if c == 0 else [("ffn", g, t, c - 1)]) +
                    ([("hwt_low", g)] if c == KC else []), take="products" if c == 0 else None)
            add("ffn_out", (g, t), "DVE", 0.62, [("ffn", g, t, KC)], give="products")
            add("y_store", (g, t), "SP", 2.8, [("ffn_out", g, t)])
        add("route_max", (g,), "DVE", 0.32, [("h_out", g, 0), ("h_out", g, 1)])
        add("route_exp", (g,), "ACT", 0.22, [("route_max", g)])
        add("route_rank", (g,), "DVE", 1.7, [("route_exp", g)])
        add("route_weight", (g,), "DVE", 1.6, [("route_rank", g)])
        add("hwt", (g,), "PE", 0.22, [("route_weight", g), ("ffn", b, 1, KC)], take="turns")
        add("hwt_high", (g,), "ACT", 0.26, [("hwt", g)])
        add("hwt_low", (g,), "DVE", 0.33, [("hwt_high", g)], give="turns")
    return steps


def phase(k):
    if k[0] in ("piece_in", "constants_in", "small_constants", "b_rows", "bounce", "w_load", "w_high", "w_low"):
        return 0
    return 0 if k[1] == 0 else 3 if k[1] == STAGES - 1 else 1 if k[1] < NB else 2


def order_of_work(urgency=URGENCY):
    steps = work()
    taken_by = {"wo_out": "wo", "ffn_out": "ffn", "h_out": "h", "qkv_out": "qkv"}
    needs, users = {}, {k: [] for k in steps}
    for k, (_, _, after, _, _) in steps.items():
        known = [d for d in after if d in steps]
        needs[k] = len(known)
        for d in known:
            users[d].append(k)
    queue = {}
    for k in sorted(steps, key=lambda k: (k[0], k[1], k[3] == 2, *k[2:]) if k[0] in ("qkv", "qkv_out") else k):
        queue.setdefault(k[0], []).append(k)
    kinds = {}
    for kind, ks in queue.items():
        kinds.setdefault(steps[ks[0]][0], []).append(kind)
    head = {kind: 0 for kind in queue}
    free = {e: 0.0 for e in kinds}
    banks, turns_free, units, given = 2, True, {}, set()
    order, events, now = [], [], 0.0
    while len(order) < len(steps):
        moved = True
        while moved:
            moved = False
            for engine in kinds:
                if free[engine] > now + 1e-9:
                    continue
                best = None
                for kind in kinds[engine]:
                    if head[kind] == len(queue[kind]):
                        continue
                    k = queue[kind][head[kind]]
                    take = steps[k][3]
                    if needs[k] or (take == "turns" and not turns_free):
                        continue
                    if take == "products" and len(units) >= banks and len(units) - banks not in given:
                        continue
                    rank = (urgency.get(kind, (0,))[phase(k)], k[1:])
                    if best is None or rank < best[0]:
                        best = (rank, k)
                if best:
                    k = best[1]
                    length, take = steps[k][1], steps[k][3]
                    head[k[0]] += 1
                    order.append(k)
                    if take == "turns":
                        turns_free = False
                    if take == "products":
                        units[k[:-1] if k[0] != "h" else k] = len(units)
                    free[engine] = now + (0.5 if engine == "SP" else length)
                    end = now + length + (0.2 if engine == "PE" else 0.15)
                    events += [(end, k, False), (end + 0.12, k, True), (free[engine], (), False)]
                    for u in users[k]:
                        if steps[u][0] == engine and engine not in ("SP", "queue"):
                            needs[u] -= 1
                    moved = True
        if not events:
            raise RuntimeError("the order of work is stuck")
        now = min(event[0] for event in events)
        due = [event for event in events if event[0] <= now + 1e-9]
        events = [event for event in events if event[0] > now + 1e-9]
        for _, k, to_tensor in due:
            if k:
                if steps[k][4] == "turns" and to_tensor:
                    turns_free = True
                if steps[k][4] == "products" and to_tensor:
                    given.add(units[(taken_by[k[0]], *k[1:])])
                for u in users[k]:
                    other = steps[u][0] != steps[k][0] or steps[k][0] in ("SP", "queue")
                    if other and (steps[u][0] == "PE") == to_tensor:
                        needs[u] -= 1
    return order, now


def build(nc, x_in, consts, wqkv, wout, wbase, wgate, wlow, rows, mid, scratch, out):
    c_ident, c_small, c_kaug, c_qaug, c_kblock = consts
    plan, _ = order_of_work()

    mm_units = [s[:4] if s[0] == "qkv" else s[:3] for s in plan if s[0] in ("wo", "h", "ffn", "qkv")]
    mm_units = list(dict.fromkeys(mm_units))
    tr_units = [s for s in plan if s[0] in ("xt", "at", "x2t", "hwt", "m_turn", "o_turn")]
    mm_no = {s: n for n, s in enumerate(mm_units)}
    tr_no = {s: n for n, s in enumerate(tr_units)}

    with ExitStack() as ctx:
        def sb(name, shape, dt=F32):
            return ctx.enter_context(nc.sbuf_tensor(name, shape, dt))

        def sem(name):
            return ctx.enter_context(nc.semaphore(name))

        wq_h = sb("wq_h", [P, 3, KC, D], F32R)
        wq_l = sb("wq_l", [P, 3, KC, D], F32R)
        wo_h = sb("wo_h", [P, KC, D], F32R)
        wo_l = sb("wo_l", [P, KC, D], F32R)
        wb_h = sb("wb_h", [P, KC, D], F32R)
        wb_l = sb("wb_l", [P, KC, D], F32R)
        wg_h = sb("wg_h", [P, KC, E + E * R], F32R)
        wg_l = sb("wg_l", [P, KC, E + E * R], F32R)
        wl_h = sb("wl_h", [P, 1, D], F32R)
        wl_l = sb("wl_l", [P, 1, D], F32R)
        row = sb("row", [P, 5, D])
        qt = sb("qt", [P, NP, SEQ], F32R)
        kt = sb("kt", [P, NP, SEQ], F32R)
        qa = sb("qa", [P, H, HROWS], F32R)
        ka = sb("ka", [P, H, HROWS], F32R)
        qf = sb("qf", [P, 2, D])
        vn = sb("vn", [P, NT, D])
        v = sb("v", [P, NT, H, HD + 1])
        pt = sb("pt", [P, PT_RING, 2, SEQ + P])
        xa = sb("xa", [P, NT, D])
        x2 = sb("x2", [P, NT, D])
        xt_h = sb("xt_h", [P, NT, KC, P], F32R)
        xt_l = sb("xt_l", [P, NT, KC, P], F32R)
        at_h = sb("at_h", [P, NT, KC, P], F32R)
        at_l = sb("at_l", [P, NT, KC, P], F32R)
        on = sb("on", [P, NT, D])
        ot = sb("ot", [P, SEQ])
        hs = sb("hs", [P, NT, E + E * R])
        hw_h = sb("hw_h", [P, NT, P], F32R)
        hw_l = sb("hw_l", [P, NT, P], F32R)
        ident_r = sb("ident_r", [P, P], F32R)
        ident = ident_r[:, :].bitcast(F32)
        cbf = sb("cbf", [P, 2 * P], BF16)
        nmt_f = hs[:, 0, 0:P]
        kblock = sb("kblock", [P, H, 2])
        fence = sb("fence", [P, 2, NT, 8], BF16)
        tri = sb("tri", [P, E, E], BF16)
        neg_half = sb("neg_half", [P, 2])
        st1 = sb("st1", [P, NT, 6])
        mv1 = sb("mv1", [P, NT, 2])
        ve1 = sb("ve1", [P, NT])
        rs1 = sb("rs1", [P, NT])
        st2 = sb("st2", [P, NT, 6])
        mv2 = sb("mv2", [P, NT, 2])
        ve2 = sb("ve2", [P, NT])
        rs2 = sb("rs2", [P, NT])
        stq = sb("stq", [P, 2, 6])
        mvq = sb("mvq", [P, 2, 2])
        veq = sb("veq", [P, 2])
        rsq = sb("rsq", [P, 2])
        pm = sb("pm", [P, NP, 2, 3])
        nm = sb("nm", [P, 2, 4, NT])
        nms = sb("nms", [P, NG, 2, 2, 4 * NT], F32R)
        nmt = sb("nmt", [P, P], F32R)
        rc = sb("rc", [P, NT, 4])
        mxl = sb("mxl", [P, NT])
        zl = sb("zl", [P, NT, E])
        el = sb("el", [P, NT, E])
        esum = sb("esum", [P, NT])
        erec = sb("erec", [P, NT])
        pr = sb("pr", [P, NT, E])
        gt = sb("gt", [P, NT * E, E], BF16)
        ge = sb("ge", [P, NT * E, E], BF16)
        rank = sb("rank", [P, NT, E])

        ps_s = ctx.enter_context(nc.psum_tensor("ps_s", [P, 1024], F32))
        ps_st = ctx.enter_context(nc.psum_tensor("ps_st", [P, 1024], F32))
        ps_mm = ctx.enter_context(nc.psum_tensor("ps_mm", [P, 2, D], F32))
        ps_tr = ctx.enter_context(nc.psum_tensor("ps_tr", [P, D], F32))
        ps_pv = ctx.enter_context(nc.psum_tensor("ps_pv", [P, D], F32))

        names = """ident_in const_in small_ready ident_ready kaug_ready rt2_step half_ready ones_ready nms_zeroed pv_zeroed
            wsplit_h wsplit_l row_in ffn_row_in
            xa_in x2_in x2_bias ln1_step ln1_rstd ln1_norm xt_done xth_ready xtl_ready
            qkv_done qkv_out lnq_step lnq_rstd lnq_norm q_ready exp_hi exp_lo aug_set
            t_done t_dve t_act v_copied s_done s_max nm_step mt_done nmt_copied mrow_in0 mrow_in1 mrow_in2 mrow_in3
            st_done st_exp p_masked pv_done o_copied ot_done o_rec o_norm at_done ath_ready atl_ready
            wo_done wo_out ln2_step ln2_rstd ln2_norm x2t_done x2h_ready x2l_ready x2_plus
            h_done h_out rt_step rt_exp hw_ready hwt_done hwh_ready hwl_ready ffn_done y_ready y_stored""".split()
        S = {n: sem(n) for n in names}

        def v_tile(g, t):
            return NT * g + t + 1

        def qkv_no(g, t, n):
            return 3 * NT * g + (2 * t + n if n < 2 else 2 * NT + t) + 1

        reads_done = {
            "xt": lambda g, t: (S["xtl_ready"], v_tile(g, t)),
            "at": lambda g, t: (S["atl_ready"], v_tile(g, t)),
            "x2t": lambda g, t: (S["x2l_ready"], v_tile(g, t)),
            "hwt": lambda g: (S["hwl_ready"], g + 1),
            "m_turn": lambda g, n: (S["nmt_copied"], NG * g + n + 1),
            "o_turn": lambda g, n: (S["o_norm"], NP // 2 * g + n + 1),
            "wo": lambda g, t: (S["wo_out"], v_tile(g, t)),
            "h": lambda g, t: (S["h_out"], v_tile(g, t)),
            "ffn": lambda g, t: (S["y_ready"], v_tile(g, t)),
            "qkv": lambda g, t, n: (S["qkv_out"], qkv_no(g, t, n)),
        }

        def wait_tr_free(eng, step):
            if tr_no[step] >= 1:
                prev = tr_units[tr_no[step] - 1]
                eng.wait_ge(*reads_done[prev[0]](*prev[1:]))

        def wait_mm_free(eng, step):
            if mm_no[step] >= 2:
                prev = mm_units[mm_no[step] - 2]
                eng.wait_ge(*reads_done[prev[0]](*prev[1:]))

        def mm_bank(step):
            return ps_mm[:, mm_no[step] % 2, :]

        pt_flat = pt[:, :, :, :].rearrange("p i e q -> p (i e q)")
        spare = [pt_flat[:, i * D:(i + 1) * D] for i in range(6)] + [vn[:, 0, :], vn[:, 1, :], on[:, 0, :], on[:, 1, :]]
        pieces = []
        for n in range(3):
            for c in range(KC):
                pieces.append((spare[len(pieces) % len(spare)], wq_h[:, n, c, :], wq_l[:, n, c, :]))
        N_QKV_A = len(pieces)
        matrices = []

        def bounced(src, n, high, low, n_chunks):
            matrices.append((src, scratch[n], low.bitcast(F32)))
            for c in range(n_chunks):
                pieces.append((low[:, c].bitcast(F32), high[:, c], low[:, c]))

        bounced(wout[0], 0, wo_h[:, :, :], wo_l[:, :, :], KC)
        N_OUT_A = len(pieces)
        bounced(wbase, 1, wb_h[:, :, :], wb_l[:, :, :], KC)
        N_BASE = len(pieces)
        bounced(wgate, 2, wg_h[:, :, :], wg_l[:, :, :], KC)
        N_GATE = len(pieces)
        bounced(wlow, 3, wl_h[:, :, :], wl_l[:, :, :], 1)
        N_LOW = len(pieces)
        for n in range(3):
            bounced(wqkv[1, n], 4 + n, wq_h[:, n, :, :], wq_l[:, n, :, :], KC)
        N_QKV_B = len(pieces)
        bounced(wout[1], 7, wo_h[:, :, :], wo_l[:, :, :], KC)
        N_OUT_B = len(pieces)
        piece_in = [sem(f"piece_in{n}") for n in range(N_QKV_A)]
        bounce_done = [sem(f"bounce_done{m}") for m in range(len(matrices))]
        matrix_in = [sem(f"matrix_in{m}") for m in range(len(matrices))]
        matrix_of = [0] * KC + [1] * KC + [2] * KC + [3] + [4 + n // KC for n in range(4 * KC)]

        block = ctx.enter_context(nc.Block())

        @block.sync
        def _(sp):
            def source(g):
                src = x_in if g < NB else mid
                b = g % NB
                return src[b * SEQ:(b + 1) * SEQ, :].rearrange("(t p) d -> p t d", p=P)

            def load_piece(n):
                if n >= len(spare):
                    sp.wait_ge(S["wsplit_l"], n - len(spare) + 1)
                sp.dma_start(pieces[n][0], wqkv[0, n // KC, :, n % KC, :]).then_inc(piece_in[n], 16)

            def load_rows(n, first):
                sp.dma_start(row[:, n, :], rows[first:first + 1, :].partition_broadcast(P)).then_inc(S["row_in"], 16)

            def x_load(g):
                sp.wait_ge(S["xt_done"], v_tile(g - 1, 1))
                if g >= NB:
                    sp.wait_ge(S["y_stored"], 16 * NT * (g - NB + 1))
                sp.dma_start(xa[:, :, :], source(g)).then_inc(S["xa_in"], 16)

            def x2_load(g):
                if g:
                    sp.wait_ge(S["y_stored"], 16 * NT * g)
                else:
                    sp.wait_ge(S["kaug_ready"], 2)
                sp.dma_start(x2[:, :, :], source(g)).then_inc(S["x2_in"], 16)

            def y_store(g, t):
                sp.wait_ge(S["y_ready"], v_tile(g, t))
                dst = mid if g < NB else out
                first = g % NB * SEQ + t * P
                sp.dma_start(dst[first:first + P, :], x2[:, t, :]).then_inc(S["y_stored"], 16)

            def m_rows(g, n):
                sp.wait_ge(S["nmt_copied"], NG * g + n + 1)
                for e in range(2):
                    r0 = 32 * n + 16 * e
                    sp.dma_start(qt[HROWS * e + EXTRA:HROWS * e + EXTRA + 2, 4 * n:4 * n + 4, :].bitcast(F32),
                                 nmt[r0:r0 + 16, :].bitcast(F32)).then_inc(S[f"mrow_in{n}"], 16)

            def bounce(m):
                src, via, _ = matrices[m]
                sp.dma_start(via, src).then_inc(bounce_done[m], 16)

            def w_load(m):
                sp.wait_ge(bounce_done[m], 16)
                if 4 <= m < 7:
                    sp.wait_ge(S["qkv_done"], qkv_no(NB - 1, 1, m - 4))
                if m == 7:
                    sp.wait_ge(S["wo_done"], NT * NB)
                sp.dma_start(matrices[m][2], matrices[m][1].bitcast(F32)).then_inc(matrix_in[m], 16)

            def b_rows(_):
                sp.wait_ge(S["q_ready"], 2 * NT * NB)
                for n in range(4):
                    load_rows(n, 4 + n)

            sp.dma_start(xa[:, :, :], source(0)).then_inc(S["xa_in"], 16)
            sp.dma_start(nmt_f[:, :], c_ident).then_inc(S["ident_in"], 16)
            for n in range(2 * KC):
                load_piece(n)
            sp.dma_start(qf[:, 0, 0:c_small.shape[-1]], c_small).then_inc(S["const_in"], 16)
            sp.dma_start(kblock[:, :, :], c_kblock).then_inc(S["const_in"], 16)
            sp.dma_start(x2[:, 0, :], c_kaug).then_inc(S["const_in"], 16)
            sp.dma_start(x2[:, 1, :], c_qaug).then_inc(S["const_in"], 16)
            for n in range(4):
                load_rows(n, n)
            for n in range(2 * KC, N_QKV_A):
                load_piece(n)
            sp.dma_start(row[:, 4, :], rows[8:9, :].partition_broadcast(P)).then_inc(S["ffn_row_in"], 16)
            does = {"x_load": x_load, "x2_load": x2_load, "y_store": y_store, "m_rows": m_rows, "bounce": bounce,
                    "w_load": w_load, "b_rows": b_rows}
            for step in plan:
                if step[0] in does and step != ("x_load", 0):
                    does[step[0]](*step[1:])
            sp.wait_ge(S["y_stored"], 16 * NT * STAGES)

        @block.tensor
        def _(pe):
            def passes(dst, a_h, a_l, b_h, b_l, c, start, stop):
                pe.matmul(dst, a_h(c), b_h(c), start=start, stop=False)
                pe.matmul(dst, a_h(c), b_l(c), start=False, stop=False)
                return pe.matmul(dst, a_l(c), b_h(c), start=False, stop=stop)

            def turn(src, parts, done):
                for c in range(parts):
                    ins = pe.transpose(ps_tr[:, c * P:(c + 1) * P], src(c), ident)
                ins.then_inc(done, 1)

            def xt(g, t):
                pe.wait_ge(S["ln1_norm"], v_tile(g, t))
                wait_tr_free(pe, ("xt", g, t))
                turn(lambda c: xa[:, t, c * P:(c + 1) * P], KC, S["xt_done"])

            def qkv(g, t, n, c):
                if c == 0:
                    pe.wait_ge(S["xtl_ready"], v_tile(g, t))
                    wait_mm_free(pe, ("qkv", g, t, n))
                if g == 0 and t == 0:
                    pe.wait_ge(S["wsplit_l"], KC * n + c + 1)
                elif g == NB and t == 0 and c == 0:
                    pe.wait_ge(S["wsplit_l"], N_LOW + KC * (n + 1))
                ins = passes(mm_bank(("qkv", g, t, n)), lambda c: xt_h[:, t, c, :], lambda c: xt_l[:, t, c, :],
                             lambda c: wq_h[:, n, c, :], lambda c: wq_l[:, n, c, :], c, c == 0, c == KC - 1)
                if c == KC - 1:
                    ins.then_inc(S["qkv_done"], 1)

            def head_turn(g, t, u, half):
                pe.wait_ge(S["exp_lo"], 2 * NT * g + 2 * t + u + 1)
                pe.wait_ge(S["aug_set"], 2 * NT * g + 2 * t + u + 1)
                src, dst = (qa, ka)[u], (ps_s, ps_st)[half]
                if t == 0 and u == 0:
                    if g:
                        pe.wait_ge((S["s_max"], S["st_exp"])[half], 2 * NP * g)
                else:
                    pe.wait_ge((S["t_dve"], S["t_act"])[half], 4 * g + 2 * t + u)
                for i in range(8):
                    p = 8 * half + i
                    ins = pe.matmul(dst[:, i * P:(i + 1) * P], src[:, 2 * p:2 * p + 2, :], ident_r[:, :],
                                    start=True, stop=True)
                ins.then_inc(S["t_done"], 1)

            def s_step(g, p, e):
                if p == 0:
                    pe.wait_ge(S["t_dve"], 4 * g + 4)
                    pe.wait_ge(S["t_act"], 4 * g + 4)
                else:
                    pe.wait_ge(S["s_max"], 2 * (NP * g + p - 1) + e + 1)
                bank = ps_s[:, e * D:(e + 1) * D]
                pe.matmul(bank[:, 0:3 * P].rearrange("p (b k) -> p b k", b=3)[:, 0:3:2, :], cbf[:, 0:P],
                          cbf[:, P:2 * P].rearrange("p (r k) -> p r k", r=1).broadcast_to([P, 2, P]),
                          start=True, stop=False, skip_group_check=True)
                r = slice(HROWS * e, HROWS * (e + 1))
                pe.matmul(bank[:, 0:P], qt[r, p, 0:P], kt[r, p, 0:P], start=False, stop=False,
                          skip_group_check=True)
                pe.matmul(bank[:, P:3 * P], qt[r, p, P:2 * P], kt[r, p, :], start=False, stop=True,
                          skip_group_check=True).then_inc(S["s_done"], 1)

            def m_turn(g, n):
                pe.wait_ge(S["nm_step"], 4 * (NG * g + n + 1))
                wait_tr_free(pe, ("m_turn", g, n))
                pe.matmul(ps_tr[:, 0:P], nms[:, :, :, :, :], ident_r[:, :], start=True, stop=True)\
                  .then_inc(S["mt_done"], 1)

            def st_step(g, p, e):
                if p:
                    pe.wait_ge(S["st_exp"], 2 * (NP * g + p - 1) + e + 1)
                if p % 4 == 0 and e == 0:
                    pe.wait_ge(S[f"mrow_in{p // 4}"], 32 * (g + 1))
                r = slice(HROWS * e, HROWS * (e + 1))
                bank = ps_st[:, e * D:(e + 1) * D]
                pe.matmul(bank[:, 0:3 * P].rearrange("p (b q) -> p b q", b=3)[:, 0:3:2, :], kt[r, p, 0:P],
                          qt[r, p, :].rearrange("p (b q) -> p b q", b=2), start=True, stop=True)
                pe.matmul(bank[:, P:2 * P], kt[r, p, P:2 * P], qt[r, p, P:2 * P], start=True,
                          stop=True).then_inc(S["st_done"], 1)

            def pv_step(g, n):
                k = NP // 2 * g + n
                pe.wait_ge(S["p_masked"], NP * g + 2 * n + 2)
                if n == 0:
                    pe.wait_ge(S["v_copied"], g + 1)
                if k:
                    pe.wait_ge(S["o_copied"], k)
                else:
                    pe.wait_ge(S["pv_zeroed"], 1)
                for part in range(NT):
                    for j in range(4):
                        h, e = 4 * n + j, j % 2
                        pair = pt[:, (2 * n + j // 2) % PT_RING, e, :]
                        if part == 0:
                            rhs = pair.rearrange("p (b q) -> p b q", b=3)[:, 0:3:2, :]
                            cols = slice(0, SEQ)
                        else:
                            rhs, cols = pair[:, P:2 * P], slice(P, SEQ)
                        ins = pe.matmul(ps_pv[32 * j:32 * j + HD + 1, cols], v[:, part, h, :], rhs,
                                        start=part == 0, stop=part == 1, skip_group_check=True,
                                        tile_position=(0, 32 * j))
                ins.then_inc(S["pv_done"], 1)

            def o_turn(g, n):
                pe.wait_ge(S["o_copied"], NP // 2 * g + n + 1)
                wait_tr_free(pe, ("o_turn", g, n))
                turn(lambda t: ot[:, t * P:(t + 1) * P], NT, S["ot_done"])

            def at(g, t):
                pe.wait_ge(S["o_norm"], NP // 2 * (g + 1))
                wait_tr_free(pe, ("at", g, t))
                turn(lambda c: on[:, t, c * P:(c + 1) * P], KC, S["at_done"])

            def wo(g, t, c):
                if c == 0:
                    pe.wait_ge(S["atl_ready"], v_tile(g, t))
                    wait_mm_free(pe, ("wo", g, t))
                    if g % NB == 0:
                        pe.wait_ge(S["wsplit_l"], N_OUT_A if g < NB else N_OUT_B)
                ins = passes(mm_bank(("wo", g, t)), lambda c: at_h[:, t, c, :], lambda c: at_l[:, t, c, :],
                             lambda c: wo_h[:, c, :], lambda c: wo_l[:, c, :], c, c == 0, c == KC - 1)
                if c == KC - 1:
                    ins.then_inc(S["wo_done"], 1)

            def x2t(g, t):
                pe.wait_ge(S["ln2_norm"], v_tile(g, t))
                wait_tr_free(pe, ("x2t", g, t))
                turn(lambda c: on[:, t, c * P:(c + 1) * P], KC, S["x2t_done"])

            def h_step(g, t):
                pe.wait_ge(S["x2l_ready"], v_tile(g, t))
                wait_mm_free(pe, ("h", g, t))
                if g == 0:
                    pe.wait_ge(S["wsplit_l"], N_GATE)
                for c in range(KC):
                    ins = passes(mm_bank(("h", g, t))[:, 0:E + E * R], lambda c: at_h[:, t, c, :],
                                 lambda c: at_l[:, t, c, :], lambda c: wg_h[:, c, :], lambda c: wg_l[:, c, :],
                                 c, c == 0, c == KC - 1)
                ins.then_inc(S["h_done"], 1)

            def hwt(g):
                pe.wait_ge(S["hw_ready"], g + 1)
                wait_tr_free(pe, ("hwt", g))
                turn(lambda t: hs[:, t, E:E + E * R], NT, S["hwt_done"])

            def ffn(g, t, c):
                dst = mm_bank(("ffn", g, t))
                if c == 0:
                    pe.wait_ge(S["x2l_ready"], v_tile(g, t))
                    wait_mm_free(pe, ("ffn", g, t))
                    if g == 0:
                        pe.wait_ge(S["wsplit_l"], N_LOW)
                if c < KC:
                    passes(dst, lambda c: at_h[:, t, c, :], lambda c: at_l[:, t, c, :],
                           lambda c: wb_h[:, c, :], lambda c: wb_l[:, c, :], c, c == 0, False)
                else:
                    pe.wait_ge(S["hwl_ready"], g + 1)
                    passes(dst, lambda c: hw_h[:, t, :], lambda c: hw_l[:, t, :],
                           lambda c: wl_h[:, 0, :], lambda c: wl_l[:, 0, :], c, False, True)\
                        .then_inc(S["ffn_done"], 1)

            pe.wait_ge(S["ident_ready"], 1)
            does = {"xt": xt, "qkv": qkv, "head_turn": head_turn, "s": s_step, "m_turn": m_turn, "st": st_step,
                    "pv": pv_step, "o_turn": o_turn, "at": at, "wo": wo, "x2t": x2t, "h": h_step, "hwt": hwt,
                    "ffn": ffn}
            for step in plan:
                if step == ("s", 0, 0, 0):
                    pe.wait_ge(S["small_ready"], 1)
                if step[0] in does:
                    does[step[0]](*step[1:])

        @block.scalar
        def _(act):
            def w_high(n):
                if n < N_QKV_A:
                    act.wait_ge(piece_in[n], 16)
                else:
                    act.wait_ge(matrix_in[matrix_of[n - N_QKV_A]], 16)
                nc.scalar.activation(pieces[n][1], pieces[n][0], ACT.Copy).then_inc(S["wsplit_h"], 1)

            def high(dst, done, ready, n):
                act.wait_ge(done, n)
                nc.scalar.activation(dst, ps_tr[:, :].rearrange("p (c q) -> p c q", c=KC), ACT.Copy).then_inc(ready, 1)

            def xt_high(g, t):
                if g:
                    act.wait_ge(S["qkv_done"], qkv_no(g - 1, t, 2))
                high(xt_h[:, t, :, :], S["xt_done"], S["xth_ready"], v_tile(g, t))

            def expand_high(g, t, u):
                k = NT * g + t
                if g < NB:
                    act.wait_ge(S["q_ready"], 2 * k + u + 1)
                else:
                    act.wait_ge(S["qkv_out"], qkv_no(g, t, u))
                if k:
                    act.wait_ge(S["t_done"], 4 * (k - 1) + 2 * u + 2)
                dst = (qa, ka)[u]
                step = (2, 1)[u]
                o = dst[:, :, 0:EXTRA + HD].rearrange("p h (r d) -> p h r d", d=HD)[:, :, 0:step + 1:step, :]
                i = qf[:, u, :].rearrange("p (h r d) -> p h r d", h=H, r=1).broadcast_to([P, H, 2, HD])
                nc.scalar.activation(o, i, ACT.Copy).then_inc(S["exp_hi"], 1)

            def turn_act(g, t, u):
                act.wait_ge(S["t_done"], 4 * (NT * g + t) + 2 * u + 2)
                nc.scalar.activation((qt, kt)[u][:, 8:16, t * P:(t + 1) * P],
                                     ps_st[:, :].rearrange("p (i q) -> p i q", i=8), ACT.Copy)\
                    .then_inc(S["t_act"], 1)

            def v_copy(g):
                if g:
                    act.wait_ge(S["pv_done"], NP // 2 * g)
                else:
                    act.wait_ge(S["ones_ready"], 1)
                act.wait_ge(S["qkv_out"], 3 * NT * (g + 1))
                nc.scalar.activation(v[:, :, :, 0:HD], vn[:, :, :].rearrange("p t (h d) -> p t h d", d=HD), ACT.Copy)\
                    .then_inc(S["v_copied"], 1)

            def m_copy(g, n):
                act.wait_ge(S["mt_done"], NG * g + n + 1)
                if g:
                    act.wait_ge(S[f"mrow_in{n}"], 32 * g)
                r = slice(32 * n, 32 * n + 32)
                nc.scalar.activation(nmt[r, :], ps_tr[r, 0:P], ACT.Copy).then_inc(S["nmt_copied"], 1)

            def exp_step(g, p, e):
                act.wait_ge(S["st_done"], 2 * (NP * g + p) + e + 1)
                if p >= PT_RING:
                    act.wait_ge(S["pv_done"], NP // 2 * g + (p - PT_RING) // 2 + 1)
                elif g:
                    act.wait_ge(S["pv_done"], NP // 2 * g)
                else:
                    act.wait_ge(S["wsplit_l"], N_QKV_A)
                nc.scalar.activation(pt[:, p % PT_RING, e, :], ps_st[:, e * D:e * D + SEQ + P],
                                     ACT.Exp, scale=HD ** -0.5).then_inc(S["st_exp"], 1)

            def o_copy(g, n):
                k = NP // 2 * g + n
                act.wait_ge(S["pv_done"], k + 1)
                if k:
                    act.wait_ge(S["ot_done"], k)
                nc.scalar.activation(ot[:, :], ps_pv[:, 0:SEQ], ACT.Copy).then_inc(S["o_copied"], 1)

            def at_high(g, t):
                if g:
                    act.wait_ge(S["ffn_done"], v_tile(g - 1, t))
                high(at_h[:, t, :, :], S["at_done"], S["ath_ready"], v_tile(g, t))

            def x2t_high(g, t):
                act.wait_ge(S["wo_done"], v_tile(g, t))
                high(at_h[:, t, :, :], S["x2t_done"], S["x2h_ready"], v_tile(g, t))

            def route_exp(g):
                act.wait_ge(S["rt_step"], 8 * g + 2)
                nc.scalar.activation(el[:, :, :], zl[:, :, :], ACT.Exp).then_inc(S["rt_exp"], 1)

            def hwt_high(g):
                act.wait_ge(S["hwt_done"], g + 1)
                if g:
                    act.wait_ge(S["ffn_done"], NT * g)
                nc.scalar.activation(hw_h[:, :, :], ps_tr[:, 0:NT * P].rearrange("p (t q) -> p t q", t=NT), ACT.Copy)\
                    .then_inc(S["hwh_ready"], 1)

            does = {"w_high": w_high, "xt_high": xt_high, "expand_high": expand_high, "turn_act": turn_act,
                    "v_copy": v_copy, "m_copy": m_copy, "exp": exp_step, "o_copy": o_copy, "at_high": at_high,
                    "x2t_high": x2t_high, "route_exp": route_exp, "hwt_high": hwt_high}
            for step in plan:
                if step == ("expand_high", 0, 0, 0):
                    act.wait_ge(S["kaug_ready"], 2)
                if step[0] in does:
                    does[step[0]](*step[1:])

        @block.gpsimd
        def _(pool):
            def power(dst, src, n):
                return nc.gpsimd.tensor_tensor(dst, src, neg_half[:, 0:n], ALU.pow)

            def ln1_power(g, t):
                pool.wait_ge(S["ln1_step"], 3 * v_tile(g, t))
                power(rs1[:, t:t + 1], ve1[:, t:t + 1], 1).then_inc(S["ln1_rstd"], 1)

            def ln2_power(g, t):
                pool.wait_ge(S["ln2_step"], 3 * v_tile(g, t))
                power(rs2[:, t:t + 1], ve2[:, t:t + 1], 1).then_inc(S["ln2_rstd"], 1)

            def qk_power(g, t, n):
                pool.wait_ge(S["lnq_step"], 3 * (2 * (NT * g + t) + n + 1))
                power(rsq[:, n:n + 1], veq[:, n:n + 1], 1).then_inc(S["lnq_rstd"], 1)

            def expand_low(g, t, u):
                dst = (qa, ka)[u]
                pool.wait_ge(S["exp_hi"], 2 * (NT * g + t) + u + 1)
                c = (HD, 2 * HD)[u]
                nc.gpsimd.tensor_tensor(dst[:, :, c:c + HD], qf[:, u, :].rearrange("p (h d) -> p h d", d=HD),
                                        dst[:, :, 0:HD], ALU.subtract).then_inc(S["exp_lo"], 1)

            def expand_extra(g, t, u):
                dst = (qa, ka)[u]
                if g == 0 and t == 0:
                    pool.wait_ge(S["kaug_ready"], 2)
                else:
                    pool.wait_ge(S["t_done"], 4 * (NT * g + t - 1) + 2 * u + 2)
                extra = nc.gpsimd.tensor_copy(dst[:, :, EXTRA + 8:HROWS],
                                              fence[:, u, t, :].rearrange("p (h r) -> p h r", h=1)
                                              .broadcast_to([P, H, 8]))
                tile_rows = dst[:, :, EXTRA + 6:EXTRA + 8]
                if g < NB and u == 0:
                    extra = nc.gpsimd.memset(tile_rows.bitcast(F32), float(t))
                elif g < NB and t == 0:
                    extra = nc.gpsimd.tensor_copy(tile_rows, kblock[:, :, :])
                elif g < NB:
                    extra = nc.gpsimd.memset(tile_rows.bitcast(F32), 0.0)
                elif g == NB and t == 0 and u == 1:
                    extra = nc.gpsimd.memset(ka[:, :, EXTRA + 2:EXTRA + 8].bitcast(F32), 0.0)
                extra.then_inc(S["aug_set"], 1)

            def mask(g, p):
                pool.wait_ge(S["st_exp"], 2 * (NP * g + p + 1))
                w = pt[:, p % PT_RING, :, 0:2 * P]
                nc.gpsimd.affine_select(out=w, in_=w, compare_op=ALU.is_ge, fill=0.0, base=0,
                                        pattern=[[0, 4], [1, P]], channel_multiplier=-1).then_inc(S["p_masked"], 1)

            def x2_plus(g, t):
                pool.wait_ge(S["ln2_norm"], v_tile(g, t))
                if g == 0:
                    pool.wait_ge(S["ffn_row_in"], 16)
                nc.gpsimd.tensor_tensor(x2[:, t, :], x2[:, t, :], row[:, 4, :], ALU.add).then_inc(S["x2_plus"], 1)

            def x2_bias(g, t):
                if t == 0:
                    pool.wait_ge(S["x2_in"], 16 * (g + 1))
                    pool.wait_ge(S["row_in"], 16 * 8)
                nc.gpsimd.tensor_tensor(x2[:, t, :], x2[:, t, :], row[:, 3, :], ALU.add).then_inc(S["x2_bias"], 1)

            nc.gpsimd.memset(neg_half[:, :], -0.5).then_inc(S["half_ready"], 1)
            nc.gpsimd.memset(nms[:, :, :, :, :].bitcast(F32), 0.0).then_inc(S["nms_zeroed"], 1)
            pool.wait_ge(S["half_ready"], 1)
            does = {"ln1_power": ln1_power, "ln2_power": ln2_power, "qk_power": qk_power, "expand_low": expand_low,
                    "expand_extra": expand_extra, "mask": mask, "x2_plus": x2_plus, "x2_bias": x2_bias}
            for step in plan:
                if step == ("expand_extra", 0, 0, 0):
                    pool.wait_ge(S["small_ready"], 1)
                if step[0] in does:
                    does[step[0]](*step[1:])

        @block.vector
        def _(dve):
            def w_low(n):
                dve.wait_ge(S["wsplit_h"], n + 1)
                nc.vector.tensor_tensor(pieces[n][2], pieces[n][0], pieces[n][1], ALU.subtract)\
                    .then_inc(S["wsplit_l"], 1)

            def norm_stats(src, st, mv, ve, steps, n):
                nc.vector.bn_stats(st, src).then_inc(steps, 1)
                dve.wait_ge(steps, 3 * n + 1)
                nc.vector.bn_aggr(mv, st).then_inc(steps, 1)
                dve.wait_ge(steps, 3 * n + 2)
                nc.vector.tensor_scalar(ve, mv[:, 1:2], LN_EPS, None, ALU.add).then_inc(steps, 1)

            def ln1_stats(g, t):
                dve.wait_ge(S["xa_in"], 16 * (g + 1))
                norm_stats(xa[:, t, :], st1[:, t, :], mv1[:, t, :], ve1[:, t:t + 1], S["ln1_step"], NT * g + t)

            def ln1_norm(g, t):
                dve.wait_ge(S["ln1_rstd"], v_tile(g, t))
                nc.vector.tensor_scalar(xa[:, t, :], xa[:, t, :], mv1[:, t, 0:1], rs1[:, t:t + 1],
                                        ALU.subtract, ALU.mult).then_inc(S["ln1_norm"], 1)

            def low(hi, lo, ready_h, ready_l, n):
                dve.wait_ge(ready_h, n)
                nc.vector.tensor_tensor(lo, ps_tr[:, :].rearrange("p (c q) -> p c q", c=KC), hi, ALU.subtract)\
                    .then_inc(ready_l, 1)

            def xt_low(g, t):
                low(xt_h[:, t, :, :], xt_l[:, t, :, :], S["xth_ready"], S["xtl_ready"], v_tile(g, t))

            def qkv_out(g, t, n):
                src = mm_bank(("qkv", g, t, n))
                dve.wait_ge(S["qkv_done"], qkv_no(g, t, n))
                k = 2 * (NT * g + t) + n
                if n == 2:
                    dst = vn[:, t, :]
                    if g:
                        dve.wait_ge(S["v_copied"], g)
                else:
                    dst = qf[:, n, :]
                    if k >= 2:
                        dve.wait_ge(S["exp_lo"], k - 1)
                if g < NB:
                    nc.vector.tensor_scalar(dst, src, CLIP, -CLIP, ALU.min, ALU.max).then_inc(S["qkv_out"], 1)
                    if n < 2:
                        dve.wait_ge(S["qkv_out"], qkv_no(g, t, n))
                        norm_stats(dst, stq[:, n, :], mvq[:, n, :], veq[:, n:n + 1], S["lnq_step"], k)
                        if k == 0:
                            dve.wait_ge(S["row_in"], 16 * 4)
                        nc.vector.scalar_tensor_tensor(dst, dst, mvq[:, n, 0:1], row[:, 2 * n, :], ALU.subtract,
                                                       ALU.mult).then_inc(S["lnq_norm"], 1)
                else:
                    dve.wait_ge(S["row_in"], 16 * 8)
                    nc.vector.tensor_tensor(dst, src, row[:, n, :], ALU.add).then_inc(S["qkv_out"], 1)

            def qk_norm(g, t, n):
                k = 2 * (NT * g + t) + n
                dve.wait_ge(S["lnq_rstd"], k + 1)
                dve.wait_ge(S["lnq_norm"], k + 1)
                nc.vector.scalar_tensor_tensor(qf[:, n, :], qf[:, n, :], rsq[:, n:n + 1], row[:, 2 * n + 1, :],
                                               ALU.mult, ALU.add).then_inc(S["q_ready"], 1)

            def turn_dve(g, t, u):
                dve.wait_ge(S["t_done"], 4 * (NT * g + t) + 2 * u + 1)
                nc.vector.tensor_copy((qt, kt)[u][:, 0:8, t * P:(t + 1) * P],
                                      ps_s[:, :].rearrange("p (i q) -> p i q", i=8)).then_inc(S["t_dve"], 1)

            def s_max(g, p, e):
                dve.wait_ge(S["s_done"], 2 * (NP * g + p) + e + 1)
                nc.vector.tensor_reduce(pm[:, p, e, :],
                                        ps_s[:, e * D:e * D + 3 * P].rearrange("p (b k) -> p b k", b=3), AX_X,
                                        ALU.max, negate=True).then_inc(S["s_max"], 1)

            def m_split(g, n):
                k = 4 * (NG * g + n)
                dve.wait_ge(S["s_max"], 2 * (NP * g + 4 * (n + 1)))
                part = pm[:, 4 * n:4 * n + 4, :, :].rearrange("p i e b -> p e i b")
                nc.vector.tensor_copy(nm[:, :, :, 0], part[:, :, :, 0]).then_inc(S["nm_step"], 1)
                nc.vector.tensor_tensor(nm[:, :, :, 1], part[:, :, :, 1], part[:, :, :, 2], ALU.min)\
                    .then_inc(S["nm_step"], 1)
                flat = nm[:, :, :, :].rearrange("p e i t -> p e (i t)")
                dve.wait_ge(S["nm_step"], k + 2)
                if k:
                    dve.wait_ge(S["mt_done"], NG * g + n)
                else:
                    dve.wait_ge(S["nms_zeroed"], 1)
                nc.vector.tensor_copy(nms[:, n, :, 0, :], flat).then_inc(S["nm_step"], 1)
                dve.wait_ge(S["nm_step"], k + 3)
                nc.vector.tensor_tensor(nms[:, n, :, 1, :], flat, nms[:, n, :, 0, :], ALU.subtract)\
                    .then_inc(S["nm_step"], 1)

            def o_norm(g, n):
                k = NP // 2 * g + n
                dve.wait_ge(S["ot_done"], k + 1)
                view = ps_tr[:, 0:NT * P].rearrange("p (t j r) -> p t j r", t=NT, j=4)
                if k:
                    dve.wait_ge(S["o_norm"], k)
                nc.vector.reciprocal(rc[:, :, :], view[:, :, :, HD]).then_inc(S["o_rec"], 1)
                dve.wait_ge(S["o_rec"], k + 1)
                if g and n == 0:
                    dve.wait_ge(S["x2t_done"], NT * g)
                o = on[:, :, 4 * HD * n:4 * HD * (n + 1)].rearrange("p t (j d) -> p t j d", j=4)
                nc.vector.tensor_tensor(o, view[:, :, :, 0:HD],
                                        rc[:, :, :].rearrange("p t (j r) -> p t j r", r=1).broadcast_to([P, NT, 4, HD]),
                                        ALU.mult).then_inc(S["o_norm"], 1)

            def at_low(g, t):
                low(at_h[:, t, :, :], at_l[:, t, :, :], S["ath_ready"], S["atl_ready"], v_tile(g, t))

            def wo_out(g, t):
                dve.wait_ge(S["wo_done"], v_tile(g, t))
                dve.wait_ge(S["x2_in"], 16 * (g + 1))
                if g >= NB:
                    dve.wait_ge(S["x2_bias"], v_tile(g - NB, t))
                nc.vector.tensor_tensor(x2[:, t, :], mm_bank(("wo", g, t)), x2[:, t, :], ALU.add)\
                    .then_inc(S["wo_out"], 1)

            def ln2_stats(g, t):
                dve.wait_ge(S["wo_out"], v_tile(g, t))
                norm_stats(x2[:, t, :], st2[:, t, :], mv2[:, t, :], ve2[:, t:t + 1], S["ln2_step"], NT * g + t)

            def ln2_norm(g, t):
                dve.wait_ge(S["ln2_rstd"], v_tile(g, t))
                dve.wait_ge(S["at_done"], v_tile(g, t))
                nc.vector.tensor_scalar(on[:, t, :], x2[:, t, :], mv2[:, t, 0:1], rs2[:, t:t + 1],
                                        ALU.subtract, ALU.mult).then_inc(S["ln2_norm"], 1)

            def x2t_low(g, t):
                low(at_h[:, t, :, :], at_l[:, t, :, :], S["x2h_ready"], S["x2l_ready"], v_tile(g, t))

            def h_out(g, t):
                dve.wait_ge(S["h_done"], v_tile(g, t))
                if g:
                    dve.wait_ge(S["hwt_done"], g)
                nc.vector.tensor_copy(hs[:, t, :], mm_bank(("h", g, t))[:, 0:E + E * R]).then_inc(S["h_out"], 1)

            def each_expert(ap):
                return ap.rearrange("p (t r) -> p t r", r=1).broadcast_to([P, NT, E])

            def route_max(g):
                k, st = 8 * g, S["rt_step"]
                dve.wait_ge(S["h_out"], NT * (g + 1))
                nc.vector.tensor_reduce(mxl[:, :], hs[:, :, 0:E], AX_X, ALU.max).then_inc(st, 1)
                dve.wait_ge(st, k + 1)
                nc.vector.tensor_tensor(zl[:, :, :], hs[:, :, 0:E], each_expert(mxl[:, :]), ALU.subtract)\
                    .then_inc(st, 1)

            def route_rank(g):
                k, st = 8 * g, S["rt_step"]
                dve.wait_ge(S["rt_exp"], g + 1)
                nc.vector.tensor_reduce(esum[:, :], el[:, :, :], AX_X, ALU.add).then_inc(st, 1)
                dve.wait_ge(st, k + 3)
                nc.vector.reciprocal(erec[:, :], esum[:, :]).then_inc(st, 1)
                dve.wait_ge(st, k + 4)
                nc.vector.tensor_tensor(pr[:, :, :], el[:, :, :], each_expert(erec[:, :]), ALU.mult).then_inc(st, 1)
                dve.wait_ge(st, k + 5)
                for t in range(NT):
                    pj = pr[:, t, :].rearrange("p (i j) -> p i j", i=1).broadcast_to([P, E, E])
                    pi = pr[:, t, :].rearrange("p (i j) -> p i j", j=1).broadcast_to([P, E, E])
                    nc.vector.tensor_tensor(gt[:, t * E:(t + 1) * E, :], pj, pi, ALU.is_gt)
                    ins = nc.vector.tensor_tensor(ge[:, t * E:(t + 1) * E, :], pj, pi, ALU.is_ge)
                ins.then_inc(st, 1)
                dve.wait_ge(st, k + 6)
                for t in range(NT):
                    ins = nc.vector.tensor_tensor(ge[:, t * E:(t + 1) * E, :], ge[:, t * E:(t + 1) * E, :],
                                                  tri[:, :, :], ALU.mult)
                ins.then_inc(st, 1)
                dve.wait_ge(st, k + 7)
                nc.vector.tensor_tensor(gt[:, :, :], gt[:, :, :], ge[:, :, :], ALU.max).then_inc(st, 1)

            def route_weight(g):
                k, st = 5 * g, S["rt2_step"]
                dve.wait_ge(S["rt_step"], 8 * (g + 1))
                flat = pr[:, :, :].rearrange("p t i -> p (t i)")
                ranks = rank[:, :, :].rearrange("p t i -> p (t i)")
                nc.vector.tensor_reduce(ranks, gt[:, :, :], AX_X, ALU.add).then_inc(st, 1)
                dve.wait_ge(st, k + 1)
                nc.vector.scalar_tensor_tensor(flat, ranks, 1.5, flat, ALU.is_lt, ALU.mult).then_inc(st, 1)
                dve.wait_ge(st, k + 2)
                nc.vector.tensor_reduce(esum[:, :], pr[:, :, :], AX_X, ALU.add).then_inc(st, 1)
                dve.wait_ge(st, k + 3)
                nc.vector.reciprocal(erec[:, :], esum[:, :]).then_inc(st, 1)
                dve.wait_ge(st, k + 4)
                nc.vector.tensor_tensor(pr[:, :, :], pr[:, :, :], each_expert(erec[:, :]), ALU.mult).then_inc(st, 1)
                dve.wait_ge(st, k + 5)
                for t in range(NT):
                    o = hs[:, t, E:E + E * R].rearrange("p (e r) -> p e r", e=E)
                    w = pr[:, t, :].rearrange("p (e r) -> p e r", r=1).broadcast_to([P, E, R])
                    ins = nc.vector.tensor_tensor(o, o, w, ALU.mult)
                ins.then_inc(S["hw_ready"], 1)

            def hwt_low(g):
                dve.wait_ge(S["hwh_ready"], g + 1)
                nc.vector.tensor_tensor(hw_l[:, :, :], ps_tr[:, 0:NT * P].rearrange("p (t q) -> p t q", t=NT),
                                        hw_h[:, :, :], ALU.subtract).then_inc(S["hwl_ready"], 1)

            def ffn_out(g, t):
                dve.wait_ge(S["ffn_done"], v_tile(g, t))
                dve.wait_ge(S["x2_plus"], v_tile(g, t))
                nc.vector.tensor_tensor(x2[:, t, :], mm_bank(("ffn", g, t)), x2[:, t, :], ALU.add)\
                    .then_inc(S["y_ready"], 1)

            def small_constants(_):
                dve.wait_ge(S["const_in"], 16 * 4)
                nc.vector.tensor_copy(cbf[:, :], qf[:, 0, 0:2 * P])
                nc.vector.tensor_copy(fence[:, :, :, :].rearrange("p c t r -> p (c t r)"), qf[:, 0, 2 * P:2 * P + 32])
                nc.vector.tensor_copy(tri[:, :, :].rearrange("p i j -> p (i j)"), qf[:, 0, 2 * P + 32:2 * P + 96])\
                    .then_inc(S["small_ready"], 1)
                nc.vector.tensor_copy(ka[:, :, EXTRA:HROWS], x2[:, 0, :].rearrange("p (h r) -> p h r", h=H))\
                    .then_inc(S["kaug_ready"], 1)
                nc.vector.tensor_copy(qa[:, :, EXTRA:HROWS], x2[:, 1, :].rearrange("p (h r) -> p h r", h=H))\
                    .then_inc(S["kaug_ready"], 1)
                dve.wait_ge(S["small_ready"], 1)

            does = {"w_low": w_low, "ln1_stats": ln1_stats, "ln1_norm": ln1_norm, "xt_low": xt_low,
                    "qkv_out": qkv_out, "qk_norm": qk_norm, "turn_dve": turn_dve, "s_max": s_max,
                    "m_split": m_split, "o_norm": o_norm, "at_low": at_low, "wo_out": wo_out,
                    "ln2_stats": ln2_stats, "ln2_norm": ln2_norm, "x2t_low": x2t_low, "h_out": h_out,
                    "route_max": route_max, "route_rank": route_rank, "route_weight": route_weight,
                    "hwt_low": hwt_low, "ffn_out": ffn_out, "small_constants": small_constants}
            nc.vector.memset(ps_pv[:, :], 0.0).then_inc(S["pv_zeroed"], 1)
            nc.vector.memset(v[:, :, :, HD:HD + 1], 1.0).then_inc(S["ones_ready"], 1)
            for step in plan:
                if step == ("ln1_norm", 0, 0):
                    dve.wait_ge(S["ident_in"], 16)
                    nc.vector.tensor_copy(ident_r[:, :], nmt_f[:, :]).then_inc(S["ident_ready"], 1)
                if step[0] in does:
                    does[step[0]](*step[1:])


def constants():
    import numpy as np

    def high(a):
        m, e = np.frexp(a.astype(np.float64))
        return np.ldexp(np.rint(m * 4096) / 4096, e).astype(np.float32)

    ident = np.eye(P, dtype=np.float32)
    q, k = np.arange(P)[:, None], np.arange(P)[None, :]
    mask = np.where(k > q, -(2.0 ** 100), 0.0).astype(np.float32)
    m = np.arange(1, H + 1, dtype=np.float32) * np.float32(8.0 / H)
    slope = (1.0 / np.power(np.float32(2.0), m)).astype(np.float32)
    root = np.float32(HD ** 0.5)
    kaug = np.zeros((P, H, HD), np.float32)
    qaug = np.zeros((P, H, HD), np.float32)
    pos = np.arange(P, dtype=np.float32)[:, None]
    kaug[:, :, 0:2] = 1.0
    a = (slope[None, :] * pos).astype(np.float32) * root
    kaug[:, :, 2] = high(a)
    kaug[:, :, 3] = a - high(a)
    qaug[:, :, 2:4] = 1.0
    s4 = slope * root
    kaug[:, :, 4] = -high(s4)
    kaug[:, :, 5] = -(s4 - high(s4))
    qaug[:, :, 4:6] = pos[:, :, None]
    kblock = np.zeros((P, H, 2), np.float32)
    kblock[:, :, 0] = -high(s4) * P
    kblock[:, :, 1] = -(s4 - high(s4)) * P
    blk = (np.arange(NT)[None, :] * P + np.arange(P)[:, None]) // 32
    n8 = np.arange(8)
    fence = np.zeros((P, 2, NT, 8), np.float32)
    fence[:, 0] = blk[:, :, None] < n8
    fence[:, 1] = np.where(blk[:, :, None] == n8, -(2.0 ** 100), 0.0)
    tri = np.broadcast_to(np.tril(np.ones((E, E), np.float32), -1)[None], (P, E, E))
    small = np.concatenate([ident, mask, fence.reshape(P, -1), tri.reshape(P, -1)], 1)
    return [ident, small, kaug.reshape(P, H * HD), qaug.reshape(P, H * HD), kblock]


def kernel(**inputs):
    import numpy as np
    import concourse.bacc as bacc
    from concourse.bass_utils import run_bass_kernel_spmd as run

    nc = bacc.Bacc("TRN2", target_bir_lowering=False, num_devices=1)
    i = {k: np.asarray(a) for k, a in inputs.items()}
    arrays = {}

    def given(name, a):
        a = np.ascontiguousarray(a)
        arrays[name] = a
        return nc.dram_tensor(name, a.shape, mybir.dt.from_np(a.dtype), kind="ExternalInput").ap()

    def turned(w):
        return w.T.reshape(KC, P, -1).transpose(1, 0, 2)

    x = given("x", i["L0_attn_a_hidden_states"].reshape(NB * SEQ, D))
    consts = [given(f"const{n}", a) for n, a in enumerate(constants())]
    a3 = i["L0_attn_a_Wqkv"].reshape(3, D, D)
    b3 = np.stack([i["L0_attn_b_Wq"], i["L0_attn_b_Wk"], i["L0_attn_b_Wv"]])
    wqkv = given("wqkv", np.stack([np.stack([turned(w) for w in ws]) for ws in (a3, b3)]))
    wout = given("wout", np.stack([turned(i["L0_attn_a_Wout"]), turned(i["L0_attn_b_Wo"])]))
    wbase = given("wbase", turned(i["L0_ffn_W_base"]))
    wgate = given("wgate", turned(np.concatenate([i["L0_ffn_W_gate"], i["L0_ffn_A"].reshape(E * R, D)])))
    wlow = given("wlow", i["L0_ffn_B"].transpose(0, 2, 1).reshape(E * R, 1, D))
    rows = given("rows", np.stack([i["L0_attn_a_q_ln_w"], i["L0_attn_a_q_ln_b"], i["L0_attn_a_k_ln_w"],
                                   i["L0_attn_a_k_ln_b"], i["L0_attn_b_bq"], i["L0_attn_b_bk"],
                                   i["L0_attn_b_bv"], i["L0_attn_b_bo"], i["L0_ffn_b_base"]]))
    mid = nc.dram_tensor("mid", (NB * SEQ, D), F32, kind="Internal").ap()
    scratch = [nc.dram_tensor(f"scratch{n}", w.shape, F32, kind="Internal").ap()
               for n, w in enumerate([wout[0], wbase, wgate, wlow, wqkv[1, 0], wqkv[1, 1], wqkv[1, 2], wout[1]])]
    out = nc.dram_tensor("out", (NB * SEQ, D), F32, kind="ExternalOutput").ap()
    build(nc, x, consts, wqkv, wout, wbase, wgate, wlow, rows, mid, scratch, out)
    r = run(nc, [arrays], core_ids=[0])
    return r.results[0]["out"].reshape(NB, SEQ, D)
```
